# Optimizing a Trainium2 kernel written in Bass

```python
import numpy as np
import jax
import jax.numpy as jnp

def _softmax(x, axis=-1):
    return jax.nn.softmax(x, axis=axis)

def _gelu(x):
    return jax.nn.gelu(x, approximate=True)

def _silu(x):
    return jax.nn.silu(x)

def _sigmoid(x):
    return jax.nn.sigmoid(x)

def _layernorm(x, axis=-1, eps=1e-05):
    m = jnp.mean(x, axis=axis, keepdims=True)
    v = jnp.var(x, axis=axis, keepdims=True)
    return (x - m) / jnp.sqrt(v + eps)

def _scatter_add(tgt, idx, src, axis=0):
    return tgt.at[idx].add(src)

def _segment_sum(src, seg, n):
    return jax.ops.segment_sum(src, seg, n)
kernel_name = 'mk_perceiver_d1_seqx_r2_3732ef'

def setup_inputs(seed: int=0):
    np.random.seed(seed)
    _w = jnp.asarray

    def _rec_inputs():
        import jax
        import jax.numpy as jnp
        _rk = jax.random.key(seed)
        x = -0.0002928 + 1 * jax.random.normal(jax.random.fold_in(_rk, 1), (64, 32, 512), jnp.float32)
        _lenS = 32 - jax.random.randint(jax.random.fold_in(_rk, 7), (64,), 0, max(1, 32 // 4) + 1, jnp.int32)
        _lenS2 = 257 - jax.random.randint(jax.random.fold_in(_rk, 8), (64,), 0, max(1, 257 // 4) + 1, jnp.int32)
        _ctx_512P = jax.random.normal(jax.random.fold_in(_rk, 11), (64, 16, 256), jnp.float32)
        _ctx_512c = jax.random.dirichlet(jax.random.fold_in(_rk, 511), 0.3 * jnp.ones((16,), jnp.float32), (64, 257))
        _ctx_512t = jnp.einsum('bsk,bkd->bsd', _ctx_512c, _ctx_512P)
        _ctx_512t = _ctx_512t * jax.lax.rsqrt(jnp.mean(jnp.square(_ctx_512t)) + 1e-12) * 0.953939
        ctx_512 = -0.000514642 + 1.00011 * (_ctx_512t + 0.3 * jax.random.normal(jax.random.fold_in(_rk, 611), (64, 257, 256), jnp.float32))
        return (x, ctx_512)
    x, ctx_512 = _rec_inputs()

    def _L0_xattn_setup():
        import jax, jax.numpy as jnp
        import numpy as np
        DIM = 512
        LATENT_DIM = 256
        NUM_HEADS = 16
        HEAD_DIM = DIM // NUM_HEADS
        SCALE = HEAD_DIM ** (-0.5)
        key = jax.random.key(seed)
        k1, k2, k3, k4, k5 = jax.random.split(key, 5)
        B, xN, zN = (2, 1024, 1024)
        x = jax.random.normal(k1, (B, xN, DIM), dtype=jnp.float32)
        z = jax.random.normal(k2, (B, zN, LATENT_DIM), dtype=jnp.float32)
        Wq = jax.random.normal(k3, (DIM, DIM), dtype=jnp.float32) * DIM ** (-0.5)
        Wkv = jax.random.normal(k4, (2 * DIM, LATENT_DIM), dtype=jnp.float32) * LATENT_DIM ** (-0.5)
        Wo = jax.random.normal(k5, (DIM, DIM), dtype=jnp.float32) * DIM ** (-0.5)
        return {'x': x, 'z': z, 'Wq': Wq, 'Wkv': Wkv, 'Wo': Wo}
    _L0_xattn_all = _L0_xattn_setup()
    _L0_xattn_in = {k: v for k, v in _L0_xattn_all.items() if k in ('Wq', 'Wkv', 'Wo')}
    del _L0_xattn_all

    def _L0_attn_setup():
        import jax, jax.numpy as jnp
        import numpy as np
        N_HEAD = 16
        PAGE_SIZE = 128
        ROPE_THETA = 10000.0

        def _rope_tables(T, D, dtype):
            inv = 1.0 / ROPE_THETA ** (np.arange(0, D, 2, dtype=np.float32) / D)
            ang = np.outer(np.arange(T, dtype=np.float32), inv)
            return (jnp.asarray(np.cos(ang), dtype), jnp.asarray(np.sin(ang), dtype))

        def _apply_rope(x, cos, sin):
            x1 = x[..., 0::2]
            x2 = x[..., 1::2]
            c = cos[None, :, None, :]
            s = sin[None, :, None, :]
            out = jnp.stack([x1 * c - x2 * s, x1 * s + x2 * c], axis=-1)
            return out.reshape(x.shape)
        key = jax.random.key(seed)
        ks = jax.random.split(key, 6)
        B, T, E = (2, 1024, 512)
        L = E // 2
        sc = lambda fan: 1.0 / np.sqrt(fan)
        return {'x': jax.random.normal(ks[0], (B, T, E), jnp.float32), 'wq': jax.random.normal(ks[1], (E, E), jnp.float32) * sc(E), 'w_down': jax.random.normal(ks[2], (E, L), jnp.float32) * sc(E), 'wk_up': jax.random.normal(ks[3], (L, E), jnp.float32) * sc(L), 'wv_up': jax.random.normal(ks[4], (L, E), jnp.float32) * sc(L), 'wo': jax.random.normal(ks[5], (E, E), jnp.float32) * sc(E)}
    _L0_attn_all = _L0_attn_setup()
    _L0_attn_in = {k: v for k, v in _L0_attn_all.items() if k in ('wq', 'w_down', 'wk_up', 'wv_up', 'wo')}
    del _L0_attn_all

    def _L0_ffn_setup():
        import jax, jax.numpy as jnp
        import numpy as np
        DIM = 512
        NUM_EXPERTS = 8
        TOP_K = 2
        HIDDEN = int(DIM * 1.5)
        key = jax.random.key(seed)
        k_x, k_r, k_w1, k_w2, k_w3 = jax.random.split(key, 5)
        B, T = (2, 2048)
        s_in = 1.0 / np.sqrt(DIM)
        s_h = 1.0 / np.sqrt(HIDDEN)
        return {'x': jax.random.normal(k_x, (B, T, DIM), dtype=jnp.float32), 'Wr': jax.random.uniform(k_r, (DIM, NUM_EXPERTS), minval=-s_in, maxval=s_in, dtype=jnp.float32), 'W1': jax.random.uniform(k_w1, (NUM_EXPERTS, DIM, HIDDEN), minval=-s_in, maxval=s_in, dtype=jnp.float32), 'W2': jax.random.uniform(k_w2, (NUM_EXPERTS, HIDDEN, DIM), minval=-s_h, maxval=s_h, dtype=jnp.float32), 'W3': jax.random.uniform(k_w3, (NUM_EXPERTS, DIM, HIDDEN), minval=-s_in, maxval=s_in, dtype=jnp.float32)}
    _L0_ffn_all = _L0_ffn_setup()
    _L0_ffn_in = {k: v for k, v in _L0_ffn_all.items() if k in ('Wr', 'W1', 'W2', 'W3')}
    del _L0_ffn_all
    return {'x': x, 'ctx_512': ctx_512, 'L0_xattn_Wq': _L0_xattn_in['Wq'], 'L0_xattn_Wkv': _L0_xattn_in['Wkv'], 'L0_xattn_Wo': _L0_xattn_in['Wo'], 'L0_attn_wq': _L0_attn_in['wq'], 'L0_attn_w_down': _L0_attn_in['w_down'], 'L0_attn_wk_up': _L0_attn_in['wk_up'], 'L0_attn_wv_up': _L0_attn_in['wv_up'], 'L0_attn_wo': _L0_attn_in['wo'], 'L0_ffn_Wr': _L0_ffn_in['Wr'], 'L0_ffn_W1': _L0_ffn_in['W1'], 'L0_ffn_W2': _L0_ffn_in['W2'], 'L0_ffn_W3': _L0_ffn_in['W3']}

def reference(x, ctx_512, L0_xattn_Wq, L0_xattn_Wkv, L0_xattn_Wo, L0_attn_wq, L0_attn_w_down, L0_attn_wk_up, L0_attn_wv_up, L0_attn_wo, L0_ffn_Wr, L0_ffn_W1, L0_ffn_W2, L0_ffn_W3):
    import jax
    import jax.numpy as jnp

    def _L0_xattn_ref(x, z, Wq, Wkv, Wo):
        import jax, jax.numpy as jnp
        import numpy as np
        DIM = 512
        LATENT_DIM = 256
        NUM_HEADS = 16
        HEAD_DIM = DIM // NUM_HEADS
        SCALE = HEAD_DIM ** (-0.5)
        B, xN, _ = x.shape
        _, zN, _ = z.shape
        Q = (x @ Wq.T).reshape(B, xN, NUM_HEADS, HEAD_DIM)
        KV = (z @ Wkv.T).reshape(B, zN, 2, NUM_HEADS, HEAD_DIM)
        K = KV[:, :, 0]
        V = KV[:, :, 1]
        attn = jnp.einsum('bqhd,bkhd->bhqk', Q, K) * SCALE
        attn = jax.nn.softmax(attn, axis=-1)
        O = jnp.einsum('bhqk,bkhd->bqhd', attn, V).reshape(B, xN, DIM)
        return O @ Wo.T

    def _L0_attn_ref(x, wq, w_down, wk_up, wv_up, wo):
        import jax, jax.numpy as jnp
        import numpy as np
        N_HEAD = 16
        PAGE_SIZE = 128
        ROPE_THETA = 10000.0

        def _rope_tables(T, D, dtype):
            inv = 1.0 / ROPE_THETA ** (np.arange(0, D, 2, dtype=np.float32) / D)
            ang = np.outer(np.arange(T, dtype=np.float32), inv)
            return (jnp.asarray(np.cos(ang), dtype), jnp.asarray(np.sin(ang), dtype))

        def _apply_rope(x, cos, sin):
            x1 = x[..., 0::2]
            x2 = x[..., 1::2]
            c = cos[None, :, None, :]
            s = sin[None, :, None, :]
            out = jnp.stack([x1 * c - x2 * s, x1 * s + x2 * c], axis=-1)
            return out.reshape(x.shape)
        B, T, E = x.shape
        H = N_HEAD
        D = E // H
        q = (x @ wq).reshape(B, T, H, D)
        lat = x @ w_down
        k = (lat @ wk_up).reshape(B, T, H, D)
        v = (lat @ wv_up).reshape(B, T, H, D)
        cos, sin = _rope_tables(T, D, x.dtype)
        q = _apply_rope(q, cos, sin)
        k = _apply_rope(k, cos, sin)
        scale = 1.0 / jnp.sqrt(jnp.asarray(D, x.dtype))
        scores = jnp.einsum('bqhd,bkhd->bhqk', q, k) * scale
        pages = jnp.arange(T) // PAGE_SIZE
        allowed = pages[None, :] <= pages[:, None]
        scores = jnp.where(allowed[None, None], scores, jnp.finfo(scores.dtype).min)
        attn = jax.nn.softmax(scores, axis=-1)
        out = jnp.einsum('bhqk,bkhd->bqhd', attn, v).reshape(B, T, E)
        return out @ wo

    def _L0_ffn_ref(x, Wr, W1, W2, W3):
        import jax, jax.numpy as jnp
        import numpy as np
        DIM = 512
        NUM_EXPERTS = 8
        TOP_K = 2
        HIDDEN = int(DIM * 1.5)
        B, T, C = x.shape
        xf = x.reshape(-1, C)
        gate_logits = xf @ Wr
        w, idx = jax.lax.top_k(gate_logits, TOP_K)
        w = jax.nn.softmax(w, axis=-1)
        comb = jnp.sum(w[:, :, None] * jax.nn.one_hot(idx, NUM_EXPERTS, dtype=w.dtype), axis=1)
        h = jnp.einsum('nc,ech->neh', xf, W1)
        g = jnp.einsum('nc,ech->neh', xf, W3)
        y = jnp.einsum('neh,ehc->nec', jax.nn.silu(h) * g, W2)
        out = jnp.einsum('nec,ne->nc', y, comb)
        return out.reshape(B, T, C)
    x = x + _L0_xattn_ref(_layernorm(x, axis=-1), ctx_512, L0_xattn_Wq, L0_xattn_Wkv, L0_xattn_Wo)
    x = x + _L0_attn_ref(_layernorm(x, axis=-1), L0_attn_wq, L0_attn_w_down, L0_attn_wk_up, L0_attn_wv_up, L0_attn_wo)
    x = x + _L0_ffn_ref(_layernorm(x, axis=-1), L0_ffn_Wr, L0_ffn_W1, L0_ffn_W2, L0_ffn_W3)
    return x

_drawn_inputs = setup_inputs


def setup_inputs(seed=0):
    import zlib

    import numpy as np

    out = dict(_drawn_inputs(seed))
    spreads = {}
    factors = {}
    for name, (base, spread) in spreads.items():
        noise = np.random.default_rng([zlib.crc32(name.encode()), seed]).standard_normal(out[name].shape)
        drawn = base * np.exp(spread * noise) if base else spread * noise
        out[name] = jnp.asarray(drawn.astype(out[name].dtype))
    for name, factor in factors.items():
        out[name] = (out[name] * factor).astype(out[name].dtype)
    return out
```

```python
from contextlib import ExitStack

import numpy as np

import concourse.bass as bass
from concourse import mybir
from concourse.alu_op_type import AluOpType as ALU

F32 = mybir.dt.float32
F32R = mybir.dt.float32r
I32 = mybir.dt.int32
U32 = mybir.dt.uint32
ACT = mybir.ActivationFunctionType
AX_X = mybir.AxisListType.X

P = 128
EPS = 1e-5
ROPE_THETA = 10000.0


def need(eng, sem, value):
    if isinstance(value, int) and value <= 0:
        return
    eng.wait_ge(sem, value)


def peeled(eng, n, body):
    body(0, True, n == 1)
    if n > 2:
        with eng.Fori(1, n - 1) as i:
            body(i, False, False)
    if n > 1:
        body(n - 1, False, True)


def product(pe, out, lhs, rhs, start, stop):
    (lh, ll), (rh, rl) = lhs, rhs
    pe.matmul(out, lh, rh, start=start, stop=False)
    pe.matmul(out, ll, rh, start=False, stop=False)
    return pe.matmul(out, lh, rl, start=False, stop=stop)


def rope_tables(T, D):
    inv = 1.0 / ROPE_THETA ** (np.arange(0, D, 2, dtype=np.float32) / D)
    ang = np.outer(np.arange(T, dtype=np.float32), inv)
    cos = np.repeat(np.cos(ang), 2, axis=1)
    sin = np.stack([-np.sin(ang), np.sin(ang)], axis=2).reshape(T, D)
    return np.ascontiguousarray(np.tile(np.concatenate([cos, sin], axis=1), (P // T, 1)).astype(np.float32))


def block_constants(nc, ctx):
    ident = ctx.enter_context(nc.sbuf_tensor("ident", [P, P], F32))
    quad_mask = ctx.enter_context(nc.sbuf_tensor("quad_mask", [4, 4, P], F32))
    s = ctx.enter_context(nc.semaphore("const_ready"))

    with nc.Block() as block:
        @block.gpsimd
        def _(pool):
            pool.memset(ident[:], 0.0).then_inc(s, 1)
            pool.memset(quad_mask[:], 1.0).then_inc(s, 1)
            pool.wait_ge(s, 2)
            pool.affine_select(out=ident[:], in_=ident[:], compare_op=ALU.not_equal, fill=1.0, base=0,
                               pattern=[[-1, P]], channel_multiplier=1).then_inc(s, 1)
            pool.affine_select(out=quad_mask[:], in_=quad_mask[:], compare_op=ALU.is_equal, fill=0.0, base=0,
                               pattern=[[-1, 4], [0, P]], channel_multiplier=1).then_inc(s, 1)
            pool.wait_ge(s, 4)
    return ident, quad_mask


def cross_attention(nc, ctx0, x_in, ctx_in, Wq, Wkv, Wo, x_res, ident, quad_mask, vlast_dram):
    n_tile = x_res.shape[1]
    C = x_res.shape[2]
    B, NK, L = ctx_in.shape
    KC = C // P
    KL = L // P
    NQ = C // P
    HD = 32
    BT = P // HD
    CH = 2
    LAST = CH * P
    assert NK == LAST + 1
    KW = LAST + 2
    SCALE = HD ** -0.5

    with ExitStack() as ctx:
        def sb(name, shape, dt=F32):
            return ctx.enter_context(nc.sbuf_tensor(name, shape, dt))

        def sem(name):
            return ctx.enter_context(nc.semaphore(name))

        WqT = sb("WqT", [P, KC, C])
        WoT = sb("WoT", [P, KC, C])
        Wkv_hi, Wkv_lo = sb("Wkv_hi", [P, KL, 2 * C], F32R), sb("Wkv_lo", [P, KL, 2 * C], F32R)
        zl_hi, zl_lo = sb("zl_hi", [P, KL, B], F32R), sb("zl_lo", [P, KL, B], F32R)
        Kl_hi, Kl_lo = sb("Kl_hi", [P, NQ, B], F32R), sb("Kl_lo", [P, NQ, B], F32R)
        Q_hi, Q_lo = sb("Q_hi", [P, NQ, BT, P], F32R), sb("Q_lo", [P, NQ, BT, P], F32R)
        K_hi, K_lo = sb("K_hi", [P, NQ, KW], F32R), sb("K_lo", [P, NQ, KW], F32R)
        psum = [ctx.enter_context(nc.psum_tensor(f"xa_bank{i}", [P, 512], F32)) for i in range(8)]

        with ExitStack() as setup:
            def sbs(name, shape, dt=F32):
                return setup.enter_context(nc.sbuf_tensor(name, shape, dt))
            raw_q = sbs("raw_q", [P, KC, C])
            raw_kv = sbs("raw_kv", [P, 2 * C // P, L])
            raw_o = sbs("raw_o", [P, KC, C])
            raw_zl = sbs("raw_zl", [B, L])
            vl_sb = sbs("vl_sb", [B, C])
            loaded = [setup.enter_context(nc.semaphore(f"w_loaded{i}")) for i in range(5)]
            turned = setup.enter_context(nc.semaphore("w_turned"))
            hi_done = setup.enter_context(nc.semaphore("w_hi"))
            lo_done = setup.enter_context(nc.semaphore("w_lo"))
            zeroed = setup.enter_context(nc.semaphore("w_zeroed"))
            jobs = []
            jobs.append((3, [raw_zl[:, k * P:(k + 1) * P] for k in range(KL)],
                         (zl_hi[:, :, :].rearrange("p k b -> p (k b)"), zl_lo[:, :, :].rearrange("p k b -> p (k b)")), B))
            for k in range(KL):
                for h in range(2):
                    jobs.append((1, [raw_kv[:, 4 * h + o, k * P:(k + 1) * P] for o in range(4)],
                                 (Wkv_hi[:, k, h * C:(h + 1) * C], Wkv_lo[:, k, h * C:(h + 1) * C]), P))
            for k in range(KC):
                jobs.append((0, [raw_q[:, o, k * P:(k + 1) * P] for o in range(KC)], (WqT[:, k, :], None), P))
            for k in range(KC):
                jobs.append((2, [raw_o[:, o, k * P:(k + 1) * P] for o in range(KC)], (WoT[:, k, :], None), P))
            n_split = sum(1 for j in jobs if j[2][1] is not None)

            with nc.Block() as block:
                @block.sync
                def _(sp):
                    sp.dma_start(raw_zl[:], ctx_in[:, LAST, :]).then_inc(loaded[3], 16)
                    sp.dma_start(raw_kv[:], Wkv.rearrange("(o p) c -> p o c", p=P)).then_inc(loaded[1], 16)
                    sp.dma_start(raw_q[:], Wq.rearrange("(o p) c -> p o c", p=P)).then_inc(loaded[0], 16)
                    sp.dma_start(raw_o[:], Wo.rearrange("(o p) c -> p o c", p=P)).then_inc(loaded[2], 16)
                    xt = x_in.rearrange("(i p) c -> p i c", p=P)
                    sp.dma_start(x_res[:], xt).then_inc(loaded[4], 16)
                    sp.wait_ge(hi_done, len(jobs) + 2)
                    sp.dma_start(vlast_dram, vl_sb[:]).then_inc(loaded[3], 16)
                    sp.wait_ge(loaded[3], 32)
                    sp.wait_ge(loaded[4], 16)

                @block.gpsimd
                def _(pool):
                    pool.memset(Q_hi[:].bitcast(F32), 0.0)
                    pool.memset(Q_lo[:].bitcast(F32), 0.0)
                    pool.memset(K_hi[:].bitcast(F32), 0.0)
                    pool.memset(K_lo[:].bitcast(F32), 0.0).then_inc(zeroed, 1)
                    pool.wait_ge(zeroed, 1)

                @block.tensor
                def _(pe):
                    for n, (load, blocks, _dst, width) in enumerate(jobs):
                        pe.wait_ge(loaded[load], 16)
                        if n >= 6:
                            pe.wait_ge(hi_done, n - 5)
                            if n - 6 < n_split:
                                pe.wait_ge(lo_done, n - 5)
                        for o, src in enumerate(blocks):
                            mm = pe.transpose(psum[n % 6][:, o * width:(o + 1) * width], src,
                                              ident[0:src.shape[0], 0:src.shape[0]])
                        mm.then_inc(turned, 1)
                    pe.wait_ge(lo_done, n_split)
                    for m in range(NQ):
                        for k in range(KL):
                            mm = product(pe, psum[6][:, m * B:(m + 1) * B],
                                         (Wkv_hi[:, k, m * P:(m + 1) * P], Wkv_lo[:, k, m * P:(m + 1) * P]),
                                         (zl_hi[:, k, :], zl_lo[:, k, :]), k == 0, k == KL - 1)
                    mm.then_inc(turned, 1)
                    for k in range(KL):
                        mm = product(pe, psum[7][0:B, :], (zl_hi[:, k, :], zl_lo[:, k, :]),
                                     (Wkv_hi[:, k, C:2 * C], Wkv_lo[:, k, C:2 * C]), k == 0, k == KL - 1)
                    mm.then_inc(turned, 1)

                @block.scalar
                def _(act):
                    for n, (_load, blocks, (hi, _lo), width) in enumerate(jobs):
                        act.wait_ge(turned, n + 1)
                        act.copy(hi, psum[n % 6][:, 0:len(blocks) * width]).then_inc(hi_done, 1)
                    act.wait_ge(turned, len(jobs) + 1)
                    act.copy(Kl_hi[:].rearrange("p m b -> p (m b)"), psum[6][:, 0:NQ * B]).then_inc(hi_done, 1)
                    act.wait_ge(turned, len(jobs) + 2)
                    act.copy(vl_sb[:], psum[7][0:B, :]).then_inc(hi_done, 1)

                @block.vector
                def _(dve):
                    for n, (_load, blocks, (hi, lo), width) in enumerate(jobs[:n_split]):
                        dve.wait_ge(hi_done, n + 1)
                        dve.tensor_tensor(lo, psum[n % 6][:, 0:len(blocks) * width], hi.bitcast(F32),
                                          ALU.subtract).then_inc(lo_done, 1)
                    dve.wait_ge(hi_done, len(jobs) + 1)
                    dve.tensor_tensor(Kl_lo[:].rearrange("p m b -> p (m b)"), psum[6][:, 0:NQ * B],
                                      Kl_hi[:].bitcast(F32).rearrange("p m b -> p (m b)"),
                                      ALU.subtract).then_inc(lo_done, 1)
                    dve.wait_ge(lo_done, n_split + 1)

        z_in = sb("z_in", [P, BT, CH, L])
        v_last = sb("v_last", [NQ, BT, P])
        zT_hi, zT_lo = sb("zT_hi", [P, KL, CH, P], F32R), sb("zT_lo", [P, KL, CH, P], F32R)
        V = sb("V", [P, 2, CH, C])
        Pr = sb("Pr", [P, NQ, KW])
        PT = sb("PT", [P, CH, NQ, P])
        PL = sb("PL", [NQ, NQ, P])
        OT = sb("OT", [P, NQ, P])
        xn = sb("xn", [P, C])
        xnT = sb("xnT", [P, KC, P])
        nmax = sb("nmax", [P, NQ])
        rsum = sb("rsum", [P, NQ])
        rinv = sb("rinv", [P, NQ])
        st6 = sb("st6", [P, 6])
        mv = sb("mv", [P, 2])
        rstd = sb("rstd", [P, 1])
        mhalf = sb("mhalf", [P, 1])
        waiter = sb("waiter", [P, 1])
        bank_misc, bank_kv, bank_s, bank_pt, bank_o = psum[0], psum[1:3], psum[3:5], psum[5:7], psum[7]

        z_got = [sem(f"z_got{j}") for j in range(BT)]
        vl_got = [sem(f"vl_got{j}") for j in range(BT)]
        pe_T, pe_K, pe_V, pe_S = sem("pe_T"), sem("pe_K"), sem("pe_V"), sem("pe_S")
        pe_PT, pe_PL, pe_O = sem("pe_PT"), sem("pe_PL"), sem("pe_O")
        pe_X, pe_Q, pe_OP = sem("pe_X"), sem("pe_Q"), sem("pe_OP")
        a_T, a_K, a_V, a_E, a_PT, a_O = (sem(n) for n in ("a_T", "a_K", "a_V", "a_E", "a_PT", "a_O"))
        a_X, a_Q = sem("a_X"), sem("a_Q")
        v_T, v_K, v_mx, v_N, v_PT, v_PL, v_O = (sem(n) for n in ("v_T", "v_K", "v_mx", "v_N", "v_PT", "v_PL", "v_O"))
        v_R = sem("v_R")
        v_Q, v_OP, v_ln = sem("v_Q"), sem("v_OP"), sem("v_ln")
        g_K, g_ln = sem("g_K"), sem("g_ln")
        mh = sem("mhalf_set")
        LN = 4

        with nc.Block() as block:
            @block.sync
            def _(sp):
                def body(i, first, last):
                    for j in range(BT):
                        s = BT * i + j
                        need(sp, pe_T, s - BT + 1)
                        b = i * BT + j
                        sp.dma_start(z_in[:, j, :, :], ctx_in[b, 0:LAST, :].rearrange("(p c) l -> p c l", c=CH)
                                     ).then_inc(z_got[j], 16)
                        need(sp, pe_O, s - BT + 1)
                        sp.dma_start(v_last[:, j, :], vlast_dram[b].rearrange("(m q) -> m q", q=P)
                                     ).then_inc(vl_got[j], 16)
                peeled(sp, n_tile, body)

            def transpose_z(pe, s, i, j):
                pe.wait_ge(z_got[j], 16 * i + 16)
                for k in range(KL):
                    for c in range(CH):
                        at = (k * CH + c) * P
                        mm = pe.transpose(bank_misc[:, at:at + P], z_in[:, j, c, k * P:(k + 1) * P], ident[:])
                mm.then_inc(pe_T, 1)

            def turn_x(pe, i):
                pe.wait_ge(v_ln, LN * i + 4)
                for k in range(KC):
                    mm = pe.transpose(bank_misc[:, k * P:(k + 1) * P], xn[:, k * P:(k + 1) * P], ident[:])
                mm.then_inc(pe_X, 1)

            def project_q(pe, i):
                pe.wait_ge(a_X, i + 1)
                for m in range(NQ):
                    for k in range(KC):
                        mm = pe.matmul(bank_misc[:, m * P:(m + 1) * P], WqT[:, k, m * P:(m + 1) * P], xnT[:, k, :],
                                       start=(k == 0), stop=(k == KC - 1))
                mm.then_inc(pe_Q, 1)

            @block.tensor
            def _(pe):
                def turn_p(s):
                    for c in range(CH):
                        pe.wait_ge(v_N, s + 1)
                        need(pe, v_PT if c == 0 else a_PT, s)
                        for m in range(NQ):
                            mm = pe.transpose(bank_pt[c][:, m * P:(m + 1) * P], Pr[:, m, c * P:(c + 1) * P], ident[:])
                        mm.then_inc(pe_PT, 1)

                def turn_last(s, i):
                    pe.wait_ge(a_Q, i + 1)
                    pe.wait_ge(v_Q, i + 1)
                    pe.transpose(bank_misc[0:NQ, 0:P], Pr[:, :, LAST], ident[:]).then_inc(pe_PL, 1)

                def values(s, i, j):
                    pe.wait_ge(vl_got[j], 16 * i + 16)
                    pe.wait_ge(v_PL, s + 1)
                    need(pe, a_O, s)
                    need(pe, v_O, s)
                    pe.matmul(bank_o[:], v_last[:, j, :], PL[:].rearrange("a m q -> a (m q)"), start=True, stop=False,
                              skip_group_check=True)
                    pe.wait_ge(a_V, 2 * s + 2)
                    pe.wait_ge(v_PT, s + 1)
                    pe.wait_ge(a_PT, s + 1)
                    for c in range(CH):
                        for m in range(NQ):
                            mm = pe.matmul(bank_o[:, m * P:(m + 1) * P], V[:, j % 2, c, m * P:(m + 1) * P],
                                           PT[:, c, m, :], start=False, stop=(c == CH - 1), skip_group_check=True)
                    mm.then_inc(pe_O, 1)

                def project_o(i):
                    pe.wait_ge(a_O, BT * i + BT)
                    pe.wait_ge(v_O, BT * i + BT)
                    for m in range(NQ):
                        mm = pe.matmul(bank_misc[:], OT[:, m, :], WoT[:, m, :], start=(m == 0), stop=(m == NQ - 1))
                    mm.then_inc(pe_OP, 1)

                turn_x(pe, 0)
                project_q(pe, 0)
                pe.wait_ge(a_Q, 1)
                pe.wait_ge(v_Q, 1)
                transpose_z(pe, 0, 0, 0)

                def body(i, first, last):
                    for j in range(BT):
                        s = BT * i + j
                        some = not (first and j == 0)
                        pe.wait_ge(a_T, s + 1)
                        pe.wait_ge(v_T, s + 1)
                        for h in range(2):
                            need(pe, a_V, 2 * s + h - 1)
                            for m in (2 * h, 2 * h + 1):
                                for k in range(KL):
                                    mm = product(pe, bank_kv[h][:, (m % 2) * LAST:(m % 2 + 1) * LAST],
                                                 (Wkv_hi[:, k, m * P:(m + 1) * P], Wkv_lo[:, k, m * P:(m + 1) * P]),
                                                 (zT_hi[:, k].rearrange("p c q -> p (c q)"),
                                                  zT_lo[:, k].rearrange("p c q -> p (c q)")),
                                                 k == 0, k == KL - 1)
                            mm.then_inc(pe_K, 1)
                        if some:
                            turn_p(s - 1)
                            turn_last(s - 1, i)
                        for c in range(CH):
                            pe.wait_ge(a_K, 2 * s + c + 1)
                            pe.wait_ge(v_K, 2 * s + c + 1)
                            for k in range(KL):
                                mm = product(pe, bank_kv[c][:], (zT_hi[:, k, c, :], zT_lo[:, k, c, :]),
                                             (Wkv_hi[:, k, C:2 * C], Wkv_lo[:, k, C:2 * C]), k == 0, k == KL - 1)
                            mm.then_inc(pe_V, 1)
                        if j == 1 and not first:
                            pe.wait_ge(v_PL, s)
                            project_o(i - 1)
                        if j == 2 and not last:
                            pe.wait_ge(v_PL, s)
                            turn_x(pe, i + 1)
                        pe.wait_ge(a_Q, i + 1)
                        pe.wait_ge(v_Q, i + 1)
                        pe.wait_ge(g_K, s + 1)
                        for m in range(NQ):
                            pe.wait_ge(v_K, 2 * s + m // 2 + 1)
                            need(pe, a_E, 4 * s + m - 1)
                            mm = product(pe, bank_s[m % 2][:, 0:KW], (Q_hi[:, m, j, :], Q_lo[:, m, j, :]),
                                         (K_hi[:, m, :], K_lo[:, m, :]), True, True)
                            mm.then_inc(pe_S, 1)
                        if not (last and j == BT - 1):
                            need(pe, v_PL, s)
                            if j == 1 and not first:
                                pe.wait_ge(v_OP, i)
                            if j == 2 and not last:
                                pe.wait_ge(a_X, i + 2)
                            transpose_z(pe, s + 1, i + (j + 1) // BT, (j + 1) % BT)
                        if some:
                            values(s - 1, i if j else i - 1, (j - 1) % BT)
                        if j == BT - 1 and not last:
                            pe.wait_ge(a_T, s + 2)
                            pe.wait_ge(v_T, s + 2)
                            project_q(pe, i + 1)
                peeled(pe, n_tile, body)
                s_end = BT * n_tile
                turn_p(s_end - 1)
                turn_last(s_end - 1, n_tile - 1)
                values(s_end - 1, n_tile - 1, BT - 1)
                pe.wait_ge(v_PL, s_end)
                project_o(n_tile - 1)

            def own_heads(eng, i, j, hhs, done, pe_first):
                for hh in hhs:
                    r = slice(hh * HD, (hh + 1) * HD)
                    src = bank_o[r, :].rearrange("p (m q) -> p m q", m=NQ)[:, :, hh * HD:(hh + 1) * HD]
                    dst = OT[r, :, j * HD:(j + 1) * HD]
                    op = eng.copy(dst, src) if pe_first else eng.tensor_copy(dst, src)
                op.then_inc(done, 1)

            @block.scalar
            def _(act):
                def z_hi(s):
                    act.wait_ge(pe_T, s + 1)
                    act.copy(zT_hi[:].rearrange("p k c q -> p (k c q)"), bank_misc[:]).then_inc(a_T, 1)

                def x_out(i):
                    act.wait_ge(pe_X, i + 1)
                    act.copy(xnT[:].rearrange("p k q -> p (k q)"), bank_misc[:]).then_inc(a_X, 1)

                def q_hi(i):
                    act.wait_ge(pe_Q, i + 1)
                    for hh in range(4):
                        r = slice(hh * HD, (hh + 1) * HD)
                        src = bank_misc[r, :].rearrange("p (m b t) -> p m b t", m=NQ, b=BT)
                        op = act.mul(Q_hi[r, :, :, hh * HD:(hh + 1) * HD], src, SCALE)
                    op.then_inc(a_Q, 1)

                def pt_out(s):
                    act.wait_ge(pe_PT, 2 * s + 2)
                    act.copy(PT[:, 1].rearrange("p m q -> p (m q)"), bank_pt[1][:]).then_inc(a_PT, 1)

                def o_out(s, i, j):
                    act.wait_ge(pe_O, s + 1)
                    if j == 0:
                        need(act, pe_OP, i)
                    own_heads(act, i, j, (0, 1), a_O, True)

                x_out(0)
                q_hi(0)
                z_hi(0)

                def body(i, first, last):
                    for j in range(BT):
                        s = BT * i + j
                        some = not (first and j == 0)
                        for h in range(2):
                            act.wait_ge(pe_K, 2 * s + h + 1)
                            act.copy(K_hi[:, 2 * h:2 * h + 2, 0:LAST],
                                     bank_kv[h][:].rearrange("p (m q) -> p m q", m=2)).then_inc(a_K, 1)
                        if some:
                            pt_out(s - 1)
                        for c in range(CH):
                            act.wait_ge(pe_V, 2 * s + c + 1)
                            act.copy(V[:, j % 2, c, :], bank_kv[c][:]).then_inc(a_V, 1)
                        if j == 2 and not last:
                            x_out(i + 1)
                        for m in range(NQ):
                            act.wait_ge(v_mx, 4 * s + m + 1)
                            if m == 0:
                                need(act, pe_PL, s)
                                need(act, v_R, s)
                            act.activation(Pr[:, m, 0:NK], bank_s[m % 2][:, 0:NK], ACT.Exp, bias=nmax[:, m:m + 1],
                                           scale=1.0, accum_out=rsum[:, m:m + 1]).then_inc(a_E, 1)
                        if not (last and j == BT - 1):
                            z_hi(s + 1)
                        if some:
                            o_out(s - 1, i if j else i - 1, (j - 1) % BT)
                        if j == BT - 1 and not last:
                            q_hi(i + 1)
                peeled(act, n_tile, body)
                s_end = BT * n_tile
                pt_out(s_end - 1)
                o_out(s_end - 1, n_tile - 1, BT - 1)

            @block.vector
            def _(dve):
                def z_lo(s):
                    dve.wait_ge(a_T, s + 1)
                    dve.tensor_tensor(zT_lo[:].rearrange("p k c q -> p (k c q)"), bank_misc[:],
                                      zT_hi[:].bitcast(F32).rearrange("p k c q -> p (k c q)"),
                                      ALU.subtract).then_inc(v_T, 1)

                def normalise(i):
                    need(dve, pe_X, i)
                    dve.bn_stats(st6[:], x_res[:, i, :]).then_inc(v_ln, 1)
                    dve.wait_ge(v_ln, LN * i + 1)
                    dve.memset(waiter[:], 0.0)
                    dve.bn_aggr(mv[:], st6[:]).then_inc(v_ln, 1)
                    dve.wait_ge(v_ln, LN * i + 2)
                    dve.tensor_scalar(mv[:, 1:2], mv[:, 1:2], EPS, None, ALU.add).then_inc(v_ln, 1)
                    dve.wait_ge(g_ln, i + 1)
                    dve.tensor_scalar(xn[:], x_res[:, i, :], mv[:, 0:1], rstd[:], ALU.subtract, ALU.mult
                                      ).then_inc(v_ln, 1)

                def q_lo(i):
                    dve.wait_ge(a_Q, i + 1)
                    for hh in range(4):
                        r = slice(hh * HD, (hh + 1) * HD)
                        for m in range(NQ):
                            c = slice(hh * HD, (hh + 1) * HD)
                            op = dve.scalar_tensor_tensor(
                                Q_lo[r, m, :, c],
                                bank_misc[r, m * P:(m + 1) * P].rearrange("p (b t) -> p b t", b=BT), SCALE,
                                Q_hi[r, m, :, c].bitcast(F32), ALU.mult, ALU.subtract)
                    op.then_inc(v_Q, 1)

                def pt_out(s):
                    dve.wait_ge(pe_PT, 2 * s + 1)
                    need(dve, pe_O, s)
                    dve.tensor_copy(PT[:, 0].rearrange("p m q -> p (m q)"), bank_pt[0][:]).then_inc(v_PT, 1)
                    dve.wait_ge(pe_PL, s + 1)
                    dve.tensor_tensor(PL[:], bank_misc[0:NQ, 0:P].unsqueeze(1).to_broadcast([NQ, NQ, P]),
                                      quad_mask[:], ALU.mult).then_inc(v_PL, 1)

                def o_out(s, i, j):
                    dve.wait_ge(pe_O, s + 1)
                    if j == 0:
                        need(dve, pe_OP, i)
                    own_heads(dve, i, j, (2, 3), v_O, False)

                def add_residual(i):
                    dve.wait_ge(pe_OP, i + 1)
                    dve.tensor_tensor(x_res[:, i, :], bank_misc[:], x_res[:, i, :], ALU.add).then_inc(v_OP, 1)

                normalise(0)
                q_lo(0)
                z_lo(0)

                def body(i, first, last):
                    for j in range(BT):
                        s = BT * i + j
                        some = not (first and j == 0)
                        for h in range(2):
                            dve.wait_ge(a_K, 2 * s + h + 1)
                            dve.tensor_tensor(K_lo[:, 2 * h:2 * h + 2, 0:LAST],
                                              bank_kv[h][:].rearrange("p (m q) -> p m q", m=2),
                                              K_hi[:, 2 * h:2 * h + 2, 0:LAST].bitcast(F32),
                                              ALU.subtract).then_inc(v_K, 1)
                        if some:
                            pt_out(s - 1)
                        if j == 1 and not first:
                            add_residual(i - 1)
                        if j == 1 and not last:
                            normalise(i + 1)
                        for m in range(NQ):
                            dve.wait_ge(pe_S, 4 * s + m + 1)
                            if m == 0:
                                need(dve, a_E, 4 * s)
                            dve.tensor_reduce(nmax[:, m:m + 1], bank_s[m % 2][:, 0:NK], AX_X, ALU.max,
                                              negate=True).then_inc(v_mx, 1)
                        if not (last and j == BT - 1):
                            z_lo(s + 1)
                        dve.wait_ge(a_E, 4 * s + 4)
                        dve.reciprocal(rinv[:], rsum[:]).then_inc(v_R, 1)
                        dve.wait_ge(v_R, s + 1)
                        for m in range(NQ):
                            op = dve.tensor_scalar(Pr[:, m, 0:NK], Pr[:, m, 0:NK], rinv[:, m:m + 1], None, ALU.mult)
                        op.then_inc(v_N, 1)
                        if some:
                            o_out(s - 1, i if j else i - 1, (j - 1) % BT)
                        if j == BT - 1 and not last:
                            q_lo(i + 1)
                peeled(dve, n_tile, body)
                s_end = BT * n_tile
                pt_out(s_end - 1)
                o_out(s_end - 1, n_tile - 1, BT - 1)
                add_residual(n_tile - 1)
                dve.wait_ge(v_OP, n_tile)

            @block.gpsimd
            def _(pool):
                pool.memset(mhalf[:], -0.5).then_inc(mh, 1)
                pool.wait_ge(mh, 1)

                def rstd_of(i):
                    pool.wait_ge(v_ln, LN * i + 3)
                    need(pool, v_ln, LN * i)
                    pool.tensor_tensor(rstd[:], mv[:, 1:2], mhalf[:], ALU.pow).then_inc(g_ln, 1)

                rstd_of(0)

                def body(i, first, last):
                    for j in range(BT):
                        s = BT * i + j
                        need(pool, pe_S, 4 * s)
                        b = i * BT + j
                        pool.tensor_copy(K_hi[:, :, LAST], Kl_hi[:, :, bass.ds(b, 1)].rearrange("p m o -> p (m o)"))
                        pool.tensor_copy(K_lo[:, :, LAST], Kl_lo[:, :, bass.ds(b, 1)].rearrange("p m o -> p (m o)")
                                         ).then_inc(g_K, 1)
                        if j == 1 and not last:
                            rstd_of(i + 1)
                peeled(pool, n_tile, body)


class Steps:

    def __init__(self, sem, names):
        self.sem, self.names, self.next = sem, names.split(), 0

    def done(self, op, name):
        assert self.names[self.next] == name, (name, self.names[self.next])
        self.next = (self.next + 1) % len(self.names)
        return op.then_inc(self.sem, 1)

    def wait(self, eng, i, name):
        need(eng, self.sem, len(self.names) * i + self.names.index(name) + 1)


def layernorm(dve, steps, pool_steps, i, suffix, x, st6, mv, rstd, out, waiter, before_out):
    dve.memset(waiter[:], 0.0)
    steps.done(dve.bn_stats(st6[:], x), "stats" + suffix)
    steps.wait(dve, i, "stats" + suffix)
    dve.memset(waiter[:], 0.0)
    steps.done(dve.bn_aggr(mv[:], st6[:]), "aggr" + suffix)
    steps.wait(dve, i, "aggr" + suffix)
    steps.done(dve.tensor_scalar(mv[:, 1:2], mv[:, 1:2], EPS, None, ALU.add), "eps" + suffix)
    before_out()
    pool_steps.wait(dve, i, "rstd" + suffix)
    steps.done(dve.tensor_scalar(out[:], x, mv[:, 0:1], rstd[:], ALU.subtract, ALU.mult), "xn" + suffix)


def self_attention_and_routing(nc, wq, w_down, wk_up, wv_up, wo, Wr, rope, x_res, ident, xs_dram,
                               gate_w, row_all, pick_all, count, region, Tlen):
    n_tile, C = x_res.shape[1], x_res.shape[2]
    E = Wr.shape[1]
    L = w_down.shape[1]
    KC, KL, NQ, HD, BT = C // P, L // P, C // P, 32, P // Tlen
    NH = C // HD
    SCALE = HD ** -0.5
    assert HD == Tlen

    with ExitStack() as ctx:
        def sb(name, shape, dt=F32):
            return ctx.enter_context(nc.sbuf_tensor(name, shape, dt))

        def steps(name, names):
            return Steps(ctx.enter_context(nc.semaphore(name)), names)

        Wq, Wdown = sb("sa_wq", [P, KC, C]), sb("sa_down", [P, KC, L])
        Wk, Wv, Wo = sb("sa_wk", [P, KL, C]), sb("sa_wv", [P, KL, C]), sb("sa_wo", [P, KC, C])
        Wg = sb("sa_wr", [P, KC, E])
        rope_t = sb("rope_t", [P, 2, HD])
        below = sb("below", [P, P])
        ones = sb("ones", [P, P])
        rank8 = sb("rank8", [P, E])
        start8 = sb("start8", [P, E])
        mhalf = sb("sa_mhalf", [P, 1])
        xn, xnT = sb("sa_xn", [P, C]), sb("sa_xnT", [P, KC, P])
        latT = sb("latT", [P, KL, P])
        tq1, tq2, tk1, tk2 = (sb(n, [P, C]) for n in ("tq1", "tq2", "tk1", "tk2"))
        qr, kr = sb("qr", [P, C]), sb("kr", [P, C])
        Vt = sb("Vt", [P, C])
        Qd = sb("Qd", [P, NQ, BT, P])
        KT = sb("sa_KT", [P, NQ, P])
        Ex, Pm = sb("Ex", [P, NQ * BT, Tlen]), sb("Pm", [P, NQ, P])
        mx, sm, ri = sb("mx", [P, NQ * BT]), sb("sm", [P, NQ * BT]), sb("ri", [P, NQ * BT])
        PTd = sb("PTd", [P, NQ, BT, P])
        OT = sb("sa_OT", [P, NQ, P])
        xn2, xn2T = sb("xn2", [P, C]), sb("xn2T", [P, KC, P])
        st6, mv, rstd = sb("sa_st6", [P, 6]), sb("sa_mv", [P, 2]), sb("sa_rstd", [P, 1])
        st6b, mvb, rstdb = sb("sb_st6", [P, 6]), sb("sb_mv", [P, 2]), sb("sb_rstd", [P, 1])
        waiter, carrier = sb("sa_waiter", [P, 1]), sb("sa_carrier", [P, 1])
        lg, cand = sb("lg", [P, E]), sb("cand", [P, E])
        oh = sb("oh", [P, 2, E])
        best, top = sb("best", [P, 2]), sb("top", [P, 2])
        both, dest = sb("both", [P, E]), sb("dest", [P, E])
        prod, posf = sb("prod", [P, 2, E]), sb("posf", [P, 2])
        idx = sb("idx", [P, 2], U32)
        dl, ex = sb("dl", [P, 1]), sb("ex", [P, 2])
        bank = [ctx.enter_context(nc.psum_tensor(f"sa_bank{i}", [P, 512], F32)) for i in range(8)]

        w_got = ctx.enter_context(nc.semaphore("sa_w_got"))
        c_set = ctx.enter_context(nc.semaphore("sa_c_set"))
        sent = ctx.enter_context(nc.semaphore("rows_sent"))
        pA, aA = steps("pA", "XT Q lat K V"), steps("aA", "xnT latT V")
        vL, gL = steps("vL", "stats aggr eps xn"), steps("gL", "rstd")
        vA, gA = steps("vA", "q k"), steps("gA", "qr kr")
        pB, aB, vB = steps("pB", "QT KT S"), steps("aB", "q kt exp"), steps("vB", "q mx sub sum rec prob")
        pC, pO, pD = steps("pC", "PT PV0 PV1 PV2 PV3"), steps("pO", "OP"), steps("pD", "XT2 G R")
        aC, aD = steps("aC", "pt ov0 ov1 ov2 ov3"), steps("aD", "xt2 ew")
        vC = steps("vC", "pt ov0 ov1 ov2 ov3 add")
        vD = steps("vD", "stats2 aggr2 eps2 xn2 lg top0 eq0 best0 oh0 less top1 eq1 best1 oh1 both dl e1 w0 w1 "
                         "dest prod pos idx cnt")
        gD = steps("gD", "rstd2")
        n_w = 7

        def has(i, k):
            return not isinstance(i, int) or i + k < n_tile

        def tiles(eng, body):
            body(0)
            if n_tile > 3:
                with eng.Fori(1, n_tile - 2) as i:
                    body(i)
            for i in range(max(1, n_tile - 2), n_tile):
                body(i)

        with nc.Block() as block:
            @block.sync
            def _(sp):
                for dst, src in ((Wq, wq), (Wdown, w_down), (Wk, wk_up), (Wv, wv_up), (Wo, wo), (Wg, Wr)):
                    sp.dma_start(dst[:], src.rearrange("(k p) c -> p k c", p=P)).then_inc(w_got, 16)
                sp.dma_start(rope_t[:], rope.rearrange("p (a d) -> p a d", a=2)).then_inc(w_got, 16)

            @block.tensor
            def _(pe):
                def A_turn(i):
                    vL.wait(pe, i, "xn")
                    vC.wait(pe, i - 2, "add")
                    for k in range(KC):
                        mm = pe.transpose(bank[0][:, k * P:(k + 1) * P], xn[:, k * P:(k + 1) * P], ident[:])
                    pA.done(mm, "XT")

                def A_q(i):
                    aA.wait(pe, i, "xnT")
                    for k in range(KC):
                        mm = pe.matmul(bank[1][:], xnT[:, k, :], Wq[:, k, :], start=(k == 0), stop=(k == KC - 1))
                    pA.done(mm, "Q")

                def A_lat(i):
                    vA.wait(pe, i - 1, "k")
                    for m in range(KL):
                        for k in range(KC):
                            mm = pe.matmul(bank[2][:, m * P:(m + 1) * P], Wdown[:, k, m * P:(m + 1) * P],
                                           xnT[:, k, :], start=(k == 0), stop=(k == KC - 1))
                    pA.done(mm, "lat")

                def A_k(i):
                    aA.wait(pe, i, "latT")
                    for k in range(KL):
                        mm = pe.matmul(bank[2][:], latT[:, k, :], Wk[:, k, :], start=(k == 0), stop=(k == KL - 1))
                    pA.done(mm, "K")

                def A_v(i):
                    aA.wait(pe, i - 1, "V")
                    for k in range(KL):
                        mm = pe.matmul(bank[3][:], latT[:, k, :], Wv[:, k, :], start=(k == 0), stop=(k == KL - 1))
                    pA.done(mm, "V")

                def C_turn(i):
                    vD.wait(pe, i, "xn2")
                    if has(i, 2):
                        aA.wait(pe, i + 2, "xnT")
                    for k in range(KC):
                        mm = pe.transpose(bank[0][:, k * P:(k + 1) * P], xn2[:, k * P:(k + 1) * P], ident[:])
                    pD.done(mm, "XT2")

                def C_gate(i):
                    aD.wait(pe, i, "xt2")
                    for k in range(KC):
                        mm = pe.matmul(bank[0][:, 0:E], xn2T[:, k, :], Wg[:, k, :], start=(k == 0), stop=(k == KC - 1))
                    pD.done(mm, "G")

                def C_rank(i):
                    vD.wait(pe, i, "both")
                    pe.matmul(bank[0][:, 2 * E:3 * E], below[:], both[:], start=True, stop=True)
                    pD.done(pe.matmul(bank[0][:, 3 * E:4 * E], ones[:], both[:], start=True, stop=True), "R")

                pe.wait_ge(w_got, 16 * n_w)
                A_turn(0)
                A_q(0)
                A_lat(0)
                A_k(0)
                A_v(0)

                def body(i):
                    gA.wait(pe, i, "qr")
                    aB.wait(pe, i - 1, "exp")
                    for m in range(NQ):
                        mm = pe.transpose(bank[4][:, m * P:(m + 1) * P], qr[:, m * P:(m + 1) * P], ident[:])
                    pB.done(mm, "QT")
                    gA.wait(pe, i, "kr")
                    aC.wait(pe, i - 1, "pt")
                    vC.wait(pe, i - 1, "pt")
                    for m in range(NQ):
                        mm = pe.transpose(bank[5][:, m * P:(m + 1) * P], kr[:, m * P:(m + 1) * P], ident[:])
                    pB.done(mm, "KT")
                    if has(i, 1):
                        A_turn(i + 1)
                        A_q(i + 1)
                    aB.wait(pe, i, "q")
                    vB.wait(pe, i, "q")
                    aB.wait(pe, i, "kt")
                    for m in range(NQ):
                        for b in range(BT):
                            at = (m * BT + b) * Tlen
                            mm = pe.matmul(bank[4][:, at:at + Tlen], Qd[:, m, b, :],
                                           KT[:, m, b * Tlen:(b + 1) * Tlen], start=True, stop=True)
                    pB.done(mm, "S")
                    if has(i, 1):
                        A_lat(i + 1)
                        A_k(i + 1)
                    if not (isinstance(i, int) and i == 0):
                        C_turn(i - 1)
                        C_gate(i - 1)
                    vB.wait(pe, i, "prob")
                    for m in range(NQ):
                        mm = pe.transpose(bank[5][:, m * P:(m + 1) * P], Pm[:, m, :], ident[:])
                    pC.done(mm, "PT")
                    aC.wait(pe, i, "pt")
                    vC.wait(pe, i, "pt")
                    for m in range(NQ):
                        g = i if m > 1 else i - 1
                        aC.wait(pe, g, f"ov{(m - 2) % NQ}")
                        vC.wait(pe, g, f"ov{(m - 2) % NQ}")
                        mm = pe.matmul(bank[6 + m % 2][:], Vt[:, m * P:(m + 1) * P],
                                       PTd[:, m].rearrange("p b q -> p (b q)"), start=True, stop=True)
                        pC.done(mm, f"PV{m}")
                    if has(i, 1):
                        A_v(i + 1)
                    if not (isinstance(i, int) and i == 0):
                        C_rank(i - 1)
                    aC.wait(pe, i, "ov3")
                    vC.wait(pe, i, "ov3")
                    if has(i, 1):
                        vA.wait(pe, i + 1, "q")
                    for m in range(NQ):
                        mm = pe.matmul(bank[1][:], OT[:, m, :], Wo[:, m, :], start=(m == 0), stop=(m == NQ - 1))
                    pO.done(mm, "OP")
                tiles(pe, body)
                C_turn(n_tile - 1)
                C_gate(n_tile - 1)
                C_rank(n_tile - 1)

            def own(eng, copy, dst, src, parts):
                for q in parts:
                    op = copy(dst(q), src(q))
                return op

            rows = [slice(q * HD, (q + 1) * HD) for q in range(4)]

            def split_q(eng, copy, parts):
                return own(eng, copy, lambda q: Qd[rows[q], :, :, rows[q]],
                           lambda q: bank[4][rows[q], :].rearrange("p (m b t) -> p m b t", m=NQ, b=BT), parts)

            def split_p(eng, copy, parts):
                return own(eng, copy, lambda q: PTd[rows[q], :, q, :],
                           lambda q: bank[5][rows[q], :].rearrange("p (m q) -> p m q", m=NQ), parts)

            def merge_o(eng, copy, m, parts):
                return own(eng, copy, lambda q: OT[rows[q], m, :].rearrange("p (b t) -> p b t", b=BT),
                           lambda q: bank[6 + m % 2][rows[q], :].rearrange("p (b q) -> p b q", b=BT)[:, :, rows[q]],
                           parts)

            @block.scalar
            def _(act):
                def out(b, n=C):
                    return bank[b][:, 0:n].rearrange("p (k q) -> p k q", q=P)

                def A_xnT(i):
                    pA.wait(act, i, "XT")
                    aA.done(act.copy(xnT[:], out(0)), "xnT")

                def A_lat(i):
                    pA.wait(act, i, "lat")
                    aA.done(act.copy(latT[:], out(2, L)), "latT")

                def A_v(i):
                    pA.wait(act, i, "V")
                    aA.done(act.copy(Vt[:], bank[3][:]), "V")

                def D_turn(i):
                    pD.wait(act, i, "XT2")
                    aD.done(act.copy(xn2T[:], out(0)), "xt2")

                def D_weight(i):
                    vD.wait(act, i, "dl")
                    aD.done(act.activation(ex[:, 0:1], dl[:], ACT.Exp), "ew")

                act.wait_ge(c_set, 8)
                A_xnT(0)
                A_lat(0)
                A_v(0)

                def body(i):
                    pB.wait(act, i, "QT")
                    aB.done(split_q(act, act.copy, (0, 1)), "q")
                    pB.wait(act, i, "KT")
                    aB.done(act.copy(KT[:], out(5)), "kt")
                    if has(i, 1):
                        A_xnT(i + 1)
                    vB.wait(act, i, "sub")
                    aB.done(act.activation(Ex[:], Ex[:], ACT.Exp, scale=SCALE), "exp")
                    if has(i, 1):
                        A_lat(i + 1)
                    if not (isinstance(i, int) and i == 0):
                        D_turn(i - 1)
                    pC.wait(act, i, "PT")
                    aC.done(split_p(act, act.copy, (0, 1)), "pt")
                    for m in range(NQ):
                        pC.wait(act, i, f"PV{m}")
                        if m == 0:
                            pO.wait(act, i - 1, "OP")
                        aC.done(merge_o(act, act.copy, m, (0, 1)), f"ov{m}")
                        if m == 0 and not (isinstance(i, int) and i == 0):
                            D_weight(i - 1)
                    if has(i, 1):
                        A_v(i + 1)
                tiles(act, body)
                D_turn(n_tile - 1)
                D_weight(n_tile - 1)

            @block.vector
            def _(dve):
                def A_norm(i):
                    layernorm(dve, vL, gL, i, "", x_res[:, i, :], st6, mv, rstd, xn, waiter,
                              lambda: pA.wait(dve, i - 1, "XT"))

                def rotate(src, t1, t2):
                    heads = "p (h d) -> p h d"
                    dve.tensor_tensor(t1[:].rearrange(heads, h=NH), src.rearrange(heads, h=NH),
                                      rope_t[:, 0, :].unsqueeze(1).to_broadcast([P, NH, HD]), ALU.mult)
                    pair = "p (h f e) -> p h f e"
                    for e in range(2):
                        op = dve.tensor_tensor(
                            t2[:].rearrange(pair, h=NH, e=2)[:, :, :, e], src.rearrange(pair, h=NH, e=2)[:, :, :, 1 - e],
                            rope_t[:, 1, :].rearrange("p (f e) -> p f e", e=2)[:, :, e].unsqueeze(1)
                            .to_broadcast([P, NH, HD // 2]), ALU.mult)
                    return op

                def A_q(i):
                    pA.wait(dve, i, "Q")
                    gA.wait(dve, i - 1, "qr")
                    vA.done(rotate(bank[1][:], tq1, tq2), "q")

                def A_k(i):
                    pA.wait(dve, i, "K")
                    gA.wait(dve, i - 1, "kr")
                    vA.done(rotate(bank[2][:], tk1, tk2), "k")

                def D_norm(i):
                    layernorm(dve, vD, gD, i, "2", x_res[:, i, :], st6b, mvb, rstdb, xn2, waiter,
                              lambda: (pD.wait(dve, i - 1, "XT2"), need(dve, sent, 32 * i)))

                def D_choose(i):
                    pD.wait(dve, i, "G")
                    vD.done(dve.tensor_copy(lg[:], bank[0][:, 0:E]), "lg")
                    for n in range(2):
                        vD.wait(dve, i, "less" if n else "lg")
                        vD.done(dve.tensor_reduce(top[:, n:n + 1], lg[:], AX_X, ALU.max), f"top{n}")
                        vD.wait(dve, i, f"top{n}")
                        vD.done(dve.scalar_tensor_tensor(cand[:], lg[:], top[:, n:n + 1], rank8[:],
                                                         ALU.is_equal, ALU.mult), f"eq{n}")
                        vD.wait(dve, i, f"eq{n}")
                        vD.done(dve.tensor_reduce(best[:, n:n + 1], cand[:], AX_X, ALU.max), f"best{n}")
                        vD.wait(dve, i, f"best{n}")
                        vD.done(dve.tensor_scalar(oh[:, n, :], rank8[:], best[:, n:n + 1], None, ALU.is_equal), f"oh{n}")
                        vD.wait(dve, i, f"oh{n}")
                        if n == 0:
                            vD.done(dve.scalar_tensor_tensor(lg[:], oh[:, 0, :], -3e38, lg[:], ALU.mult, ALU.add), "less")
                    vD.done(dve.tensor_tensor(both[:], oh[:, 0, :], oh[:, 1, :], ALU.add), "both")
                    vD.done(dve.tensor_tensor(dl[:], top[:, 1:2], top[:, 0:1], ALU.subtract), "dl")

                def D_place(i):
                    aD.wait(dve, i, "ew")
                    vD.done(dve.tensor_scalar(ex[:, 1:2], ex[:, 0:1], 1.0, None, ALU.add), "e1")
                    vD.wait(dve, i, "e1")
                    vD.done(dve.reciprocal(gate_w[:, i, 0:1], ex[:, 1:2]), "w0")
                    vD.wait(dve, i, "w0")
                    vD.done(dve.tensor_tensor(gate_w[:, i, 1:2], ex[:, 0:1], gate_w[:, i, 0:1], ALU.mult), "w1")
                    pD.wait(dve, i, "R")
                    vD.done(dve.tensor_tensor(dest[:], bank[0][:, 2 * E:3 * E], count[:], ALU.add), "dest")
                    vD.wait(dve, i, "dest")
                    vD.done(dve.tensor_tensor(prod[:], oh[:], dest[:].unsqueeze(1).to_broadcast([P, 2, E]), ALU.mult), "prod")
                    vD.wait(dve, i, "prod")
                    vD.done(dve.tensor_reduce(posf[:], prod[:], AX_X, ALU.add), "pos")
                    vD.wait(dve, i, "pos")
                    need(dve, sent, 32 * i)
                    dve.tensor_copy(row_all[:, i, :], posf[:])
                    dve.tensor_copy(pick_all[:, i, :], oh[:].rearrange("p n e -> p (n e)"))
                    vD.done(dve.tensor_copy(idx[:], posf[:]), "idx")
                    vD.done(dve.tensor_tensor(count[:], bank[0][:, 3 * E:4 * E], count[:], ALU.add), "cnt")
                    vD.wait(dve, i, "cnt")

                A_norm(0)
                dve.wait_ge(w_got, 16 * n_w)
                dve.wait_ge(c_set, 8)
                A_q(0)
                A_k(0)
                A_norm(1)

                def body(i):
                    pB.wait(dve, i, "QT")
                    vB.done(split_q(dve, dve.tensor_copy, (2, 3)), "q")
                    if has(i, 1):
                        A_q(i + 1)
                    pB.wait(dve, i, "S")
                    group = "p (g k) -> p g k"
                    vB.done(dve.tensor_reduce(mx[:], bank[4][:].rearrange(group, k=Tlen), AX_X, ALU.max), "mx")
                    vB.wait(dve, i, "mx")
                    vB.wait(dve, i - 1, "prob")
                    vB.done(dve.tensor_tensor(Ex[:], bank[4][:].rearrange(group, k=Tlen),
                                              mx[:].unsqueeze(2).to_broadcast([P, NQ * BT, Tlen]), ALU.subtract), "sub")
                    if has(i, 2):
                        A_norm(i + 2)
                    aB.wait(dve, i, "exp")
                    vB.done(dve.tensor_reduce(sm[:], Ex[:], AX_X, ALU.add), "sum")
                    vB.wait(dve, i, "sum")
                    vB.done(dve.reciprocal(ri[:], sm[:]), "rec")
                    vB.wait(dve, i, "rec")
                    vB.done(dve.tensor_tensor(Pm[:].rearrange("p m (b k) -> p (m b) k", k=Tlen), Ex[:],
                                              ri[:].unsqueeze(2).to_broadcast([P, NQ * BT, Tlen]), ALU.mult), "prob")
                    if has(i, 1):
                        A_k(i + 1)
                    if not (isinstance(i, int) and i == 0):
                        D_choose(i - 1)
                    pC.wait(dve, i, "PT")
                    vC.done(split_p(dve, dve.tensor_copy, (2, 3)), "pt")
                    for m in range(NQ):
                        pC.wait(dve, i, f"PV{m}")
                        if m == 0:
                            pO.wait(dve, i - 1, "OP")
                        vC.done(merge_o(dve, dve.tensor_copy, m, (2, 3)), f"ov{m}")
                    if not (isinstance(i, int) and i == 0):
                        D_place(i - 1)
                    pO.wait(dve, i, "OP")
                    vC.done(dve.tensor_tensor(x_res[:, i, :], bank[1][:], x_res[:, i, :], ALU.add), "add")
                    vC.wait(dve, i, "add")
                    D_norm(i)
                tiles(dve, body)
                D_choose(n_tile - 1)
                D_place(n_tile - 1)

            @block.gpsimd
            def _(pool):
                pool.memset(Qd[:], 0.0).then_inc(c_set, 1)
                pool.memset(PTd[:], 0.0).then_inc(c_set, 1)
                pool.memset(ones[:], 1.0).then_inc(c_set, 1)
                pool.memset(mhalf[:], -0.5).then_inc(c_set, 1)
                pool.iota(rank8[:], pattern=[[-1, E]], base=E, channel_multiplier=0,
                          allow_small_or_imprecise_dtypes=True).then_inc(c_set, 1)
                pool.iota(start8[:], pattern=[[region, E]], base=0, channel_multiplier=0,
                          allow_small_or_imprecise_dtypes=True).then_inc(c_set, 1)
                pool.wait_ge(c_set, 6)
                pool.tensor_copy(count[:], start8[:]).then_inc(c_set, 1)
                pool.affine_select(out=below[:], in_=ones[:], compare_op=ALU.is_ge, fill=0.0, base=-1,
                                   pattern=[[1, P]], channel_multiplier=-1).then_inc(c_set, 1)
                pool.wait_ge(c_set, 8)

                def power(steps_in, steps_out, i, suffix, mv_, rstd_):
                    steps_in.wait(pool, i, "eps" + suffix)
                    steps_in.wait(pool, i - 1, "xn" + suffix)
                    steps_out.done(pool.tensor_tensor(rstd_[:], mv_[:, 1:2], mhalf[:], ALU.pow), "rstd" + suffix)

                def add_up(i, name, out, t1, t2):
                    vA.wait(pool, i, name[0])
                    pB.wait(pool, i - 1, "QT" if name == "qr" else "KT")
                    gA.done(pool.tensor_tensor(out[:], t1[:], t2[:], ALU.add), name)

                def send(i):
                    vD.wait(pool, i, "idx")
                    pool.tensor_tensor(carrier[:], mhalf[:], mhalf[:], ALU.add)
                    for n in range(2):
                        pool.indirect_dma_start(xs_dram, bass.IndirectOffsetOnAxis(ap=idx[:, n:n + 1], axis=0),
                                                xn2[:], None).then_inc(sent, 16)

                power(vL, gL, 0, "", mv, rstd)
                add_up(0, "qr", qr, tq1, tq2)
                add_up(0, "kr", kr, tk1, tk2)
                power(vL, gL, 1, "", mv, rstd)

                def body(i):
                    if has(i, 1):
                        add_up(i + 1, "qr", qr, tq1, tq2)
                    if has(i, 2):
                        power(vL, gL, i + 2, "", mv, rstd)
                    if has(i, 1):
                        add_up(i + 1, "kr", kr, tk1, tk2)
                    if not (isinstance(i, int) and i == 0):
                        send(i - 1)
                    power(vD, gD, i, "2", mvb, rstdb)
                tiles(pool, body)
                send(n_tile - 1)
                pool.wait_ge(sent, 32 * n_tile)


def tile_table(nc, xs_dram, count, row_all, pick_all, table, pos_all, E, n_work, rows, region, most):
    with ExitStack() as ctx:
        def sb(name, shape, dt=F32):
            return ctx.enter_context(nc.sbuf_tensor(name, shape, dt))
        n_step = most // rows
        n_pick = pick_all.shape[1] * 2
        zeros = sb("zeros", [P, rows // P, xs_dram.shape[1]])
        start = sb("t_start", [P, E])
        level = sb("t_level", [P, n_step])
        upto = sb("t_upto", [P, E, E])
        ks = sb("t_ks", [P, n_work])
        n_row, n_t, incl, shift = (sb(n, [P, E]) for n in ("t_nrow", "t_nt", "t_incl", "t_shift"))
        cmp, trip = sb("t_cmp", [P, E, n_step]), sb("t_trip", [P, E, E])
        past, pastv = sb("t_past", [P, n_work, E]), sb("t_pastv", [P, n_work, E])
        ek, first, used, d1, d2, d3 = (sb(n, [P, n_work]) for n in ("t_ek", "t_first", "t_used", "t_d1", "t_d2", "t_d3"))
        moved, move = sb("t_moved", [P, n_pick, E]), sb("t_move", [P, n_pick])
        end_row = sb("t_end", [1, E], I32)
        cs = ctx.enter_context(nc.semaphore("t_const"))
        v = ctx.enter_context(nc.semaphore("t_vector"))
        z = ctx.enter_context(nc.semaphore("t_zeroed"))
        imprecise = dict(allow_small_or_imprecise_dtypes=True)

        with nc.Block() as block:
            @block.gpsimd
            def _(pool):
                pool.iota(start[:], pattern=[[region, E]], base=0, channel_multiplier=0, **imprecise).then_inc(cs, 1)
                pool.iota(level[:], pattern=[[rows, n_step]], base=0, channel_multiplier=0, **imprecise).then_inc(cs, 1)
                pool.iota(ks[:], pattern=[[1, n_work]], base=0, channel_multiplier=0, **imprecise).then_inc(cs, 1)
                pool.memset(upto[:], 1.0).then_inc(cs, 1)
                pool.wait_ge(cs, 4)
                pool.affine_select(out=upto[:], in_=upto[:], compare_op=ALU.is_ge, fill=0.0, base=0,
                                   pattern=[[1, E], [-1, E]], channel_multiplier=0).then_inc(cs, 1)
                pool.memset(zeros[:], 0.0).then_inc(cs, 1)

            @block.vector
            def _(dve):
                n = [0]

                def chain(op):
                    n[0] += 1
                    op.then_inc(v, 1)
                    dve.wait_ge(v, n[0])

                def each_e(t, m):
                    return t[:].unsqueeze(1).to_broadcast([P, m, E])

                chain(dve.tensor_copy(end_row[:], count[0:1, :]))
                dve.wait_ge(cs, 5)
                chain(dve.tensor_tensor(n_row[:], count[:], start[:], ALU.subtract))
                chain(dve.tensor_tensor(cmp[:], n_row[:].unsqueeze(2).to_broadcast([P, E, n_step]),
                                        level[:].unsqueeze(1).to_broadcast([P, E, n_step]), ALU.is_gt))
                chain(dve.tensor_reduce(n_t[:], cmp[:], AX_X, ALU.add))
                chain(dve.tensor_tensor(trip[:], each_e(n_t, E), upto[:], ALU.mult))
                chain(dve.tensor_reduce(incl[:], trip[:], AX_X, ALU.add))
                chain(dve.tensor_tensor(past[:], each_e(incl, n_work),
                                        ks[:].unsqueeze(2).to_broadcast([P, n_work, E]), ALU.is_le))
                chain(dve.tensor_reduce(ek[:], past[:], AX_X, ALU.add))
                chain(dve.tensor_tensor(pastv[:], past[:], each_e(incl, n_work), ALU.mult))
                chain(dve.tensor_reduce(first[:], pastv[:], AX_X, ALU.max))
                chain(dve.tensor_scalar(used[:], ek[:], float(E), None, ALU.is_lt))
                chain(dve.tensor_tensor(d1[:], ks[:], first[:], ALU.subtract))
                chain(dve.tensor_tensor(d2[:], d1[:], used[:], ALU.mult))
                chain(dve.tensor_scalar(d1[:], d2[:], float(rows), None, ALU.mult))
                chain(dve.scalar_tensor_tensor(d3[:], ek[:], float(region), d1[:], ALU.mult, ALU.add))
                chain(dve.tensor_copy(table[:, 1, :], d3[0:1, :]))
                chain(dve.tensor_scalar(d1[:], ek[:], float(E - 1), None, ALU.min))
                chain(dve.tensor_copy(table[:, 0, :], d1[0:1, :]))
                chain(dve.tensor_tensor(shift[:], incl[:], n_t[:], ALU.subtract))
                chain(dve.tensor_scalar(shift[:], shift[:], float(rows), None, ALU.mult))
                chain(dve.tensor_tensor(shift[:], shift[:], start[:], ALU.subtract))
                chain(dve.tensor_tensor(moved[:], pick_all[:].rearrange("p i (n e) -> p (i n) e", e=E),
                                        each_e(shift, n_pick), ALU.mult))
                chain(dve.tensor_reduce(move[:], moved[:], AX_X, ALU.add))
                chain(dve.tensor_tensor(pos_all[:].rearrange("p i n -> p (i n)"),
                                        row_all[:].rearrange("p i n -> p (i n)"), move[:], ALU.add))

            @block.sync
            def _(sp):
                sp.wait_ge(cs, 6)
                sp.dma_start(xs_dram[E * region:E * region + rows, :]
                             .rearrange("(c p) w -> p c w", p=P), zeros[:]).then_inc(z, 16)
                sp.wait_ge(v, 1)
                for e in range(E):
                    at = sp.value_load(end_row[0:1, e:e + 1], min_val=e * region, max_val=e * region + most)
                    sp.dma_start(xs_dram[bass.ds(at, rows), :].rearrange("(c p) w -> p c w", p=P), zeros[:]).then_inc(z, 16)
                sp.wait_ge(z, 16 * (E + 1))


def experts(nc, W1, W3, W2, xs_dram, ys_dram, table, n_work, rows, ident):
    E, C, H = W1.shape
    KC, NH = C // P, H // P
    PAIR = 2
    NS = NH // PAIR
    CH = rows // P
    W = PAIR * P
    n_rows = xs_dram.shape[0]

    with ExitStack() as ctx:
        def sb(name, shape, dt=F32):
            return ctx.enter_context(nc.sbuf_tensor(name, shape, dt))

        def steps(name, names):
            return Steps(ctx.enter_context(nc.semaphore(name)), names)

        raw13, raw2 = sb("raw13", [P, NS, 2, KC, W]), sb("raw2", [P, NS, PAIR, C])
        hi13, lo13 = sb("hi13", [P, NS, 2, KC, W], F32R), sb("lo13", [P, NS, 2, KC, W], F32R)
        hi2, lo2 = sb("hi2", [P, NS, PAIR, C], F32R), sb("lo2", [P, NS, PAIR, C], F32R)
        xg = sb("xg", [P, CH, C])
        xT_hi, xT_lo = sb("xT_hi", [P, KC, rows], F32R), sb("xT_lo", [P, KC, rows], F32R)
        sl, af = sb("sl", [P, 2, rows]), sb("af", [P, 2, rows])
        a_hi, a_lo = sb("a_hi", [P, 2, rows], F32R), sb("a_lo", [P, 2, rows], F32R)
        ysb = sb("ysb", [P, CH, C])
        bank = [ctx.enter_context(nc.psum_tensor(f"mo_bank{i}", [P, 512], F32)) for i in range(6)]
        bank_hg, bank_y, bank_x = bank[0:2], bank[2:4], bank[4:6]

        raw_got = [ctx.enter_context(nc.semaphore(f"raw_got{c}")) for c in range(NS)]
        x_got = ctx.enter_context(nc.semaphore("x_got"))
        y_put = ctx.enter_context(nc.semaphore("y_put"))
        pM = steps("pM", "HG0 HG1 Y0 HG2 Y1 HG3 Y2 HG4 Y3 HG5 Y4 Y5")
        pX = steps("pX", "XT")
        pieces = [(c, q) for c in range(NS) for q in range(3)]
        aM, aX = steps("aM", "s0 s1 s2 s3 s4 s5 y"), steps("aX", "x0 x1")
        aW, vW = (steps(n, " ".join(f"p{c}{q}" for c, q in pieces)) for n in ("aW", "vW"))
        vM, vX = steps("vM", " ".join(f"m{j} h{j} a{j}" for j in range(NH)) + " y"), steps("vX", "x0 x1")
        when = {0: [(0, 2, 0)], 1: [(0, 2, 1), (0, 2, 2)], 2: [(1, 0, 0), (1, 0, 1)], 3: [(1, 0, 2)],
                4: [(1, 1, 0), (1, 1, 1)], 6: [(1, 1, 2)]}

        def part(c, q):
            if q == 2:
                return [t[:, c].rearrange("p b w -> p (b w)") for t in (raw2, hi2, lo2)]
            return [t[:, c, q].rearrange("p k w -> p (k w)") for t in (raw13, hi13, lo13)]

        with nc.Block() as block:
            @block.sync
            def _(sp):
                def load(k):
                    e = sp.value_load(table[0:1, 0, bass.ds(k, 1)], min_val=0, max_val=E - 1)
                    row = sp.value_load(table[0:1, 1, bass.ds(k, 1)], min_val=0, max_val=n_rows - rows)
                    pX.wait(sp, k - 1, "XT")
                    sp.dma_start(xg[:], xs_dram[bass.ds(row, rows), :].rearrange("(c p) w -> p c w", p=P)).then_inc(x_got, 16)
                    for c in range(NS):
                        vW.wait(sp, k - 1, f"p{c}2")
                        for a, src in enumerate((W1, W3)):
                            sp.dma_start(raw13[:, c, a], src[bass.ds(e, 1), :, c * W:(c + 1) * W]
                                         .rearrange("e (k p) h -> p (e k) h", p=P)).then_inc(raw_got[c], 16)
                        sp.dma_start(raw2[:, c], W2[bass.ds(e, 1), c * W:(c + 1) * W, :]
                                     .rearrange("e (b p) w -> p (e b) w", p=P)).then_inc(raw_got[c], 16)

                def store(k):
                    aM.wait(sp, k, "y")
                    vM.wait(sp, k, "y")
                    sp.dma_start(ys_dram[bass.ds(k * rows, rows), :].rearrange("(c p) w -> p c w", p=P), ysb[:]).then_inc(y_put, 16)

                def body(k, first, last):
                    load(k)
                    if not first:
                        store(k - 1)
                peeled(sp, n_work, body)
                store(n_work - 1)
                sp.wait_ge(y_put, 16 * n_work)

            @block.tensor
            def _(pe):
                def turn(k):
                    pe.wait_ge(x_got, 16 * k + 16)
                    aX.wait(pe, k - 1, "x1")
                    vX.wait(pe, k - 1, "x1")
                    for c in range(CH):
                        for q in range(KC):
                            mm = pe.transpose(bank_x[c][:, q * P:(q + 1) * P], xg[:, c, q * P:(q + 1) * P], ident[:])
                    pX.done(mm, "XT")

                def hg(k, j):
                    c, o = j // PAIR, (j % PAIR) * P
                    if j == 0:
                        aX.wait(pe, k, "x1")
                        vX.wait(pe, k, "x1")
                    vW.wait(pe, k, f"p{c}1")
                    if j > 1:
                        vM.wait(pe, k, f"m{j - 2}")
                    else:
                        vM.wait(pe, k - 1, f"m{NH - 2 + j}")
                    for a in range(2):
                        for q in range(KC):
                            mm = product(pe, bank_hg[j % 2][:, a * rows:(a + 1) * rows],
                                         (hi13[:, c, a, q, o:o + P], lo13[:, c, a, q, o:o + P]),
                                         (xT_hi[:, q, :], xT_lo[:, q, :]), q == 0, q == KC - 1)
                    pM.done(mm, f"HG{j}")

                def down(k, j):
                    if j == 0:
                        aM.wait(pe, k - 1, "y")
                        vM.wait(pe, k - 1, "y")
                    c, b = j // PAIR, j % PAIR
                    vW.wait(pe, k, f"p{c}2")
                    vM.wait(pe, k, f"a{j}")
                    for r in range(CH):
                        mm = product(pe, bank_y[r][:], (a_hi[:, j % 2, r * P:(r + 1) * P], a_lo[:, j % 2, r * P:(r + 1) * P]),
                                     (hi2[:, c, b, :], lo2[:, c, b, :]), j == 0, j == NH - 1)
                    pM.done(mm, f"Y{j}")

                turn(0)

                def body(k, first, last):
                    for j in range(NH):
                        if j == NH - 1 and not last:
                            turn(k + 1)
                        hg(k, j)
                        if j:
                            down(k, j - 1)
                    down(k, NH - 1)
                peeled(pe, n_work, body)

            def slot_free(eng, k, c):
                pM.wait(eng, k - 1, f"Y{PAIR * c + PAIR - 1}")

            @block.scalar
            def _(act):
                def split(k, c, q):
                    raw, hi, _lo = part(c, q)
                    act.wait_ge(raw_got[c], 48 * k + 48)
                    slot_free(act, k, c)
                    aW.done(act.copy(hi, raw), f"p{c}{q}")

                def x_hi(k):
                    if not (isinstance(k, int) and k == 0):
                        pM.wait(act, k - 1, f"HG{NH - 1}")
                    pX.wait(act, k, "XT")
                    for c in range(CH):
                        aX.done(act.copy(xT_hi[:, :, c * P:(c + 1) * P],
                                         bank_x[c][:].rearrange("p (k q) -> p k q", q=P)), f"x{c}")

                x_hi(0)
                for c in range(NS - 1):
                    for q in range(3):
                        split(0, c, q)

                def body(k, first, last):
                    for j in range(NH):
                        pM.wait(act, k, f"HG{j}")
                        if j > 1:
                            vM.wait(act, k, f"m{j - 2}")
                        else:
                            vM.wait(act, k - 1, f"m{NH - 2 + j}")
                        aM.done(act.activation(sl[:, j % 2, :], bank_hg[j % 2][:, 0:rows], ACT.Silu), f"s{j}")
                        if j == NH - 1 and not last:
                            x_hi(k + 1)
                        for ahead, c, q in when.get(j, ()):
                            if not (ahead and last):
                                split(k + ahead, c, q)
                    pM.wait(act, k, f"Y{NH - 1}")
                    need(act, y_put, 16 * k)
                    aM.done(act.copy(ysb[:, 0, :], bank_y[0][:]), "y")
                    if not last:
                        for ahead, c, q in when[NH]:
                            split(k + ahead, c, q)
                peeled(act, n_work, body)

            @block.vector
            def _(dve):
                def split(k, c, q):
                    raw, hi, lo = part(c, q)
                    aW.wait(dve, k, f"p{c}{q}")
                    vW.done(dve.tensor_tensor(lo, raw, hi.bitcast(F32), ALU.subtract), f"p{c}{q}")

                def x_lo(k):
                    for c in range(CH):
                        aX.wait(dve, k, f"x{c}")
                        vX.done(dve.tensor_tensor(xT_lo[:, :, c * P:(c + 1) * P],
                                                  bank_x[c][:].rearrange("p (k q) -> p k q", q=P),
                                                  xT_hi[:, :, c * P:(c + 1) * P].bitcast(F32), ALU.subtract), f"x{c}")

                x_lo(0)
                for c in range(NS - 1):
                    for q in range(3):
                        split(0, c, q)

                def body(k, first, last):
                    for j in range(NH):
                        u = j % 2
                        aM.wait(dve, k, f"s{j}")
                        vM.done(dve.tensor_tensor(af[:, u, :], bank_hg[u][:, rows:2 * rows], sl[:, u, :], ALU.mult), f"m{j}")
                        if j > 1:
                            pM.wait(dve, k, f"Y{j - 2}")
                        else:
                            pM.wait(dve, k - 1, f"Y{NH - 2 + j}")
                        vM.wait(dve, k, f"m{j}")
                        vM.done(dve.tensor_copy(a_hi[:, u, :], af[:, u, :]), f"h{j}")
                        vM.wait(dve, k, f"h{j}")
                        vM.done(dve.tensor_tensor(a_lo[:, u, :], af[:, u, :], a_hi[:, u, :].bitcast(F32), ALU.subtract), f"a{j}")
                        if j == NH - 1 and not last:
                            x_lo(k + 1)
                        for ahead, c, q in when.get(j, ()):
                            if not (ahead and last):
                                split(k + ahead, c, q)
                    pM.wait(dve, k, f"Y{NH - 1}")
                    need(dve, y_put, 16 * k)
                    vM.done(dve.tensor_copy(ysb[:, 1, :], bank_y[1][:]), "y")
                    if not last:
                        for ahead, c, q in when[NH]:
                            split(k + ahead, c, q)
                peeled(dve, n_work, body)


def combine(nc, x_res, ys_dram, gate_w, pos_all, out):
    n_tile, C = x_res.shape[1], x_res.shape[2]
    U = 4
    with ExitStack() as ctx:
        def sb(name, shape, dt=F32):
            return ctx.enter_context(nc.sbuf_tensor(name, shape, dt))

        idx = sb("c_idx", [P, U, 2], U32)
        ya, yb, ob = sb("c_ya", [P, U, C]), sb("c_yb", [P, U, C]), sb("c_ob", [P, U, C])
        one, carrier = sb("c_one", [P, 1]), sb("c_carrier", [P, 1])
        c_set = ctx.enter_context(nc.semaphore("c_one_set"))
        carried = ctx.enter_context(nc.semaphore("c_carried"))
        v_idx = ctx.enter_context(nc.semaphore("c_v_idx"))
        vS = Steps(ctx.enter_context(nc.semaphore("c_vS")), " ".join(f"a{u} b{u}" for u in range(U)))
        got = [ctx.enter_context(nc.semaphore(f"c_got{u}")) for u in range(U)]
        put = [ctx.enter_context(nc.semaphore(f"c_put{u}")) for u in range(U)]
        n_round = n_tile // U
        out_t = out.rearrange("(g u p) c -> g u p c", u=U, p=P)

        with nc.Block() as block:
            @block.gpsimd
            def _(pool):
                pool.memset(one[:], 1.0).then_inc(c_set, 1)
                pool.wait_ge(c_set, 1)

                def body(g, first, last):
                    for u in range(U):
                        pool.wait_ge(v_idx, U * g + u + 1)
                        vS.wait(pool, g - 1, f"b{u}")
                        need(pool, carried, U * g + u)
                        pool.tensor_tensor(carrier[:], one[:], one[:], ALU.add).then_inc(carried, 1)
                        for n, y in ((0, ya), (1, yb)):
                            pool.indirect_dma_start(y[:, u, :], None, ys_dram,
                                                    bass.IndirectOffsetOnAxis(ap=idx[:, u, n:n + 1], axis=0)
                                                    ).then_inc(got[u], 16)
                peeled(pool, n_round, body)

            @block.vector
            def _(dve):
                def body(g, first, last):
                    for u in range(U):
                        need(dve, got[u], 32 * g)
                        i = U * g + u
                        dve.tensor_copy(idx[:, u, :], pos_all[:, i, :]).then_inc(v_idx, 1)
                    for u in range(U):
                        i = U * g + u
                        dve.wait_ge(got[u], 32 * g + 32)
                        need(dve, put[u], 16 * g)
                        vS.done(dve.scalar_tensor_tensor(ob[:, u, :], ya[:, u, :], gate_w[:, i, 0:1], x_res[:, i, :],
                                                         ALU.mult, ALU.add), f"a{u}")
                        vS.wait(dve, g, f"a{u}")
                        vS.done(dve.scalar_tensor_tensor(ob[:, u, :], yb[:, u, :], gate_w[:, i, 1:2], ob[:, u, :],
                                                         ALU.mult, ALU.add), f"b{u}")
                peeled(dve, n_round, body)

            @block.sync
            def _(sp):
                def body(g, first, last):
                    for u in range(U):
                        vS.wait(sp, g, f"b{u}")
                        i = U * g + u
                        sp.dma_start(out[bass.ds(i * P, P), :], ob[:, u, :]).then_inc(put[u], 16)
                peeled(sp, n_round, body)
                for u in range(U):
                    sp.wait_ge(put[u], 16 * n_round)


def perceiver_block(nc, x, ctx_512, xWq, xWkv, xWo, wq, w_down, wk_up, wv_up, wo, Wr, W1, W2, W3, rope, out):
    B, T, C = x.shape
    E = Wr.shape[1]
    n_tok = B * T
    n_tile = n_tok // P
    rows = 2 * P
    region = n_tok + rows
    n_work = (2 * n_tok - E) // rows + E
    xs = nc.dram_tensor("xs", (E * region + rows, C), F32).ap()
    ys = nc.dram_tensor("ys", (n_work * rows, C), F32).ap()
    v_last = nc.dram_tensor("v_last_rows", (B, C), F32).ap()

    with ExitStack() as ctx:
        def sb(name, shape, dt=F32):
            return ctx.enter_context(nc.sbuf_tensor(name, shape, dt))
        x_res = sb("x_res", [P, n_tile, C])
        gate_w = sb("gate_w", [P, n_tile, 2])
        pos_all = sb("pos_all", [P, n_tile, 2], U32)
        row_all = sb("row_all", [P, n_tile, 2])
        pick_all = sb("pick_all", [P, n_tile, 2 * E])
        count = sb("count", [P, E])
        table = sb("table", [1, 2, n_work], I32)
        ident, quad_mask = block_constants(nc, ctx)
        cross_attention(nc, ctx, x.rearrange("b t c -> (b t) c"), ctx_512, xWq, xWkv, xWo, x_res, ident, quad_mask, v_last)
        self_attention_and_routing(nc, wq, w_down, wk_up, wv_up, wo, Wr, rope, x_res, ident, xs,
                                   gate_w, row_all, pick_all, count, region, T)
        tile_table(nc, xs, count, row_all, pick_all, table, pos_all, E, n_work, rows, region, n_tok)
        experts(nc, W1, W3, W2, xs, ys, table, n_work, rows, ident)
        combine(nc, x_res, ys, gate_w, pos_all, out.rearrange("b t c -> (b t) c"))


_INS = ['x', 'ctx_512', 'L0_xattn_Wq', 'L0_xattn_Wkv', 'L0_xattn_Wo', 'L0_attn_wq', 'L0_attn_w_down', 'L0_attn_wk_up',
        'L0_attn_wv_up', 'L0_attn_wo', 'L0_ffn_Wr', 'L0_ffn_W1', 'L0_ffn_W2', 'L0_ffn_W3']


def kernel(**inputs):
    import numpy as _np
    import concourse.bacc as _bacc
    from concourse import mybir as _mybir
    from concourse.bass_utils import run_bass_kernel_spmd as _run

    nc = _bacc.Bacc("TRN2", target_bir_lowering=False, num_devices=1)
    arrays, args = {}, []
    for name in _INS:
        a = _np.ascontiguousarray(inputs[name])
        arrays[f"in_{name}_dram"] = a
        args.append(nc.dram_tensor(f"in_{name}_dram", a.shape, _mybir.dt.from_np(a.dtype), kind="ExternalInput").ap())
    B, T, C = inputs['x'].shape
    args.append(nc.inline_tensor(rope_tables(T, 32), name="rope_tables").ap())
    out = nc.dram_tensor("out_0_dram", (B, T, C), _mybir.dt.float32, kind="ExternalOutput").ap()
    perceiver_block(nc, *args, out)
    r = _run(nc, [arrays], core_ids=[0])
    return r.results[0]["out_0_dram"]
```

```python
from contextlib import ExitStack

import numpy as np

import concourse.bass as bass
from concourse import mybir
from concourse.alu_op_type import AluOpType as ALU

F32 = mybir.dt.float32
F32R = mybir.dt.float32r
I32 = mybir.dt.int32
U32 = mybir.dt.uint32
ACT = mybir.ActivationFunctionType
AX_X = mybir.AxisListType.X

P = 128
EPS = 1e-5
ROPE_THETA = 10000.0
LO_ROW = 32
LAST_ROWS = LO_ROW + 4


def need(eng, sem, value):
    if isinstance(value, int) and value <= 0:
        return
    eng.wait_ge(sem, value)


def peeled(eng, n, body):
    body(0, True, n == 1)
    if n > 2:
        with eng.Fori(1, n - 1) as i:
            body(i, False, False)
    if n > 1:
        body(n - 1, False, True)


def product(pe, out, lhs, rhs, start, stop):
    (lh, ll), (rh, rl) = lhs, rhs
    pe.matmul(out, lh, rh, start=start, stop=False)
    pe.matmul(out, ll, rh, start=False, stop=False)
    return pe.matmul(out, lh, rl, start=False, stop=stop)


def rope_tables(T, D):
    inv = 1.0 / ROPE_THETA ** (np.arange(0, D, 2, dtype=np.float32) / D)
    ang = np.outer(np.arange(T, dtype=np.float32), inv)
    cos = np.repeat(np.cos(ang), 2, axis=1)
    sin = np.stack([-np.sin(ang), np.sin(ang)], axis=2).reshape(T, D)
    return np.ascontiguousarray(np.tile(np.concatenate([cos, sin], axis=1), (P // T, 1)).astype(np.float32))


def block_constants(nc, ctx):
    ident = ctx.enter_context(nc.sbuf_tensor("ident", [P, P], F32))
    quad_mask = ctx.enter_context(nc.sbuf_tensor("quad_mask", [LAST_ROWS, 4, P], F32))
    s = ctx.enter_context(nc.semaphore("const_ready"))

    with nc.Block() as block:
        @block.gpsimd
        def _(pool):
            pool.memset(ident[:], 0.0).then_inc(s, 1)
            pool.memset(quad_mask[:], 0.0).then_inc(s, 1)
            pool.wait_ge(s, 2)
            pool.affine_select(out=ident[:], in_=ident[:], compare_op=ALU.not_equal, fill=1.0, base=0,
                               pattern=[[-1, P]], channel_multiplier=1).then_inc(s, 1)
            for n, row in enumerate((0, 4, LO_ROW)):
                pool.wait_ge(s, 3 + n)
                pool.affine_select(out=quad_mask[:], in_=quad_mask[:], compare_op=ALU.not_equal, fill=1.0, base=-row,
                                   pattern=[[-1, 4], [0, P]], channel_multiplier=1).then_inc(s, 1)
            pool.wait_ge(s, 6)
    return ident, quad_mask


def cross_attention(nc, ctx0, x_in, ctx_in, Wq, Wkv, Wo, x_res, ident, quad_mask, vlast_dram, ahead):
    n_tile = x_res.shape[1]
    C = x_res.shape[2]
    B, NK, L = ctx_in.shape
    KC = C // P
    KL = L // P
    NQ = C // P
    HD = 32
    BT = P // HD
    CH = 2
    LAST = CH * P
    assert NK == LAST + 1
    KW = LAST + 2
    SCALE = HD ** -0.5

    with ExitStack() as ctx:
        def sb(name, shape, dt=F32):
            return ctx.enter_context(nc.sbuf_tensor(name, shape, dt))

        def sem(name):
            return ctx.enter_context(nc.semaphore(name))

        WqT = sb("WqT", [P, KC, C])
        WoT_hi, WoT_lo = sb("WoT_hi", [P, KC, C], F32R), sb("WoT_lo", [P, KC, C], F32R)
        Wkv_hi, Wkv_lo = sb("Wkv_hi", [P, KL, 2 * C], F32R), sb("Wkv_lo", [P, KL, 2 * C], F32R)
        zl_hi, zl_lo = sb("zl_hi", [P, KL, B], F32R), sb("zl_lo", [P, KL, B], F32R)
        Kl_hi, Kl_lo = sb("Kl_hi", [P, NQ, B], F32R), sb("Kl_lo", [P, NQ, B], F32R)
        Q_hi, Q_lo = sb("Q_hi", [P, NQ, BT, P], F32R), sb("Q_lo", [P, NQ, BT, P], F32R)
        K_hi, K_lo = sb("K_hi", [P, NQ, KW], F32R), sb("K_lo", [P, NQ, KW], F32R)
        v_last_in = sb("v_last_in", [LAST_ROWS, BT, P])
        xn = sb("xn", [P, C])
        st6 = sb("st6", [P, 6])
        mv = sb("mv", [P, 2])
        rstd = sb("rstd", [P, 1])
        mhalf = sb("mhalf", [P, 1])
        waiter = sb("waiter", [P, 1])
        LN = 4
        v_ln, g_ln, mh = sem("v_ln"), sem("g_ln"), sem("mhalf_set")
        x_first, x_rest = sem("x_first"), sem("x_rest")
        pe_X = sem("pe_X")

        def statistics(dve, i):
            dve.bn_stats(st6[:], x_res[:, i, :]).then_inc(v_ln, 1)
            dve.wait_ge(v_ln, LN * i + 1)
            dve.memset(waiter[:], 0.0)
            dve.bn_aggr(mv[:], st6[:]).then_inc(v_ln, 1)
            dve.wait_ge(v_ln, LN * i + 2)
            dve.tensor_scalar(mv[:, 1:2], mv[:, 1:2], EPS, None, ALU.add).then_inc(v_ln, 1)

        def normalise(dve, i):
            need(dve, pe_X, i)
            dve.wait_ge(g_ln, i + 1)
            dve.tensor_scalar(xn[:], x_res[:, i, :], mv[:, 0:1], rstd[:], ALU.subtract, ALU.mult
                              ).then_inc(v_ln, 1)

        def rstd_of(pool, i):
            pool.wait_ge(v_ln, LN * i + 3)
            need(pool, v_ln, LN * i)
            pool.tensor_tensor(rstd[:], mv[:, 1:2], mhalf[:], ALU.pow).then_inc(g_ln, 1)

        psum = [ctx.enter_context(nc.psum_tensor(f"xa_bank{i}", [P, 512], F32)) for i in range(8)]

        with ExitStack() as setup:
            def sbs(name, shape, dt=F32):
                return setup.enter_context(nc.sbuf_tensor(name, shape, dt))
            raw_q = sbs("raw_q", [P, KC, C])
            raw_kv = sbs("raw_kv", [P, 2 * C // P, L])
            raw_o = sbs("raw_o", [P, KC, C])
            raw_zl = sbs("raw_zl", [B, L])
            vl_hi, vl_lo = sbs("vl_hi", [B, C], F32R), sbs("vl_lo", [B, C], F32R)
            loaded = [setup.enter_context(nc.semaphore(f"w_loaded{i}")) for i in range(4)]
            turned = setup.enter_context(nc.semaphore("w_turned"))
            hi_done = setup.enter_context(nc.semaphore("w_hi"))
            lo_done = setup.enter_context(nc.semaphore("w_lo"))
            zeroed = setup.enter_context(nc.semaphore("w_zeroed"))
            jobs = []
            jobs.append((3, [raw_zl[:, k * P:(k + 1) * P] for k in range(KL)],
                         (zl_hi[:, :, :].rearrange("p k b -> p (k b)"), zl_lo[:, :, :].rearrange("p k b -> p (k b)")), B))
            for k in range(KL):
                for h in range(2):
                    jobs.append((1, [raw_kv[:, 4 * h + o, k * P:(k + 1) * P] for o in range(4)],
                                 (Wkv_hi[:, k, h * C:(h + 1) * C], Wkv_lo[:, k, h * C:(h + 1) * C]), P))
            for k in range(KC):
                jobs.append((2, [raw_o[:, o, k * P:(k + 1) * P] for o in range(KC)], (WoT_hi[:, k, :], WoT_lo[:, k, :]), P))
            for k in range(KC):
                jobs.append((0, [raw_q[:, o, k * P:(k + 1) * P] for o in range(KC)], (WqT[:, k, :], None), P))
            n_split = sum(1 for j in jobs if j[2][1] is not None)

            with nc.Block() as block:
                @block.sync
                def _(sp):
                    sp.dma_start(raw_zl[:], ctx_in[:, LAST, :]).then_inc(loaded[3], 16)
                    sp.dma_start(raw_kv[:], Wkv.rearrange("(o p) c -> p o c", p=P)).then_inc(loaded[1], 16)
                    xt = x_in.rearrange("(i p) c -> p i c", p=P)
                    sp.dma_start(x_res[:, 0, :], xt[:, 0, :]).then_inc(x_first, 16)
                    sp.dma_start(raw_o[:], Wo.rearrange("(o p) c -> p o c", p=P)).then_inc(loaded[2], 16)
                    sp.dma_start(raw_q[:], Wq.rearrange("(o p) c -> p o c", p=P)).then_inc(loaded[0], 16)
                    sp.dma_start(x_res[:, 1:, :], xt[:, 1:, :]).then_inc(x_rest, 16)
                    sp.wait_ge(hi_done, len(jobs) + 2)
                    sp.wait_ge(lo_done, n_split + 2)
                    sp.dma_start(vlast_dram[:, 0, :], vl_hi[:].bitcast(F32)).then_inc(loaded[3], 16)
                    sp.dma_start(vlast_dram[:, 1, :], vl_lo[:].bitcast(F32)).then_inc(loaded[3], 16)
                    sp.wait_ge(loaded[3], 48)

                @block.gpsimd
                def _(pool):
                    pool.memset(mhalf[:], -0.5).then_inc(mh, 1)
                    pool.wait_ge(mh, 1)
                    rstd_of(pool, 0)
                    pool.memset(Q_hi[:].bitcast(F32), 0.0)
                    pool.memset(Q_lo[:].bitcast(F32), 0.0)
                    pool.memset(K_hi[:].bitcast(F32), 0.0)
                    pool.memset(K_lo[:].bitcast(F32), 0.0)
                    pool.memset(v_last_in[:], 0.0).then_inc(zeroed, 1)
                    pool.wait_ge(zeroed, 1)

                @block.tensor
                def _(pe):
                    for n, (load, blocks, _dst, width) in enumerate(jobs):
                        pe.wait_ge(loaded[load], 16)
                        if n >= 6:
                            pe.wait_ge(hi_done, n - 5)
                            if n - 6 < n_split:
                                pe.wait_ge(lo_done, n - 5)
                        for o, src in enumerate(blocks):
                            mm = pe.transpose(psum[n % 6][:, o * width:(o + 1) * width], src,
                                              ident[0:src.shape[0], 0:src.shape[0]])
                        mm.then_inc(turned, 1)
                    pe.wait_ge(lo_done, n_split)
                    for m in range(NQ):
                        for k in range(KL):
                            mm = product(pe, psum[6][:, m * B:(m + 1) * B],
                                         (Wkv_hi[:, k, m * P:(m + 1) * P], Wkv_lo[:, k, m * P:(m + 1) * P]),
                                         (zl_hi[:, k, :], zl_lo[:, k, :]), k == 0, k == KL - 1)
                    mm.then_inc(turned, 1)
                    for k in range(KL):
                        mm = product(pe, psum[7][0:B, :], (zl_hi[:, k, :], zl_lo[:, k, :]),
                                     (Wkv_hi[:, k, C:2 * C], Wkv_lo[:, k, C:2 * C]), k == 0, k == KL - 1)
                    mm.then_inc(turned, 1)

                @block.scalar
                def _(act):
                    for n, (_load, blocks, (hi, _lo), width) in enumerate(jobs):
                        act.wait_ge(turned, n + 1)
                        act.copy(hi, psum[n % 6][:, 0:len(blocks) * width]).then_inc(hi_done, 1)
                    act.wait_ge(turned, len(jobs) + 1)
                    act.copy(Kl_hi[:].rearrange("p m b -> p (m b)"), psum[6][:, 0:NQ * B]).then_inc(hi_done, 1)
                    act.wait_ge(turned, len(jobs) + 2)
                    act.copy(vl_hi[:], psum[7][0:B, :]).then_inc(hi_done, 1)

                @block.vector
                def _(dve):
                    dve.wait_ge(x_first, 16)
                    statistics(dve, 0)
                    normalise(dve, 0)
                    for n, (_load, blocks, (hi, lo), width) in enumerate(jobs[:n_split]):
                        dve.wait_ge(hi_done, n + 1)
                        dve.tensor_tensor(lo, psum[n % 6][:, 0:len(blocks) * width], hi.bitcast(F32),
                                          ALU.subtract).then_inc(lo_done, 1)
                    dve.wait_ge(hi_done, len(jobs) + 1)
                    dve.tensor_tensor(Kl_lo[:].rearrange("p m b -> p (m b)"), psum[6][:, 0:NQ * B],
                                      Kl_hi[:].bitcast(F32).rearrange("p m b -> p (m b)"),
                                      ALU.subtract).then_inc(lo_done, 1)
                    dve.wait_ge(hi_done, len(jobs) + 2)
                    dve.tensor_tensor(vl_lo[:], psum[7][0:B, :], vl_hi[:].bitcast(F32), ALU.subtract).then_inc(lo_done, 1)
                    dve.wait_ge(lo_done, n_split + 2)

        z_in = sb("z_in", [P, BT, CH, L])
        zT_hi, zT_lo = sb("zT_hi", [P, KL, CH, P], F32R), sb("zT_lo", [P, KL, CH, P], F32R)
        V = sb("V", [P, 2, CH, C])
        Pr = sb("Pr", [P, NQ, KW])
        p_last = sb("p_last", [P, LAST_ROWS // NQ, NQ])
        PT = sb("PT", [P, CH, NQ, P])
        pl_parts = sb("pl_parts", [LAST_ROWS, P], F32R)
        v_last = sb("v_last", [LAST_ROWS, P], F32R)
        PL = sb("PL", [LAST_ROWS, NQ, P], F32R)
        OT = sb("OT", [P, NQ, P])
        OT_hi, OT_lo = sb("OT_hi", [P, NQ, P], F32R), sb("OT_lo", [P, NQ, P], F32R)
        Qp = sb("Qp", [P, C])
        xnT = sb("xnT", [P, KC, P])
        nmax = sb("nmax", [P, NQ])
        rsum = sb("rsum", [P, NQ])
        rinv = sb("rinv", [P, NQ])
        bank_misc, bank_kv, bank_s, bank_pt, bank_o = psum[0], psum[1:3], psum[3:7], psum[5:7], psum[7]

        z_got = [sem(f"z_got{j}") for j in range(BT)]
        vl_got = [sem(f"vl_got{j}") for j in range(BT)]
        pe_T, pe_K, pe_V, pe_S = sem("pe_T"), sem("pe_K"), sem("pe_V"), sem("pe_S")
        pe_PT, pe_PL, pe_O = sem("pe_PT"), sem("pe_PL"), sem("pe_O")
        pe_Q, pe_OP = sem("pe_Q"), sem("pe_OP")
        a_T, a_K, a_V, a_E, a_PT, a_O = (sem(n) for n in ("a_T", "a_K", "a_V", "a_E", "a_PT", "a_O"))
        a_X, a_Q = sem("a_X"), sem("a_Q")
        v_T, v_K, v_mx, v_N, v_PT, v_PL, v_O = (sem(n) for n in ("v_T", "v_K", "v_mx", "v_N", "v_PT", "v_PL", "v_O"))
        v_R = sem("v_R")
        v_Q, a_Qh, v_OP = sem("v_Q"), sem("a_Qh"), sem("v_OP")
        a_OT, v_OT = sem("a_OT"), sem("v_OT")
        g_K = sem("g_K")
        a_PL, g_PL = sem("a_PL"), sem("g_PL")

        with nc.Block() as block:
            @block.sync
            def _(sp):
                def body(i, first, last):
                    for j in range(BT):
                        s = BT * i + j
                        need(sp, pe_T, s - BT + 1)
                        b = i * BT + j
                        sp.dma_start(z_in[:, j, :, :], ctx_in[b, 0:LAST, :].rearrange("(p c) l -> p c l", c=CH)
                                     ).then_inc(z_got[j], 16)
                        need(sp, v_PL, s - BT + 1)
                        sp.dma_start(v_last_in[0:2 * NQ, j, :], vlast_dram[b].rearrange("a (m q) -> (a m) q", q=P)
                                     ).then_inc(vl_got[j], 16)
                        sp.dma_start(v_last_in[LO_ROW:LAST_ROWS, j, :], vlast_dram[b, 0].rearrange("(m q) -> m q", q=P)
                                     ).then_inc(vl_got[j], 16)
                    if first:
                        ahead(sp)
                peeled(sp, n_tile, body)

            def transpose_z(pe, s, i, j):
                pe.wait_ge(z_got[j], 16 * i + 16)
                for k in range(KL):
                    for c in range(CH):
                        at = (k * CH + c) * P
                        mm = pe.transpose(bank_misc[:, at:at + P], z_in[:, j, c, k * P:(k + 1) * P], ident[:])
                mm.then_inc(pe_T, 1)

            def turn_x(pe, i):
                pe.wait_ge(v_ln, LN * i + 4)
                for k in range(KC):
                    mm = pe.transpose(bank_misc[:, k * P:(k + 1) * P], xn[:, k * P:(k + 1) * P], ident[:])
                mm.then_inc(pe_X, 1)

            def project_q(pe, i):
                pe.wait_ge(a_X, i + 1)
                for m in range(NQ):
                    for k in range(KC):
                        mm = pe.matmul(bank_misc[:, m * P:(m + 1) * P], WqT[:, k, m * P:(m + 1) * P], xnT[:, k, :],
                                       start=(k == 0), stop=(k == KC - 1))
                mm.then_inc(pe_Q, 1)

            @block.tensor
            def _(pe):
                def turn_p(s):
                    need(pe, a_O, s)
                    need(pe, v_O, s)
                    for c in range(CH):
                        pe.wait_ge(v_N, s + 1)
                        for m in range(NQ):
                            mm = pe.transpose(bank_pt[c][:, m * P:(m + 1) * P], Pr[:, m, c * P:(c + 1) * P], ident[:])
                        mm.then_inc(pe_PT, 1)

                def turn_last(s):
                    pe.transpose(bank_o[0:LAST_ROWS, 0:P],
                                 p_last[:].rearrange("p a m -> p (a m)"), ident[:]).then_inc(pe_PL, 1)

                def values(s, j):
                    pe.wait_ge(g_PL, s + 1)
                    pe.matmul(bank_o[:], v_last[:], PL[:].rearrange("a m q -> a (m q)"), start=True, stop=False,
                              skip_group_check=True)
                    pe.wait_ge(a_V, 2 * s + 2)
                    pe.wait_ge(v_PT, s + 1)
                    pe.wait_ge(a_PT, s + 1)
                    for c in range(CH):
                        for m in range(NQ):
                            mm = pe.matmul(bank_o[:, m * P:(m + 1) * P], V[:, j % 2, c, m * P:(m + 1) * P],
                                           PT[:, c, m, :], start=False, stop=(c == CH - 1), skip_group_check=True)
                    mm.then_inc(pe_O, 1)

                def project_o(i):
                    pe.wait_ge(a_OT, i + 1)
                    pe.wait_ge(v_OT, i + 1)
                    for m in range(NQ):
                        mm = product(pe, bank_misc[:], (OT_hi[:, m, :], OT_lo[:, m, :]),
                                     (WoT_hi[:, m, :], WoT_lo[:, m, :]), m == 0, m == NQ - 1)
                    mm.then_inc(pe_OP, 1)

                turn_x(pe, 0)
                project_q(pe, 0)
                pe.wait_ge(a_Q, 1)
                transpose_z(pe, 0, 0, 0)

                def body(i, first, last):
                    for j in range(BT):
                        s = BT * i + j
                        some = not (first and j == 0)
                        pe.wait_ge(a_T, s + 1)
                        pe.wait_ge(v_T, s + 1)
                        for h in range(2):
                            need(pe, a_V, 2 * s + h - 1)
                            for m in (2 * h, 2 * h + 1):
                                for k in range(KL):
                                    mm = product(pe, bank_kv[h][:, (m % 2) * LAST:(m % 2 + 1) * LAST],
                                                 (Wkv_hi[:, k, m * P:(m + 1) * P], Wkv_lo[:, k, m * P:(m + 1) * P]),
                                                 (zT_hi[:, k].rearrange("p c q -> p (c q)"),
                                                  zT_lo[:, k].rearrange("p c q -> p (c q)")),
                                                 k == 0, k == KL - 1)
                            mm.then_inc(pe_K, 1)
                        if some:
                            turn_p(s - 1)
                            turn_last(s - 1)
                        for c in range(CH):
                            pe.wait_ge(a_K, 2 * s + c + 1)
                            pe.wait_ge(v_K, 2 * s + c + 1)
                            for k in range(KL):
                                mm = product(pe, bank_kv[c][:], (zT_hi[:, k, c, :], zT_lo[:, k, c, :]),
                                             (Wkv_hi[:, k, C:2 * C], Wkv_lo[:, k, C:2 * C]), k == 0, k == KL - 1)
                            mm.then_inc(pe_V, 1)
                        if not (last and j == BT - 1):
                            if j == 0 and not first:
                                pe.wait_ge(v_OP, i)
                            if j == 2 and not last:
                                pe.wait_ge(a_X, i + 2)
                            if j == 3:
                                pe.wait_ge(a_Q, i + 2)
                            transpose_z(pe, s + 1, i + (j + 1) // BT, (j + 1) % BT)
                        pe.wait_ge(v_Q, i + 1)
                        pe.wait_ge(g_K, s + 1)
                        for m in range(NQ):
                            pe.wait_ge(v_K, 2 * s + m // 2 + 1)
                            if m < 2:
                                need(pe, a_E, 4 * s + m - 3)
                            elif some:
                                pe.wait_ge(v_PT if m == 2 else a_PT, s)
                            mm = product(pe, bank_s[m][:, 0:KW], (Q_hi[:, m, j, :], Q_lo[:, m, j, :]),
                                         (K_hi[:, m, :], K_lo[:, m, :]), True, True)
                            mm.then_inc(pe_S, 1)
                        if some:
                            values(s - 1, (j - 1) % BT)
                        if j > 0 and not (last and j < 3):
                            pe.wait_ge(a_T, s + 1 if last else s + 2)
                            pe.wait_ge(v_T, s + 1 if last else s + 2)
                        if j == 1 and not last:
                            turn_x(pe, i + 1)
                        if j == 2 and not last:
                            project_q(pe, i + 1)
                        if j == 3 and not first:
                            project_o(i - 1)
                peeled(pe, n_tile, body)
                s_end = BT * n_tile
                turn_p(s_end - 1)
                turn_last(s_end - 1)
                values(s_end - 1, BT - 1)
                pe.wait_ge(v_OP, n_tile)
                project_o(n_tile - 1)

            def own_heads(eng, i, j, hhs, done, pe_first):
                for hh in hhs:
                    r = slice(hh * HD, (hh + 1) * HD)
                    src = bank_o[r, :].rearrange("p (m q) -> p m q", m=NQ)[:, :, hh * HD:(hh + 1) * HD]
                    dst = OT[r, :, j * HD:(j + 1) * HD]
                    op = eng.copy(dst, src) if pe_first else eng.tensor_copy(dst, src)
                op.then_inc(done, 1)

            @block.scalar
            def _(act):
                def z_hi(s):
                    act.wait_ge(pe_T, s + 1)
                    act.copy(zT_hi[:].rearrange("p k c q -> p (k c q)"), bank_misc[:]).then_inc(a_T, 1)

                def x_out(i):
                    act.wait_ge(pe_X, i + 1)
                    act.copy(xnT[:].rearrange("p k q -> p (k q)"), bank_misc[:]).then_inc(a_X, 1)

                def q_hi(i):
                    act.wait_ge(pe_Q, i + 1)
                    need(act, v_Q, i)
                    act.mul(Qp[:], bank_misc[:], SCALE).then_inc(a_Q, 1)

                def spread_hi(i):
                    act.wait_ge(a_Q, i + 1)
                    need(act, pe_S, 4 * BT * i)
                    for hh in range(4):
                        r = slice(hh * HD, (hh + 1) * HD)
                        op = act.copy(Q_hi[r, :, :, r], Qp[r, :].rearrange("p (m b t) -> p m b t", m=NQ, b=BT))
                    op.then_inc(a_Qh, 1)

                def pt_out(s):
                    act.wait_ge(pe_PT, 2 * s + 2)
                    act.copy(PT[:, 1].rearrange("p m q -> p (m q)"), bank_pt[1][:]).then_inc(a_PT, 1)
                    act.wait_ge(pe_PL, s + 1)
                    need(act, g_PL, s)
                    act.copy(pl_parts[:], bank_o[0:LAST_ROWS, 0:P]).then_inc(a_PL, 1)

                def ot_hi(i):
                    act.wait_ge(a_O, BT * i + BT)
                    act.wait_ge(v_O, BT * i + BT)
                    act.copy(OT_hi[:], OT[:]).then_inc(a_OT, 1)

                def o_out(s, i, j):
                    act.wait_ge(pe_O, s + 1)
                    if j == 0:
                        need(act, v_OT, i)
                    own_heads(act, i, j, (0, 1), a_O, True)

                x_out(0)
                q_hi(0)
                spread_hi(0)
                z_hi(0)

                def body(i, first, last):
                    for j in range(BT):
                        s = BT * i + j
                        some = not (first and j == 0)
                        for h in range(2):
                            act.wait_ge(pe_K, 2 * s + h + 1)
                            act.copy(K_hi[:, 2 * h:2 * h + 2, 0:LAST],
                                     bank_kv[h][:].rearrange("p (m q) -> p m q", m=2)).then_inc(a_K, 1)
                        if j == 1 and not first:
                            ot_hi(i - 1)
                        if some:
                            pt_out(s - 1)
                        for c in range(CH):
                            act.wait_ge(pe_V, 2 * s + c + 1)
                            act.copy(V[:, j % 2, c, :], bank_kv[c][:]).then_inc(a_V, 1)
                        if not (last and j == BT - 1):
                            z_hi(s + 1)
                        for m in range(NQ):
                            act.wait_ge(v_mx, 4 * s + m + 1)
                            if m == 0:
                                need(act, pe_PL, s)
                                need(act, v_R, s)
                            act.activation(Pr[:, m, 0:NK], bank_s[m][:, 0:NK], ACT.Exp, bias=nmax[:, m:m + 1],
                                           scale=1.0, accum_out=rsum[:, m:m + 1]).then_inc(a_E, 1)
                        if j == BT - 1 and not last:
                            spread_hi(i + 1)
                        if some:
                            o_out(s - 1, i if j else i - 1, (j - 1) % BT)
                        if j == 1 and not last:
                            x_out(i + 1)
                        if j == 2 and not last:
                            q_hi(i + 1)
                peeled(act, n_tile, body)
                s_end = BT * n_tile
                pt_out(s_end - 1)
                o_out(s_end - 1, n_tile - 1, BT - 1)
                ot_hi(n_tile - 1)

            @block.vector
            def _(dve):
                def z_lo(s):
                    dve.wait_ge(a_T, s + 1)
                    dve.tensor_tensor(zT_lo[:].rearrange("p k c q -> p (k c q)"), bank_misc[:],
                                      zT_hi[:].bitcast(F32).rearrange("p k c q -> p (k c q)"),
                                      ALU.subtract).then_inc(v_T, 1)

                def spread_lo(i):
                    dve.wait_ge(a_Qh, i + 1)
                    for hh in range(4):
                        r = slice(hh * HD, (hh + 1) * HD)
                        op = dve.tensor_tensor(Q_lo[r, :, :, r], Qp[r, :].rearrange("p (m b t) -> p m b t", m=NQ, b=BT),
                                               Q_hi[r, :, :, r].bitcast(F32), ALU.subtract)
                    op.then_inc(v_Q, 1)

                def pt_out(s, i, j):
                    dve.wait_ge(pe_PT, 2 * s + 1)
                    need(dve, pe_O, s)
                    dve.tensor_copy(PT[:, 0].rearrange("p m q -> p (m q)"), bank_pt[0][:]).then_inc(v_PT, 1)
                    dve.wait_ge(vl_got[j], 32 * i + 32)
                    dve.tensor_copy(v_last[:], v_last_in[:, j, :])
                    dve.wait_ge(a_PL, s + 1)
                    low = slice(LO_ROW, LAST_ROWS)
                    dve.tensor_tensor(pl_parts[low, :], bank_o[low, 0:P], pl_parts[low, :].bitcast(F32),
                                      ALU.subtract).then_inc(v_PL, 1)

                def ot_lo(i):
                    dve.wait_ge(a_OT, i + 1)
                    dve.tensor_tensor(OT_lo[:], OT[:], OT_hi[:].bitcast(F32), ALU.subtract).then_inc(v_OT, 1)

                def o_out(s, i, j):
                    dve.wait_ge(pe_O, s + 1)
                    if j == 0:
                        need(dve, v_OT, i)
                    own_heads(dve, i, j, (2, 3), v_O, False)

                def add_residual(i):
                    dve.wait_ge(pe_OP, i + 1)
                    dve.tensor_tensor(x_res[:, i, :], bank_misc[:], x_res[:, i, :], ALU.add).then_inc(v_OP, 1)

                dve.memset(waiter[:], 0.0).then_inc(v_OP, 1)
                spread_lo(0)
                z_lo(0)

                def body(i, first, last):
                    for j in range(BT):
                        s = BT * i + j
                        some = not (first and j == 0)
                        if j == 1 and not last:
                            normalise(dve, i + 1)
                        for h in range(2):
                            dve.wait_ge(a_K, 2 * s + h + 1)
                            dve.tensor_tensor(K_lo[:, 2 * h:2 * h + 2, 0:LAST],
                                              bank_kv[h][:].rearrange("p (m q) -> p m q", m=2),
                                              K_hi[:, 2 * h:2 * h + 2, 0:LAST].bitcast(F32),
                                              ALU.subtract).then_inc(v_K, 1)
                        if j == 1 and not first:
                            ot_lo(i - 1)
                        if some:
                            pt_out(s - 1, i if j else i - 1, (j - 1) % BT)
                        if j == 0 and not last:
                            if first:
                                dve.wait_ge(x_rest, 16)
                            statistics(dve, i + 1)
                        for m in range(NQ):
                            dve.wait_ge(pe_S, 4 * s + m + 1)
                            if m == 0:
                                need(dve, a_E, 4 * s)
                            dve.tensor_reduce(nmax[:, m:m + 1], bank_s[m][:, 0:NK], AX_X, ALU.max,
                                              negate=True).then_inc(v_mx, 1)
                            if m == 1 and not (last and j == BT - 1):
                                z_lo(s + 1)
                        dve.wait_ge(a_E, 4 * s + 4)
                        dve.reciprocal(rinv[:], rsum[:]).then_inc(v_R, 1)
                        dve.wait_ge(v_R, s + 1)
                        need(dve, pe_PL, s)
                        dve.tensor_tensor(p_last[:], Pr[:, :, LAST].unsqueeze(1).to_broadcast([P, LAST_ROWS // NQ, NQ]),
                                          rinv[:].unsqueeze(1).to_broadcast([P, LAST_ROWS // NQ, NQ]), ALU.mult)
                        for m in range(NQ):
                            op = dve.tensor_scalar(Pr[:, m, 0:LAST], Pr[:, m, 0:LAST], rinv[:, m:m + 1], None, ALU.mult)
                        op.then_inc(v_N, 1)
                        if some:
                            o_out(s - 1, i if j else i - 1, (j - 1) % BT)
                        if j == BT - 1 and not last:
                            spread_lo(i + 1)
                        if j == BT - 1 and not first:
                            add_residual(i - 1)
                peeled(dve, n_tile, body)
                s_end = BT * n_tile
                pt_out(s_end - 1, n_tile - 1, BT - 1)
                o_out(s_end - 1, n_tile - 1, BT - 1)
                ot_lo(n_tile - 1)
                add_residual(n_tile - 1)
                dve.wait_ge(v_OP, n_tile + 1)

            @block.gpsimd
            def _(pool):
                def mask_last(s):
                    pool.wait_ge(v_PL, s + 1)
                    need(pool, pe_O, s)
                    pool.tensor_tensor(PL[:], pl_parts[:].bitcast(F32).unsqueeze(1).to_broadcast([LAST_ROWS, NQ, P]),
                                       quad_mask[:], ALU.mult).then_inc(g_PL, 1)

                def body(i, first, last):
                    for j in range(BT):
                        s = BT * i + j
                        need(pool, pe_S, 4 * s)
                        b = i * BT + j
                        pool.tensor_copy(K_hi[:, :, LAST], Kl_hi[:, :, bass.ds(b, 1)].rearrange("p m o -> p (m o)"))
                        pool.tensor_copy(K_lo[:, :, LAST], Kl_lo[:, :, bass.ds(b, 1)].rearrange("p m o -> p (m o)")
                                         ).then_inc(g_K, 1)
                        if not (first and j == 0):
                            mask_last(s - 1)
                        if j == 0 and not last:
                            rstd_of(pool, i + 1)
                peeled(pool, n_tile, body)
                mask_last(BT * n_tile - 1)


class Steps:

    def __init__(self, sem, names):
        self.sem, self.names, self.next = sem, names.split(), 0

    def done(self, op, name):
        assert self.names[self.next] == name, (name, self.names[self.next])
        self.next = (self.next + 1) % len(self.names)
        return op.then_inc(self.sem, 1)

    def wait(self, eng, i, name):
        need(eng, self.sem, len(self.names) * i + self.names.index(name) + 1)


def statistics(dve, steps, i, suffix, x, st6, mv, waiter):
    dve.memset(waiter[:], 0.0)
    steps.done(dve.bn_stats(st6[:], x), "stats" + suffix)
    steps.wait(dve, i, "stats" + suffix)
    dve.memset(waiter[:], 0.0)
    steps.done(dve.bn_aggr(mv[:], st6[:]), "aggr" + suffix)
    steps.wait(dve, i, "aggr" + suffix)
    steps.done(dve.tensor_scalar(mv[:, 1:2], mv[:, 1:2], EPS, None, ALU.add), "eps" + suffix)


def normalise(dve, steps, pool_steps, i, suffix, x, mv, rstd, out):
    pool_steps.wait(dve, i, "rstd" + suffix)
    steps.done(dve.tensor_scalar(out[:], x, mv[:, 0:1], rstd[:], ALU.subtract, ALU.mult), "xn" + suffix)


def self_attention_and_routing(nc, wq, w_down, wk_up, wv_up, wo, Wr, rope, x_res, ident, xs_dram,
                               gate_w, row_all, pick_all, count, region, Tlen):
    n_tile, C = x_res.shape[1], x_res.shape[2]
    E = Wr.shape[1]
    L = w_down.shape[1]
    KC, KL, NQ, HD, BT = C // P, L // P, C // P, 32, P // Tlen
    NH = C // HD
    SCALE = HD ** -0.5
    assert HD == Tlen

    with ExitStack() as ctx:
        def sb(name, shape, dt=F32):
            return ctx.enter_context(nc.sbuf_tensor(name, shape, dt))

        def steps(name, names):
            return Steps(ctx.enter_context(nc.semaphore(name)), names)

        Wq, Wdown = sb("sa_wq", [P, KC, C]), sb("sa_down", [P, KC, L])
        Wk, Wv, Wo = sb("sa_wk", [P, KL, C]), sb("sa_wv", [P, KL, C]), sb("sa_wo", [P, KC, C])
        Wg = sb("sa_wr", [P, KC, E])
        rope_t = sb("rope_t", [P, 2, HD])
        below = sb("below", [P, P])
        ones = sb("ones", [P, P])
        rank8 = sb("rank8", [P, E])
        start8 = sb("start8", [P, E])
        mhalf = sb("sa_mhalf", [P, 1])
        xn, xnT = sb("sa_xn", [P, C]), sb("sa_xnT", [P, KC, P])
        latT = sb("latT", [P, KL, P])
        tq1, tq2, tk1, tk2 = (sb(n, [P, C]) for n in ("tq1", "tq2", "tk1", "tk2"))
        qr, kr = sb("qr", [P, C]), sb("kr", [P, C])
        Vt = sb("Vt", [P, C])
        Qd = sb("Qd", [P, NQ, BT, P])
        KT = sb("sa_KT", [P, NQ, P])
        Ex, Pm = sb("Ex", [P, NQ * BT, Tlen]), sb("Pm", [P, NQ, P])
        mx, sm, ri = sb("mx", [P, NQ * BT]), sb("sm", [P, NQ * BT]), sb("ri", [P, NQ * BT])
        PTd = sb("PTd", [P, NQ, BT, P])
        OT = sb("sa_OT", [P, NQ, P])
        xn2, xn2T = sb("xn2", [P, C]), sb("xn2T", [P, KC, P])
        st6, mv, rstd = sb("sa_st6", [P, 6]), sb("sa_mv", [P, 2]), sb("sa_rstd", [P, 1])
        st6b, mvb, rstdb = sb("sb_st6", [P, 6]), sb("sb_mv", [P, 2]), sb("sb_rstd", [P, 1])
        waiter, carrier = sb("sa_waiter", [P, 1]), sb("sa_carrier", [P, 1])
        lg, cand = sb("lg", [P, E]), sb("cand", [P, E])
        oh = sb("oh", [P, 2, E])
        best, top = sb("best", [P, 2]), sb("top", [P, 2])
        both, dest = sb("both", [P, E]), sb("dest", [P, E])
        prod, posf = sb("prod", [P, 2, E]), sb("posf", [P, 2])
        idx = sb("idx", [P, 2], U32)
        dl, ex = sb("dl", [P, 1]), sb("ex", [P, 2])
        bank = [ctx.enter_context(nc.psum_tensor(f"sa_bank{i}", [P, 512], F32)) for i in range(8)]

        w_got = ctx.enter_context(nc.semaphore("sa_w_got"))
        c_set = ctx.enter_context(nc.semaphore("sa_c_set"))
        sent = ctx.enter_context(nc.semaphore("rows_sent"))
        pA, aA = steps("pA", "XT Q lat K V"), steps("aA", "xnT latT V")
        vL, gL = steps("vL", "stats aggr eps xn"), steps("gL", "rstd")
        vA, gA = steps("vA", "q k"), steps("gA", "qr kr")
        pB, aB, vB = steps("pB", "QT KT S"), steps("aB", "q kt exp"), steps("vB", "q mx sub sum rec prob")
        pC, pO, pD = steps("pC", "PT PV0 PV1 PV2 PV3"), steps("pO", "OP"), steps("pD", "XT2 G R")
        aC, aD = steps("aC", "pt ov0 ov1 ov2 ov3"), steps("aD", "xt2 ew")
        vC = steps("vC", "pt ov0 ov1 ov2 ov3 add")
        vD = steps("vD", "stats2 aggr2 eps2 xn2 lg top0 eq0 best0 oh0 less top1 eq1 best1 oh1 both dl e1 w0 w1 "
                         "dest prod pos idx cnt")
        gD = steps("gD", "rstd2")
        n_w = 7

        def has(i, k):
            return not isinstance(i, int) or i + k < n_tile

        def tiles(eng, body):
            for i in range(2):
                body(i)
            with eng.Fori(2, n_tile - 2) as i:
                body(i)
            for i in range(n_tile - 2, n_tile):
                body(i)

        with nc.Block() as block:
            @block.sync
            def _(sp):
                for dst, src in ((Wq, wq), (Wdown, w_down), (Wk, wk_up), (Wv, wv_up), (Wo, wo), (Wg, Wr)):
                    sp.dma_start(dst[:], src.rearrange("(k p) c -> p k c", p=P)).then_inc(w_got, 16)
                sp.dma_start(rope_t[:], rope.rearrange("p (a d) -> p a d", a=2)).then_inc(w_got, 16)

            @block.tensor
            def _(pe):
                def A_turn(i):
                    vL.wait(pe, i, "xn")
                    vD.wait(pe, i - 3, "cnt")
                    for k in range(KC):
                        mm = pe.transpose(bank[0][:, k * P:(k + 1) * P], xn[:, k * P:(k + 1) * P], ident[:])
                    pA.done(mm, "XT")

                def A_q(i):
                    aA.wait(pe, i, "xnT")
                    vC.wait(pe, i - 2, "add")
                    for k in range(KC):
                        mm = pe.matmul(bank[1][:], xnT[:, k, :], Wq[:, k, :], start=(k == 0), stop=(k == KC - 1))
                    pA.done(mm, "Q")

                def A_lat(i):
                    vA.wait(pe, i - 1, "k")
                    for m in range(KL):
                        for k in range(KC):
                            mm = pe.matmul(bank[2][:, m * P:(m + 1) * P], Wdown[:, k, m * P:(m + 1) * P],
                                           xnT[:, k, :], start=(k == 0), stop=(k == KC - 1))
                    pA.done(mm, "lat")

                def A_k(i):
                    aA.wait(pe, i, "latT")
                    for k in range(KL):
                        mm = pe.matmul(bank[2][:], latT[:, k, :], Wk[:, k, :], start=(k == 0), stop=(k == KL - 1))
                    pA.done(mm, "K")

                def A_v(i):
                    aA.wait(pe, i - 1, "V")
                    for k in range(KL):
                        mm = pe.matmul(bank[3][:], latT[:, k, :], Wv[:, k, :], start=(k == 0), stop=(k == KL - 1))
                    pA.done(mm, "V")

                def C_turn(i):
                    vD.wait(pe, i, "xn2")
                    if has(i, 2):
                        aA.wait(pe, i + 2, "xnT")
                    for k in range(KC):
                        mm = pe.transpose(bank[0][:, k * P:(k + 1) * P], xn2[:, k * P:(k + 1) * P], ident[:])
                    pD.done(mm, "XT2")

                def C_gate(i):
                    aD.wait(pe, i, "xt2")
                    for k in range(KC):
                        mm = pe.matmul(bank[0][:, 0:E], xn2T[:, k, :], Wg[:, k, :], start=(k == 0), stop=(k == KC - 1))
                    pD.done(mm, "G")

                def C_rank(i):
                    vD.wait(pe, i, "both")
                    pe.matmul(bank[0][:, 2 * E:3 * E], below[:], both[:], start=True, stop=True)
                    pD.done(pe.matmul(bank[0][:, 3 * E:4 * E], ones[:], both[:], start=True, stop=True), "R")

                pe.wait_ge(w_got, 16 * n_w)
                A_turn(0)
                A_q(0)
                A_lat(0)
                A_k(0)
                A_v(0)

                def body(i):
                    behind = not (isinstance(i, int) and i == 0)
                    if has(i, 1):
                        A_turn(i + 1)
                    gA.wait(pe, i, "qr")
                    aB.wait(pe, i - 1, "exp")
                    for m in range(NQ):
                        mm = pe.transpose(bank[4][:, m * P:(m + 1) * P], qr[:, m * P:(m + 1) * P], ident[:])
                    pB.done(mm, "QT")
                    gA.wait(pe, i, "kr")
                    aC.wait(pe, i - 1, "pt")
                    vC.wait(pe, i - 1, "pt")
                    for m in range(NQ):
                        mm = pe.transpose(bank[5][:, m * P:(m + 1) * P], kr[:, m * P:(m + 1) * P], ident[:])
                    pB.done(mm, "KT")
                    if has(i, 1):
                        A_q(i + 1)
                    aB.wait(pe, i, "q")
                    vB.wait(pe, i, "q")
                    aB.wait(pe, i, "kt")
                    for m in range(NQ):
                        for b in range(BT):
                            at = (m * BT + b) * Tlen
                            mm = pe.matmul(bank[4][:, at:at + Tlen], Qd[:, m, b, :],
                                           KT[:, m, b * Tlen:(b + 1) * Tlen], start=True, stop=True)
                    pB.done(mm, "S")
                    if has(i, 1):
                        A_lat(i + 1)
                    if behind:
                        C_turn(i - 1)
                    if has(i, 1):
                        A_k(i + 1)
                    if behind:
                        C_gate(i - 1)
                    if has(i, 1):
                        A_v(i + 1)
                    vB.wait(pe, i, "prob")
                    for m in range(NQ):
                        mm = pe.transpose(bank[5][:, m * P:(m + 1) * P], Pm[:, m, :], ident[:])
                    pC.done(mm, "PT")
                    aC.wait(pe, i, "pt")
                    vC.wait(pe, i, "pt")
                    for m in range(NQ):
                        g = i if m > 1 else i - 1
                        aC.wait(pe, g, f"ov{(m - 2) % NQ}")
                        vC.wait(pe, g, f"ov{(m - 2) % NQ}")
                        mm = pe.matmul(bank[6 + m % 2][:], Vt[:, m * P:(m + 1) * P],
                                       PTd[:, m].rearrange("p b q -> p (b q)"), start=True, stop=True)
                        pC.done(mm, f"PV{m}")
                    aC.wait(pe, i, "ov3")
                    vC.wait(pe, i, "ov3")
                    if has(i, 1):
                        vA.wait(pe, i + 1, "q")
                    for m in range(NQ):
                        mm = pe.matmul(bank[1][:], OT[:, m, :], Wo[:, m, :], start=(m == 0), stop=(m == NQ - 1))
                    pO.done(mm, "OP")
                    if behind:
                        C_rank(i - 1)
                tiles(pe, body)
                C_turn(n_tile - 1)
                C_gate(n_tile - 1)
                C_rank(n_tile - 1)

            def own(eng, copy, dst, src, parts):
                for q in parts:
                    op = copy(dst(q), src(q))
                return op

            rows = [slice(q * HD, (q + 1) * HD) for q in range(4)]

            def split_q(eng, copy, parts):
                return own(eng, copy, lambda q: Qd[rows[q], :, :, rows[q]],
                           lambda q: bank[4][rows[q], :].rearrange("p (m b t) -> p m b t", m=NQ, b=BT), parts)

            def split_p(eng, copy, parts):
                return own(eng, copy, lambda q: PTd[rows[q], :, q, :],
                           lambda q: bank[5][rows[q], :].rearrange("p (m q) -> p m q", m=NQ), parts)

            def merge_o(eng, copy, m, parts):
                return own(eng, copy, lambda q: OT[rows[q], m, :].rearrange("p (b t) -> p b t", b=BT),
                           lambda q: bank[6 + m % 2][rows[q], :].rearrange("p (b q) -> p b q", b=BT)[:, :, rows[q]],
                           parts)

            @block.scalar
            def _(act):
                def out(b, n=C):
                    return bank[b][:, 0:n].rearrange("p (k q) -> p k q", q=P)

                def A_xnT(i):
                    pA.wait(act, i, "XT")
                    aA.done(act.copy(xnT[:], out(0)), "xnT")

                def A_lat(i):
                    pA.wait(act, i, "lat")
                    aA.done(act.copy(latT[:], out(2, L)), "latT")

                def A_v(i):
                    pA.wait(act, i, "V")
                    pC.wait(act, i - 1, "PV3")
                    aA.done(act.copy(Vt[:], bank[3][:]), "V")

                def D_turn(i):
                    pD.wait(act, i, "XT2")
                    aD.done(act.copy(xn2T[:], out(0)), "xt2")

                def D_weight(i):
                    vD.wait(act, i, "dl")
                    aD.done(act.activation(ex[:, 0:1], dl[:], ACT.Exp), "ew")

                act.wait_ge(c_set, 8)
                A_xnT(0)
                A_lat(0)
                A_v(0)

                def body(i):
                    if has(i, 1):
                        A_xnT(i + 1)
                    pB.wait(act, i, "QT")
                    aB.done(split_q(act, act.copy, (0, 1)), "q")
                    pB.wait(act, i, "KT")
                    aB.done(act.copy(KT[:], out(5)), "kt")
                    vB.wait(act, i, "sub")
                    aB.done(act.activation(Ex[:], Ex[:], ACT.Exp, scale=SCALE), "exp")
                    if has(i, 1):
                        A_lat(i + 1)
                    if not (isinstance(i, int) and i == 0):
                        D_turn(i - 1)
                    pC.wait(act, i, "PT")
                    aC.done(split_p(act, act.copy, (0, 1)), "pt")
                    for m in range(NQ):
                        pC.wait(act, i, f"PV{m}")
                        if m == 0:
                            pO.wait(act, i - 1, "OP")
                        aC.done(merge_o(act, act.copy, m, (0, 1)), f"ov{m}")
                    if has(i, 1):
                        A_v(i + 1)
                    if not (isinstance(i, int) and i == 0):
                        D_weight(i - 1)
                tiles(act, body)
                D_turn(n_tile - 1)
                D_weight(n_tile - 1)

            @block.vector
            def _(dve):
                def A_stats(i):
                    statistics(dve, vL, i, "", x_res[:, i, :], st6, mv, waiter)

                def A_norm(i):
                    pA.wait(dve, i - 1, "XT")
                    normalise(dve, vL, gL, i, "", x_res[:, i, :], mv, rstd, xn)

                def rotate(src, t1, t2):
                    heads = "p (h d) -> p h d"
                    dve.tensor_tensor(t1[:].rearrange(heads, h=NH), src.rearrange(heads, h=NH),
                                      rope_t[:, 0, :].unsqueeze(1).to_broadcast([P, NH, HD]), ALU.mult)
                    pair = "p (h f e) -> p h f e"
                    for e in range(2):
                        op = dve.tensor_tensor(
                            t2[:].rearrange(pair, h=NH, e=2)[:, :, :, e], src.rearrange(pair, h=NH, e=2)[:, :, :, 1 - e],
                            rope_t[:, 1, :].rearrange("p (f e) -> p f e", e=2)[:, :, e].unsqueeze(1)
                            .to_broadcast([P, NH, HD // 2]), ALU.mult)
                    return op

                def A_q(i):
                    pA.wait(dve, i, "Q")
                    gA.wait(dve, i - 1, "qr")
                    vA.done(rotate(bank[1][:], tq1, tq2), "q")

                def A_k(i):
                    pA.wait(dve, i, "K")
                    gA.wait(dve, i - 1, "kr")
                    vA.done(rotate(bank[2][:], tk1, tk2), "k")

                def D_stats(i):
                    statistics(dve, vD, i, "2", x_res[:, i, :], st6b, mvb, waiter)

                def D_norm(i):
                    need(dve, sent, 32 * i)
                    normalise(dve, vD, gD, i, "2", x_res[:, i, :], mvb, rstdb, xn2)

                def D_choose(i):
                    pD.wait(dve, i, "G")
                    vD.done(dve.tensor_copy(lg[:], bank[0][:, 0:E]), "lg")
                    for n in range(2):
                        vD.wait(dve, i, "less" if n else "lg")
                        vD.done(dve.tensor_reduce(top[:, n:n + 1], lg[:], AX_X, ALU.max), f"top{n}")
                        vD.wait(dve, i, f"top{n}")
                        vD.done(dve.scalar_tensor_tensor(cand[:], lg[:], top[:, n:n + 1], rank8[:],
                                                         ALU.is_equal, ALU.mult), f"eq{n}")
                        vD.wait(dve, i, f"eq{n}")
                        vD.done(dve.tensor_reduce(best[:, n:n + 1], cand[:], AX_X, ALU.max), f"best{n}")
                        vD.wait(dve, i, f"best{n}")
                        vD.done(dve.tensor_scalar(oh[:, n, :], rank8[:], best[:, n:n + 1], None, ALU.is_equal), f"oh{n}")
                        vD.wait(dve, i, f"oh{n}")
                        if n == 0:
                            vD.done(dve.scalar_tensor_tensor(lg[:], oh[:, 0, :], -3e38, lg[:], ALU.mult, ALU.add), "less")
                    vD.done(dve.tensor_tensor(both[:], oh[:, 0, :], oh[:, 1, :], ALU.add), "both")
                    vD.done(dve.tensor_tensor(dl[:], top[:, 1:2], top[:, 0:1], ALU.subtract), "dl")

                def D_place(i):
                    aD.wait(dve, i, "ew")
                    vD.done(dve.tensor_scalar(ex[:, 1:2], ex[:, 0:1], 1.0, None, ALU.add), "e1")
                    vD.wait(dve, i, "e1")
                    vD.done(dve.reciprocal(gate_w[:, i, 0:1], ex[:, 1:2]), "w0")
                    vD.wait(dve, i, "w0")
                    vD.done(dve.tensor_tensor(gate_w[:, i, 1:2], ex[:, 0:1], gate_w[:, i, 0:1], ALU.mult), "w1")
                    pD.wait(dve, i, "R")
                    vD.done(dve.tensor_tensor(dest[:], bank[0][:, 2 * E:3 * E], count[:], ALU.add), "dest")
                    vD.wait(dve, i, "dest")
                    vD.done(dve.tensor_tensor(prod[:], oh[:], dest[:].unsqueeze(1).to_broadcast([P, 2, E]), ALU.mult), "prod")
                    vD.wait(dve, i, "prod")
                    vD.done(dve.tensor_reduce(posf[:], prod[:], AX_X, ALU.add), "pos")
                    vD.wait(dve, i, "pos")
                    need(dve, sent, 32 * i)
                    dve.tensor_copy(row_all[:, i, :], posf[:])
                    dve.tensor_copy(pick_all[:, i, :], oh[:].rearrange("p n e -> p (n e)"))
                    vD.done(dve.tensor_copy(idx[:], posf[:]), "idx")
                    vD.done(dve.tensor_tensor(count[:], bank[0][:, 3 * E:4 * E], count[:], ALU.add), "cnt")
                    vD.wait(dve, i, "cnt")

                A_stats(0)
                A_norm(0)
                dve.wait_ge(w_got, 16 * n_w)
                dve.wait_ge(c_set, 8)
                A_q(0)
                A_k(0)
                A_stats(1)
                A_norm(1)

                def body(i):
                    behind = not (isinstance(i, int) and i == 0)
                    pB.wait(dve, i, "QT")
                    vB.done(split_q(dve, dve.tensor_copy, (2, 3)), "q")
                    if behind:
                        D_norm(i - 1)
                    if has(i, 2):
                        A_stats(i + 2)
                    if has(i, 1):
                        A_q(i + 1)
                    pB.wait(dve, i, "S")
                    group = "p (g k) -> p g k"
                    vB.done(dve.tensor_reduce(mx[:], bank[4][:].rearrange(group, k=Tlen), AX_X, ALU.max), "mx")
                    vB.wait(dve, i, "mx")
                    vB.wait(dve, i - 1, "prob")
                    vB.done(dve.tensor_tensor(Ex[:], bank[4][:].rearrange(group, k=Tlen),
                                              mx[:].unsqueeze(2).to_broadcast([P, NQ * BT, Tlen]), ALU.subtract), "sub")
                    aB.wait(dve, i, "exp")
                    vB.done(dve.tensor_reduce(sm[:], Ex[:], AX_X, ALU.add), "sum")
                    vB.wait(dve, i, "sum")
                    vB.done(dve.reciprocal(ri[:], sm[:]), "rec")
                    vB.wait(dve, i, "rec")
                    vB.done(dve.tensor_tensor(Pm[:].rearrange("p m (b k) -> p (m b) k", k=Tlen), Ex[:],
                                              ri[:].unsqueeze(2).to_broadcast([P, NQ * BT, Tlen]), ALU.mult), "prob")
                    if has(i, 2):
                        A_norm(i + 2)
                    if has(i, 1):
                        A_k(i + 1)
                    pC.wait(dve, i, "PT")
                    vC.done(split_p(dve, dve.tensor_copy, (2, 3)), "pt")
                    for m in range(NQ):
                        pC.wait(dve, i, f"PV{m}")
                        if m == 0:
                            pO.wait(dve, i - 1, "OP")
                        vC.done(merge_o(dve, dve.tensor_copy, m, (2, 3)), f"ov{m}")
                    if behind:
                        D_choose(i - 1)
                    pO.wait(dve, i, "OP")
                    vC.done(dve.tensor_tensor(x_res[:, i, :], bank[1][:], x_res[:, i, :], ALU.add), "add")
                    vC.wait(dve, i, "add")
                    if behind:
                        D_place(i - 1)
                    D_stats(i)
                tiles(dve, body)
                D_norm(n_tile - 1)
                D_choose(n_tile - 1)
                D_place(n_tile - 1)

            @block.gpsimd
            def _(pool):
                pool.memset(Qd[:], 0.0).then_inc(c_set, 1)
                pool.memset(PTd[:], 0.0).then_inc(c_set, 1)
                pool.memset(ones[:], 1.0).then_inc(c_set, 1)
                pool.memset(mhalf[:], -0.5).then_inc(c_set, 1)
                pool.iota(rank8[:], pattern=[[-1, E]], base=E, channel_multiplier=0,
                          allow_small_or_imprecise_dtypes=True).then_inc(c_set, 1)
                pool.iota(start8[:], pattern=[[region, E]], base=0, channel_multiplier=0,
                          allow_small_or_imprecise_dtypes=True).then_inc(c_set, 1)
                pool.wait_ge(c_set, 6)
                pool.tensor_copy(count[:], start8[:]).then_inc(c_set, 1)
                pool.affine_select(out=below[:], in_=ones[:], compare_op=ALU.is_ge, fill=0.0, base=-1,
                                   pattern=[[1, P]], channel_multiplier=-1).then_inc(c_set, 1)
                pool.wait_ge(c_set, 8)

                def power(steps_in, steps_out, i, suffix, mv_, rstd_):
                    steps_in.wait(pool, i, "eps" + suffix)
                    steps_in.wait(pool, i - 1, "xn" + suffix)
                    steps_out.done(pool.tensor_tensor(rstd_[:], mv_[:, 1:2], mhalf[:], ALU.pow), "rstd" + suffix)

                def add_up(i, name, out, t1, t2):
                    vA.wait(pool, i, name[0])
                    pB.wait(pool, i - 1, "QT" if name == "qr" else "KT")
                    gA.done(pool.tensor_tensor(out[:], t1[:], t2[:], ALU.add), name)

                def send(i):
                    vD.wait(pool, i, "idx")
                    pool.tensor_tensor(carrier[:], mhalf[:], mhalf[:], ALU.add)
                    for n in range(2):
                        pool.indirect_dma_start(xs_dram, bass.IndirectOffsetOnAxis(ap=idx[:, n:n + 1], axis=0),
                                                xn2[:], None).then_inc(sent, 16)

                power(vL, gL, 0, "", mv, rstd)
                add_up(0, "qr", qr, tq1, tq2)
                add_up(0, "kr", kr, tk1, tk2)
                power(vL, gL, 1, "", mv, rstd)

                def body(i):
                    if has(i, 2):
                        power(vL, gL, i + 2, "", mv, rstd)
                    if has(i, 1):
                        add_up(i + 1, "qr", qr, tq1, tq2)
                    if has(i, 1):
                        add_up(i + 1, "kr", kr, tk1, tk2)
                    if not (isinstance(i, int) and i == 0):
                        send(i - 1)
                    power(vD, gD, i, "2", mvb, rstdb)
                tiles(pool, body)
                send(n_tile - 1)
                pool.wait_ge(sent, 32 * n_tile)


def tile_table(nc, xs_dram, count, row_all, pick_all, table, pos_all, E, n_work, rows, region, most):
    with ExitStack() as ctx:
        def sb(name, shape, dt=F32):
            return ctx.enter_context(nc.sbuf_tensor(name, shape, dt))
        n_step = most // rows
        n_pick = pick_all.shape[1] * 2
        zeros = sb("zeros", [P, rows // P, xs_dram.shape[1]])
        start = sb("t_start", [P, E])
        level = sb("t_level", [P, n_step])
        upto = sb("t_upto", [P, E, E])
        ks = sb("t_ks", [P, n_work])
        n_row, n_t, incl, shift = (sb(n, [P, E]) for n in ("t_nrow", "t_nt", "t_incl", "t_shift"))
        cmp, trip = sb("t_cmp", [P, E, n_step]), sb("t_trip", [P, E, E])
        past, pastv = sb("t_past", [P, n_work, E]), sb("t_pastv", [P, n_work, E])
        ek, first, used, d1, d2, d3 = (sb(n, [P, n_work]) for n in ("t_ek", "t_first", "t_used", "t_d1", "t_d2", "t_d3"))
        moved, move = sb("t_moved", [P, n_pick, E]), sb("t_move", [P, n_pick])
        end_row = sb("t_end", [1, E], I32)
        cs = ctx.enter_context(nc.semaphore("t_const"))
        v = ctx.enter_context(nc.semaphore("t_vector"))
        z = ctx.enter_context(nc.semaphore("t_zeroed"))
        imprecise = dict(allow_small_or_imprecise_dtypes=True)

        with nc.Block() as block:
            @block.gpsimd
            def _(pool):
                pool.iota(start[:], pattern=[[region, E]], base=0, channel_multiplier=0, **imprecise).then_inc(cs, 1)
                pool.iota(level[:], pattern=[[rows, n_step]], base=0, channel_multiplier=0, **imprecise).then_inc(cs, 1)
                pool.iota(ks[:], pattern=[[1, n_work]], base=0, channel_multiplier=0, **imprecise).then_inc(cs, 1)
                pool.memset(upto[:], 1.0).then_inc(cs, 1)
                pool.wait_ge(cs, 4)
                pool.affine_select(out=upto[:], in_=upto[:], compare_op=ALU.is_ge, fill=0.0, base=0,
                                   pattern=[[1, E], [-1, E]], channel_multiplier=0).then_inc(cs, 1)
                pool.memset(zeros[:], 0.0).then_inc(cs, 1)

            @block.vector
            def _(dve):
                n = [0]

                def chain(op):
                    n[0] += 1
                    op.then_inc(v, 1)
                    dve.wait_ge(v, n[0])

                def each_e(t, m):
                    return t[:].unsqueeze(1).to_broadcast([P, m, E])

                chain(dve.tensor_copy(end_row[:], count[0:1, :]))
                dve.wait_ge(cs, 5)
                chain(dve.tensor_tensor(n_row[:], count[:], start[:], ALU.subtract))
                chain(dve.tensor_tensor(cmp[:], n_row[:].unsqueeze(2).to_broadcast([P, E, n_step]),
                                        level[:].unsqueeze(1).to_broadcast([P, E, n_step]), ALU.is_gt))
                chain(dve.tensor_reduce(n_t[:], cmp[:], AX_X, ALU.add))
                chain(dve.tensor_tensor(trip[:], each_e(n_t, E), upto[:], ALU.mult))
                chain(dve.tensor_reduce(incl[:], trip[:], AX_X, ALU.add))
                chain(dve.tensor_tensor(past[:], each_e(incl, n_work),
                                        ks[:].unsqueeze(2).to_broadcast([P, n_work, E]), ALU.is_le))
                chain(dve.tensor_reduce(ek[:], past[:], AX_X, ALU.add))
                chain(dve.tensor_tensor(pastv[:], past[:], each_e(incl, n_work), ALU.mult))
                chain(dve.tensor_reduce(first[:], pastv[:], AX_X, ALU.max))
                chain(dve.tensor_scalar(used[:], ek[:], float(E), None, ALU.is_lt))
                chain(dve.tensor_tensor(d1[:], ks[:], first[:], ALU.subtract))
                chain(dve.tensor_tensor(d2[:], d1[:], used[:], ALU.mult))
                chain(dve.tensor_scalar(d1[:], d2[:], float(rows), None, ALU.mult))
                chain(dve.scalar_tensor_tensor(d3[:], ek[:], float(region), d1[:], ALU.mult, ALU.add))
                chain(dve.tensor_copy(table[:, 1, :], d3[0:1, :]))
                chain(dve.tensor_scalar(d1[:], ek[:], float(E - 1), None, ALU.min))
                chain(dve.tensor_copy(table[:, 0, :], d1[0:1, :]))
                chain(dve.tensor_tensor(shift[:], incl[:], n_t[:], ALU.subtract))
                chain(dve.tensor_scalar(shift[:], shift[:], float(rows), None, ALU.mult))
                chain(dve.tensor_tensor(shift[:], shift[:], start[:], ALU.subtract))
                chain(dve.tensor_tensor(moved[:], pick_all[:].rearrange("p i (n e) -> p (i n) e", e=E),
                                        each_e(shift, n_pick), ALU.mult))
                chain(dve.tensor_reduce(move[:], moved[:], AX_X, ALU.add))
                chain(dve.tensor_tensor(pos_all[:].rearrange("p i n -> p (i n)"),
                                        row_all[:].rearrange("p i n -> p (i n)"), move[:], ALU.add))

            @block.sync
            def _(sp):
                sp.wait_ge(cs, 6)
                sp.dma_start(xs_dram[E * region:E * region + rows, :]
                             .rearrange("(c p) w -> p c w", p=P), zeros[:]).then_inc(z, 16)
                sp.wait_ge(v, 1)
                for e in range(E):
                    at = sp.value_load(end_row[0:1, e:e + 1], min_val=e * region, max_val=e * region + most)
                    sp.dma_start(xs_dram[bass.ds(at, rows), :].rearrange("(c p) w -> p c w", p=P), zeros[:]).then_inc(z, 16)
                sp.wait_ge(z, 16 * (E + 1))


def experts(nc, W1, W3, W2, xs_dram, ys_dram, table, n_work, rows, ident):
    E, C, H = W1.shape
    KC, NH = C // P, H // P
    PAIR = 2
    NS = NH // PAIR
    CH = rows // P
    W = PAIR * P
    n_rows = xs_dram.shape[0]

    with ExitStack() as ctx:
        def sb(name, shape, dt=F32):
            return ctx.enter_context(nc.sbuf_tensor(name, shape, dt))

        def steps(name, names):
            return Steps(ctx.enter_context(nc.semaphore(name)), names)

        raw13, raw2 = sb("raw13", [P, NS, 2, KC, W]), sb("raw2", [P, NS, PAIR, C])
        hi13, lo13 = sb("hi13", [P, NS, 2, KC, W], F32R), sb("lo13", [P, NS, 2, KC, W], F32R)
        hi2, lo2 = sb("hi2", [P, NS, PAIR, C], F32R), sb("lo2", [P, NS, PAIR, C], F32R)
        xg = sb("xg", [P, CH, C])
        xT_hi, xT_lo = sb("xT_hi", [P, KC, rows], F32R), sb("xT_lo", [P, KC, rows], F32R)
        sl, af = sb("sl", [P, 2, rows]), sb("af", [P, 2, rows])
        a_hi, a_lo = sb("a_hi", [P, 2, rows], F32R), sb("a_lo", [P, 2, rows], F32R)
        ysb = sb("ysb", [P, CH, C])
        bank = [ctx.enter_context(nc.psum_tensor(f"mo_bank{i}", [P, 512], F32)) for i in range(6)]
        bank_hg, bank_y, bank_x = bank[0:2], bank[2:4], bank[4:6]

        raw_got = [ctx.enter_context(nc.semaphore(f"raw_got{c}")) for c in range(NS)]
        x_got = ctx.enter_context(nc.semaphore("x_got"))
        y_put = ctx.enter_context(nc.semaphore("y_put"))
        pM = steps("pM", "HG0 HG1 Y0 HG2 Y1 HG3 Y2 HG4 Y3 HG5 Y4 Y5")
        pX = steps("pX", "XT")
        pieces = [(c, q) for c in range(NS) for q in range(3)]
        aM, aX = steps("aM", "s0 s1 s2 s3 s4 s5 y"), steps("aX", "x0 x1")
        aW, vW = (steps(n, " ".join(f"p{c}{q}" for c, q in pieces)) for n in ("aW", "vW"))
        vM, vX = steps("vM", " ".join(f"m{j} h{j} a{j}" for j in range(NH)) + " y"), steps("vX", "x0 x1")
        when = {0: [(0, 2, 0)], 1: [(0, 2, 1), (0, 2, 2)], 2: [(1, 0, 0), (1, 0, 1)], 3: [(1, 0, 2)],
                4: [(1, 1, 0), (1, 1, 1)], 6: [(1, 1, 2)]}

        def part(c, q):
            if q == 2:
                return [t[:, c].rearrange("p b w -> p (b w)") for t in (raw2, hi2, lo2)]
            return [t[:, c, q].rearrange("p k w -> p (k w)") for t in (raw13, hi13, lo13)]

        with nc.Block() as block:
            @block.sync
            def _(sp):
                def load(k):
                    e = sp.value_load(table[0:1, 0, bass.ds(k, 1)], min_val=0, max_val=E - 1)
                    row = sp.value_load(table[0:1, 1, bass.ds(k, 1)], min_val=0, max_val=n_rows - rows)
                    pX.wait(sp, k - 1, "XT")
                    sp.dma_start(xg[:], xs_dram[bass.ds(row, rows), :].rearrange("(c p) w -> p c w", p=P)).then_inc(x_got, 16)
                    for c in range(NS):
                        vW.wait(sp, k - 1, f"p{c}2")
                        for a, src in enumerate((W1, W3)):
                            sp.dma_start(raw13[:, c, a], src[bass.ds(e, 1), :, c * W:(c + 1) * W]
                                         .rearrange("e (k p) h -> p (e k) h", p=P)).then_inc(raw_got[c], 16)
                        sp.dma_start(raw2[:, c], W2[bass.ds(e, 1), c * W:(c + 1) * W, :]
                                     .rearrange("e (b p) w -> p (e b) w", p=P)).then_inc(raw_got[c], 16)

                def store(k):
                    aM.wait(sp, k, "y")
                    vM.wait(sp, k, "y")
                    sp.dma_start(ys_dram[bass.ds(k * rows, rows), :].rearrange("(c p) w -> p c w", p=P), ysb[:]).then_inc(y_put, 16)

                def body(k, first, last):
                    load(k)
                    if not first:
                        store(k - 1)
                peeled(sp, n_work, body)
                store(n_work - 1)
                sp.wait_ge(y_put, 16 * n_work)

            @block.tensor
            def _(pe):
                def turn(k):
                    pe.wait_ge(x_got, 16 * k + 16)
                    aX.wait(pe, k - 1, "x1")
                    vX.wait(pe, k - 1, "x1")
                    for c in range(CH):
                        for q in range(KC):
                            mm = pe.transpose(bank_x[c][:, q * P:(q + 1) * P], xg[:, c, q * P:(q + 1) * P], ident[:])
                    pX.done(mm, "XT")

                def hg(k, j):
                    c, o = j // PAIR, (j % PAIR) * P
                    if j == 0:
                        aX.wait(pe, k, "x1")
                        vX.wait(pe, k, "x1")
                    vW.wait(pe, k, f"p{c}1")
                    if j > 1:
                        vM.wait(pe, k, f"m{j - 2}")
                    else:
                        vM.wait(pe, k - 1, f"m{NH - 2 + j}")
                    for a in range(2):
                        for q in range(KC):
                            mm = product(pe, bank_hg[j % 2][:, a * rows:(a + 1) * rows],
                                         (hi13[:, c, a, q, o:o + P], lo13[:, c, a, q, o:o + P]),
                                         (xT_hi[:, q, :], xT_lo[:, q, :]), q == 0, q == KC - 1)
                    pM.done(mm, f"HG{j}")

                def down(k, j):
                    if j == 0:
                        aM.wait(pe, k - 1, "y")
                        vM.wait(pe, k - 1, "y")
                    c, b = j // PAIR, j % PAIR
                    vW.wait(pe, k, f"p{c}2")
                    vM.wait(pe, k, f"a{j}")
                    for r in range(CH):
                        mm = product(pe, bank_y[r][:], (a_hi[:, j % 2, r * P:(r + 1) * P], a_lo[:, j % 2, r * P:(r + 1) * P]),
                                     (hi2[:, c, b, :], lo2[:, c, b, :]), j == 0, j == NH - 1)
                    pM.done(mm, f"Y{j}")

                turn(0)

                def body(k, first, last):
                    for j in range(NH):
                        if j == NH - 1 and not last:
                            turn(k + 1)
                        hg(k, j)
                        if j:
                            down(k, j - 1)
                    down(k, NH - 1)
                peeled(pe, n_work, body)

            def slot_free(eng, k, c):
                pM.wait(eng, k - 1, f"Y{PAIR * c + PAIR - 1}")

            @block.scalar
            def _(act):
                def split(k, c, q):
                    raw, hi, _lo = part(c, q)
                    act.wait_ge(raw_got[c], 48 * k + 48)
                    slot_free(act, k, c)
                    aW.done(act.copy(hi, raw), f"p{c}{q}")

                def x_hi(k):
                    if not (isinstance(k, int) and k == 0):
                        pM.wait(act, k - 1, f"HG{NH - 1}")
                    pX.wait(act, k, "XT")
                    for c in range(CH):
                        aX.done(act.copy(xT_hi[:, :, c * P:(c + 1) * P],
                                         bank_x[c][:].rearrange("p (k q) -> p k q", q=P)), f"x{c}")

                x_hi(0)
                for c in range(NS - 1):
                    for q in range(3):
                        split(0, c, q)

                def body(k, first, last):
                    for j in range(NH):
                        pM.wait(act, k, f"HG{j}")
                        if j > 1:
                            vM.wait(act, k, f"m{j - 2}")
                        else:
                            vM.wait(act, k - 1, f"m{NH - 2 + j}")
                        aM.done(act.activation(sl[:, j % 2, :], bank_hg[j % 2][:, 0:rows], ACT.Silu), f"s{j}")
                        if j == NH - 1 and not last:
                            x_hi(k + 1)
                        for ahead, c, q in when.get(j, ()):
                            if not (ahead and last):
                                split(k + ahead, c, q)
                    pM.wait(act, k, f"Y{NH - 1}")
                    need(act, y_put, 16 * k)
                    aM.done(act.copy(ysb[:, 0, :], bank_y[0][:]), "y")
                    if not last:
                        for ahead, c, q in when[NH]:
                            split(k + ahead, c, q)
                peeled(act, n_work, body)

            @block.vector
            def _(dve):
                def split(k, c, q):
                    raw, hi, lo = part(c, q)
                    aW.wait(dve, k, f"p{c}{q}")
                    vW.done(dve.tensor_tensor(lo, raw, hi.bitcast(F32), ALU.subtract), f"p{c}{q}")

                def x_lo(k):
                    for c in range(CH):
                        aX.wait(dve, k, f"x{c}")
                        vX.done(dve.tensor_tensor(xT_lo[:, :, c * P:(c + 1) * P],
                                                  bank_x[c][:].rearrange("p (k q) -> p k q", q=P),
                                                  xT_hi[:, :, c * P:(c + 1) * P].bitcast(F32), ALU.subtract), f"x{c}")

                x_lo(0)
                for c in range(NS - 1):
                    for q in range(3):
                        split(0, c, q)

                def body(k, first, last):
                    for j in range(NH):
                        u = j % 2
                        aM.wait(dve, k, f"s{j}")
                        vM.done(dve.tensor_tensor(af[:, u, :], bank_hg[u][:, rows:2 * rows], sl[:, u, :], ALU.mult), f"m{j}")
                        if j > 1:
                            pM.wait(dve, k, f"Y{j - 2}")
                        else:
                            pM.wait(dve, k - 1, f"Y{NH - 2 + j}")
                        vM.wait(dve, k, f"m{j}")
                        vM.done(dve.tensor_copy(a_hi[:, u, :], af[:, u, :]), f"h{j}")
                        vM.wait(dve, k, f"h{j}")
                        vM.done(dve.tensor_tensor(a_lo[:, u, :], af[:, u, :], a_hi[:, u, :].bitcast(F32), ALU.subtract), f"a{j}")
                        if j == NH - 1 and not last:
                            x_lo(k + 1)
                        for ahead, c, q in when.get(j, ()):
                            if not (ahead and last):
                                split(k + ahead, c, q)
                    pM.wait(dve, k, f"Y{NH - 1}")
                    need(dve, y_put, 16 * k)
                    vM.done(dve.tensor_copy(ysb[:, 1, :], bank_y[1][:]), "y")
                    if not last:
                        for ahead, c, q in when[NH]:
                            split(k + ahead, c, q)
                peeled(dve, n_work, body)


def combine(nc, x_res, ys_dram, gate_w, pos_all, out):
    n_tile, C = x_res.shape[1], x_res.shape[2]
    U = 4
    with ExitStack() as ctx:
        def sb(name, shape, dt=F32):
            return ctx.enter_context(nc.sbuf_tensor(name, shape, dt))

        idx = sb("c_idx", [P, U, 2], U32)
        ya, yb, ob = sb("c_ya", [P, U, C]), sb("c_yb", [P, U, C]), sb("c_ob", [P, U, C])
        one, carrier = sb("c_one", [P, 1]), sb("c_carrier", [P, 1])
        c_set = ctx.enter_context(nc.semaphore("c_one_set"))
        carried = ctx.enter_context(nc.semaphore("c_carried"))
        v_idx = ctx.enter_context(nc.semaphore("c_v_idx"))
        vS = Steps(ctx.enter_context(nc.semaphore("c_vS")), " ".join(f"a{u} b{u}" for u in range(U)))
        got = [ctx.enter_context(nc.semaphore(f"c_got{u}")) for u in range(U)]
        put = [ctx.enter_context(nc.semaphore(f"c_put{u}")) for u in range(U)]
        n_round = n_tile // U
        out_t = out.rearrange("(g u p) c -> g u p c", u=U, p=P)

        with nc.Block() as block:
            @block.gpsimd
            def _(pool):
                pool.memset(one[:], 1.0).then_inc(c_set, 1)
                pool.wait_ge(c_set, 1)

                def body(g, first, last):
                    for u in range(U):
                        pool.wait_ge(v_idx, U * g + u + 1)
                        vS.wait(pool, g - 1, f"b{u}")
                        need(pool, carried, U * g + u)
                        pool.tensor_tensor(carrier[:], one[:], one[:], ALU.add).then_inc(carried, 1)
                        for n, y in ((0, ya), (1, yb)):
                            pool.indirect_dma_start(y[:, u, :], None, ys_dram,
                                                    bass.IndirectOffsetOnAxis(ap=idx[:, u, n:n + 1], axis=0)
                                                    ).then_inc(got[u], 16)
                peeled(pool, n_round, body)

            @block.vector
            def _(dve):
                def body(g, first, last):
                    for u in range(U):
                        need(dve, got[u], 32 * g)
                        i = U * g + u
                        dve.tensor_copy(idx[:, u, :], pos_all[:, i, :]).then_inc(v_idx, 1)
                    for u in range(U):
                        i = U * g + u
                        dve.wait_ge(got[u], 32 * g + 32)
                        need(dve, put[u], 16 * g)
                        vS.done(dve.scalar_tensor_tensor(ob[:, u, :], ya[:, u, :], gate_w[:, i, 0:1], x_res[:, i, :],
                                                         ALU.mult, ALU.add), f"a{u}")
                        vS.wait(dve, g, f"a{u}")
                        vS.done(dve.scalar_tensor_tensor(ob[:, u, :], yb[:, u, :], gate_w[:, i, 1:2], ob[:, u, :],
                                                         ALU.mult, ALU.add), f"b{u}")
                peeled(dve, n_round, body)

            @block.sync
            def _(sp):
                def body(g, first, last):
                    for u in range(U):
                        vS.wait(sp, g, f"b{u}")
                        i = U * g + u
                        sp.dma_start(out[bass.ds(i * P, P), :], ob[:, u, :]).then_inc(put[u], 16)
                peeled(sp, n_round, body)
                for u in range(U):
                    sp.wait_ge(put[u], 16 * n_round)


def perceiver_block(nc, x, ctx_512, xWq, xWkv, xWo, wq, w_down, wk_up, wv_up, wo, Wr, W1, W2, W3, rope, out):
    B, T, C = x.shape
    E = Wr.shape[1]
    n_tok = B * T
    n_tile = n_tok // P
    rows = 2 * P
    region = n_tok + rows
    n_work = (2 * n_tok - E) // rows + E
    xs = nc.dram_tensor("xs", (E * region + rows, C), F32).ap()
    ys = nc.dram_tensor("ys", (n_work * rows, C), F32).ap()
    v_last = nc.dram_tensor("v_last_rows", (B, 2, C), F32).ap()

    with ExitStack() as ctx:
        def sb(name, shape, dt=F32):
            return ctx.enter_context(nc.sbuf_tensor(name, shape, dt))
        x_res = sb("x_res", [P, n_tile, C])
        gate_w = sb("gate_w", [P, n_tile, 2])
        pos_all = sb("pos_all", [P, n_tile, 2], U32)
        row_all = sb("row_all", [P, n_tile, 2])
        pick_all = sb("pick_all", [P, n_tile, 2 * E])
        count = sb("count", [P, E])
        table = sb("table", [1, 2, n_work], I32)
        ident, quad_mask = block_constants(nc, ctx)
        cross_attention(nc, ctx, x.rearrange("b t c -> (b t) c"), ctx_512, xWq, xWkv, xWo, x_res, ident, quad_mask, v_last, lambda sp: None)
        self_attention_and_routing(nc, wq, w_down, wk_up, wv_up, wo, Wr, rope, x_res, ident, xs,
                                   gate_w, row_all, pick_all, count, region, T)
        tile_table(nc, xs, count, row_all, pick_all, table, pos_all, E, n_work, rows, region, n_tok)
        experts(nc, W1, W3, W2, xs, ys, table, n_work, rows, ident)
        combine(nc, x_res, ys, gate_w, pos_all, out.rearrange("b t c -> (b t) c"))


_INS = ['x', 'ctx_512', 'L0_xattn_Wq', 'L0_xattn_Wkv', 'L0_xattn_Wo', 'L0_attn_wq', 'L0_attn_w_down', 'L0_attn_wk_up',
        'L0_attn_wv_up', 'L0_attn_wo', 'L0_ffn_Wr', 'L0_ffn_W1', 'L0_ffn_W2', 'L0_ffn_W3']


def kernel(**inputs):
    import numpy as _np
    import concourse.bacc as _bacc
    from concourse import mybir as _mybir
    from concourse.bass_utils import run_bass_kernel_spmd as _run

    nc = _bacc.Bacc("TRN2", target_bir_lowering=False, num_devices=1)
    arrays, args = {}, []
    for name in _INS:
        a = _np.ascontiguousarray(inputs[name])
        arrays[f"in_{name}_dram"] = a
        args.append(nc.dram_tensor(f"in_{name}_dram", a.shape, _mybir.dt.from_np(a.dtype), kind="ExternalInput").ap())
    B, T, C = inputs['x'].shape
    args.append(nc.inline_tensor(rope_tables(T, 32), name="rope_tables").ap())
    out = nc.dram_tensor("out_0_dram", (B, T, C), _mybir.dt.float32, kind="ExternalOutput").ap()
    perceiver_block(nc, *args, out)
    r = _run(nc, [arrays], core_ids=[0])
    return r.results[0]["out_0_dram"]
```

```python
from contextlib import ExitStack

import numpy as np

import concourse.bass as bass
from concourse import mybir
from concourse.alu_op_type import AluOpType as ALU

F32 = mybir.dt.float32
F32R = mybir.dt.float32r
I32 = mybir.dt.int32
U32 = mybir.dt.uint32
ACT = mybir.ActivationFunctionType
AX_X = mybir.AxisListType.X

P = 128
EPS = 1e-5
ROPE_THETA = 10000.0
LO_ROW = 32
LAST_ROWS = LO_ROW + 4


def need(eng, sem, value):
    if isinstance(value, int) and value <= 0:
        return
    eng.wait_ge(sem, value)


def peeled(eng, n, body):
    body(0, True, n == 1)
    if n > 2:
        with eng.Fori(1, n - 1) as i:
            body(i, False, False)
    if n > 1:
        body(n - 1, False, True)


def product(pe, out, lhs, rhs, start, stop):
    (lh, ll), (rh, rl) = lhs, rhs
    pe.matmul(out, lh, rh, start=start, stop=False)
    pe.matmul(out, ll, rh, start=False, stop=False)
    return pe.matmul(out, lh, rl, start=False, stop=stop)


def rope_tables(T, D):
    inv = 1.0 / ROPE_THETA ** (np.arange(0, D, 2, dtype=np.float32) / D)
    ang = np.outer(np.arange(T, dtype=np.float32), inv)
    cos = np.repeat(np.cos(ang), 2, axis=1)
    sin = np.stack([-np.sin(ang), np.sin(ang)], axis=2).reshape(T, D)
    return np.ascontiguousarray(np.tile(np.concatenate([cos, sin], axis=1), (P // T, 1)).astype(np.float32))


def block_constants(nc, ctx, zeros, tiles):
    ident = ctx.enter_context(nc.sbuf_tensor("ident", [P, P], F32))
    quad_mask = ctx.enter_context(nc.sbuf_tensor("quad_mask", [LAST_ROWS, 4, P], F32))
    s = ctx.enter_context(nc.semaphore("const_ready"))

    with nc.Block() as block:
        @block.gpsimd
        def _(pool):
            pool.memset(ident[:], 0.0).then_inc(s, 1)
            pool.memset(quad_mask[:], 0.0).then_inc(s, 1)
            pool.wait_ge(s, 2)
            pool.affine_select(out=ident[:], in_=ident[:], compare_op=ALU.not_equal, fill=1.0, base=0,
                               pattern=[[-1, P]], channel_multiplier=1).then_inc(s, 1)
            for n, row in enumerate((0, 4, LO_ROW)):
                pool.wait_ge(s, 3 + n)
                pool.affine_select(out=quad_mask[:], in_=quad_mask[:], compare_op=ALU.not_equal, fill=1.0, base=-row,
                                   pattern=[[-1, 4], [0, P]], channel_multiplier=1).then_inc(s, 1)
            pool.memset(zeros[:], 0.0).then_inc(s, 1)
            tiles.constants(pool)
            pool.wait_ge(s, 7)
    return ident, quad_mask


def cross_attention(nc, x_in, ctx_in, Wq, Wkv, Wo, x_res, ident, quad_mask, vlast_dram, ahead,
                    beside):
    n_tile = x_res.shape[1]
    C = x_res.shape[2]
    B, NK, L = ctx_in.shape
    KC = C // P
    KL = L // P
    NQ = C // P
    HD = 32
    BT = P // HD
    CH = 2
    LAST = CH * P
    assert NK == LAST + 1
    KW = LAST + 2
    SCALE = HD ** -0.5

    with ExitStack() as ctx:
        def sb(name, shape, dt=F32):
            return ctx.enter_context(nc.sbuf_tensor(name, shape, dt))

        def sem(name):
            return ctx.enter_context(nc.semaphore(name))

        WqT = sb("WqT", [P, KC, C])
        WoT_hi, WoT_lo = sb("WoT_hi", [P, KC, C], F32R), sb("WoT_lo", [P, KC, C], F32R)
        Wkv_hi, Wkv_lo = sb("Wkv_hi", [P, KL, 2 * C], F32R), sb("Wkv_lo", [P, KL, 2 * C], F32R)
        zl_hi, zl_lo = sb("zl_hi", [P, KL, B], F32R), sb("zl_lo", [P, KL, B], F32R)
        Kl_hi, Kl_lo = sb("Kl_hi", [P, NQ, B], F32R), sb("Kl_lo", [P, NQ, B], F32R)
        vl_hi, vl_lo = sb("vl_hi", [B, C], F32R), sb("vl_lo", [B, C], F32R)
        vl_put = sem("vl_put")
        Q_hi, Q_lo = sb("Q_hi", [P, NQ, BT, P], F32R), sb("Q_lo", [P, NQ, BT, P], F32R)
        K_hi, K_lo = sb("K_hi", [P, NQ, KW], F32R), sb("K_lo", [P, NQ, KW], F32R)
        v_last_in = sb("v_last_in", [LAST_ROWS, BT, P])
        xn = sb("xn", [P, C])
        st6 = sb("st6", [P, 6])
        mv = sb("mv", [P, 2])
        rstd = sb("rstd", [P, 1])
        mhalf = sb("mhalf", [P, 1])
        waiter = sb("waiter", [P, 1])
        LN = 4
        v_ln, g_ln, mh = sem("v_ln"), sem("g_ln"), sem("mhalf_set")
        x_first, x_rest = sem("x_first"), sem("x_rest")
        pe_X = sem("pe_X")

        def statistics(dve, i):
            dve.bn_stats(st6[:], x_res[:, i, :]).then_inc(v_ln, 1)
            dve.wait_ge(v_ln, LN * i + 1)
            dve.memset(waiter[:], 0.0)
            dve.bn_aggr(mv[:], st6[:]).then_inc(v_ln, 1)
            dve.wait_ge(v_ln, LN * i + 2)
            dve.tensor_scalar(mv[:, 1:2], mv[:, 1:2], EPS, None, ALU.add).then_inc(v_ln, 1)

        def normalise(dve, i):
            need(dve, pe_X, i)
            dve.wait_ge(g_ln, i + 1)
            dve.tensor_scalar(xn[:], x_res[:, i, :], mv[:, 0:1], rstd[:], ALU.subtract, ALU.mult
                              ).then_inc(v_ln, 1)

        def rstd_of(pool, i):
            pool.wait_ge(v_ln, LN * i + 3)
            need(pool, v_ln, LN * i)
            pool.tensor_tensor(rstd[:], mv[:, 1:2], mhalf[:], ALU.pow).then_inc(g_ln, 1)

        psum = [ctx.enter_context(nc.psum_tensor(f"xa_bank{i}", [P, 512], F32)) for i in range(8)]

        with ExitStack() as setup:
            def sbs(name, shape, dt=F32):
                return setup.enter_context(nc.sbuf_tensor(name, shape, dt))
            raw_q = sbs("raw_q", [P, KC, C])
            raw_kv = sbs("raw_kv", [P, 2 * C // P, L])
            raw_o = sbs("raw_o", [P, KC, C])
            raw_zl = sbs("raw_zl", [B, L])
            loaded = [setup.enter_context(nc.semaphore(f"w_loaded{i}")) for i in range(4)]
            turned = setup.enter_context(nc.semaphore("w_turned"))
            hi_done = setup.enter_context(nc.semaphore("w_hi"))
            lo_done = setup.enter_context(nc.semaphore("w_lo"))
            zeroed = setup.enter_context(nc.semaphore("w_zeroed"))
            jobs = []
            jobs.append((3, [raw_zl[:, k * P:(k + 1) * P] for k in range(KL)],
                         (zl_hi[:, :, :].rearrange("p k b -> p (k b)"), zl_lo[:, :, :].rearrange("p k b -> p (k b)")), B))
            for k in range(KL):
                for h in range(2):
                    jobs.append((1, [raw_kv[:, 4 * h + o, k * P:(k + 1) * P] for o in range(4)],
                                 (Wkv_hi[:, k, h * C:(h + 1) * C], Wkv_lo[:, k, h * C:(h + 1) * C]), P))
            for k in range(KC):
                jobs.append((2, [raw_o[:, o, k * P:(k + 1) * P] for o in range(KC)], (WoT_hi[:, k, :], WoT_lo[:, k, :]), P))
            for k in range(KC):
                jobs.append((0, [raw_q[:, o, k * P:(k + 1) * P] for o in range(KC)], (WqT[:, k, :], None), P))
            n_split = sum(1 for j in jobs if j[2][1] is not None)

            with nc.Block() as block:
                @block.sync
                def _(sp):
                    sp.dma_start(raw_zl[:], ctx_in[:, LAST, :]).then_inc(loaded[3], 16)
                    sp.dma_start(raw_kv[:], Wkv.rearrange("(o p) c -> p o c", p=P)).then_inc(loaded[1], 16)
                    xt = x_in.rearrange("(i p) c -> p i c", p=P)
                    sp.dma_start(x_res[:, 0, :], xt[:, 0, :]).then_inc(x_first, 16)
                    sp.dma_start(raw_o[:], Wo.rearrange("(o p) c -> p o c", p=P)).then_inc(loaded[2], 16)
                    sp.dma_start(raw_q[:], Wq.rearrange("(o p) c -> p o c", p=P)).then_inc(loaded[0], 16)
                    sp.dma_start(x_res[:, 1:, :], xt[:, 1:, :]).then_inc(x_rest, 16)
                    sp.wait_ge(hi_done, len(jobs) + 2)
                    sp.wait_ge(lo_done, n_split + 2)
                    sp.dma_start(vlast_dram[:, 0, :], vl_hi[:].bitcast(F32)).then_inc(vl_put, 16)
                    sp.dma_start(vlast_dram[:, 1, :], vl_lo[:].bitcast(F32)).then_inc(vl_put, 16)

                @block.gpsimd
                def _(pool):
                    pool.memset(mhalf[:], -0.5).then_inc(mh, 1)
                    pool.wait_ge(mh, 1)
                    rstd_of(pool, 0)
                    pool.memset(Q_hi[:].bitcast(F32), 0.0)
                    pool.memset(Q_lo[:].bitcast(F32), 0.0)
                    pool.memset(K_hi[:].bitcast(F32), 0.0)
                    pool.memset(K_lo[:].bitcast(F32), 0.0)
                    pool.memset(v_last_in[:], 0.0).then_inc(zeroed, 1)
                    pool.wait_ge(zeroed, 1)

                @block.tensor
                def _(pe):
                    for n, (load, blocks, _dst, width) in enumerate(jobs):
                        pe.wait_ge(loaded[load], 16)
                        if n >= 6:
                            pe.wait_ge(hi_done, n - 5)
                            if n - 6 < n_split:
                                pe.wait_ge(lo_done, n - 5)
                        for o, src in enumerate(blocks):
                            mm = pe.transpose(psum[n % 6][:, o * width:(o + 1) * width], src,
                                              ident[0:src.shape[0], 0:src.shape[0]])
                        mm.then_inc(turned, 1)
                    pe.wait_ge(lo_done, n_split)
                    for m in range(NQ):
                        for k in range(KL):
                            mm = product(pe, psum[6][:, m * B:(m + 1) * B],
                                         (Wkv_hi[:, k, m * P:(m + 1) * P], Wkv_lo[:, k, m * P:(m + 1) * P]),
                                         (zl_hi[:, k, :], zl_lo[:, k, :]), k == 0, k == KL - 1)
                    mm.then_inc(turned, 1)
                    for k in range(KL):
                        mm = product(pe, psum[7][0:B, :], (zl_hi[:, k, :], zl_lo[:, k, :]),
                                     (Wkv_hi[:, k, C:2 * C], Wkv_lo[:, k, C:2 * C]), k == 0, k == KL - 1)
                    mm.then_inc(turned, 1)

                @block.scalar
                def _(act):
                    for n, (_load, blocks, (hi, _lo), width) in enumerate(jobs):
                        act.wait_ge(turned, n + 1)
                        act.copy(hi, psum[n % 6][:, 0:len(blocks) * width]).then_inc(hi_done, 1)
                    act.wait_ge(turned, len(jobs) + 1)
                    act.copy(Kl_hi[:].rearrange("p m b -> p (m b)"), psum[6][:, 0:NQ * B]).then_inc(hi_done, 1)
                    act.wait_ge(turned, len(jobs) + 2)
                    act.copy(vl_hi[:], psum[7][0:B, :]).then_inc(hi_done, 1)

                @block.vector
                def _(dve):
                    dve.wait_ge(x_first, 16)
                    statistics(dve, 0)
                    normalise(dve, 0)
                    for n, (_load, blocks, (hi, lo), width) in enumerate(jobs[:n_split]):
                        dve.wait_ge(hi_done, n + 1)
                        dve.tensor_tensor(lo, psum[n % 6][:, 0:len(blocks) * width], hi.bitcast(F32),
                                          ALU.subtract).then_inc(lo_done, 1)
                    dve.wait_ge(hi_done, len(jobs) + 1)
                    dve.tensor_tensor(Kl_lo[:].rearrange("p m b -> p (m b)"), psum[6][:, 0:NQ * B],
                                      Kl_hi[:].bitcast(F32).rearrange("p m b -> p (m b)"),
                                      ALU.subtract).then_inc(lo_done, 1)
                    dve.wait_ge(hi_done, len(jobs) + 2)
                    dve.tensor_tensor(vl_lo[:], psum[7][0:B, :], vl_hi[:].bitcast(F32), ALU.subtract).then_inc(lo_done, 1)
                    dve.wait_ge(lo_done, n_split + 2)

        z_in = sb("z_in", [P, BT, CH, L])
        zT_hi, zT_lo = sb("zT_hi", [P, KL, CH, P], F32R), sb("zT_lo", [P, KL, CH, P], F32R)
        V = sb("V", [P, 2, CH, C])
        Pr = sb("Pr", [P, NQ, KW])
        p_last = sb("p_last", [P, LAST_ROWS // NQ, NQ])
        PT = sb("PT", [P, CH, NQ, P])
        pl_parts = sb("pl_parts", [LAST_ROWS, P], F32R)
        v_last = sb("v_last", [LAST_ROWS, P], F32R)
        PL = sb("PL", [LAST_ROWS, NQ, P], F32R)
        OT = sb("OT", [P, NQ, P])
        OT_hi, OT_lo = sb("OT_hi", [P, NQ, P], F32R), sb("OT_lo", [P, NQ, P], F32R)
        Qp = sb("Qp", [P, C])
        xnT = sb("xnT", [P, KC, P])
        nmax = sb("nmax", [P, NQ])
        rsum = sb("rsum", [P, NQ])
        rinv = sb("rinv", [P, NQ])
        bank_misc, bank_kv, bank_s, bank_pt, bank_o = psum[0], psum[1:3], psum[3:7], psum[5:7], psum[7]

        z_got = [sem(f"z_got{j}") for j in range(BT)]
        vl_got = [sem(f"vl_got{j}") for j in range(BT)]
        pe_T, pe_K, pe_V, pe_S = sem("pe_T"), sem("pe_K"), sem("pe_V"), sem("pe_S")
        pe_PT, pe_PL, pe_O = sem("pe_PT"), sem("pe_PL"), sem("pe_O")
        pe_Q, pe_OP = sem("pe_Q"), sem("pe_OP")
        a_T, a_K, a_V, a_E, a_PT, a_O = (sem(n) for n in ("a_T", "a_K", "a_V", "a_E", "a_PT", "a_O"))
        a_X, a_Q = sem("a_X"), sem("a_Q")
        v_T, v_K, v_mx, v_N, v_PT, v_PL, v_O = (sem(n) for n in ("v_T", "v_K", "v_mx", "v_N", "v_PT", "v_PL", "v_O"))
        v_R = sem("v_R")
        v_Q, a_Qh, v_OP = sem("v_Q"), sem("a_Qh"), sem("v_OP")
        a_OT, v_OT = sem("a_OT"), sem("v_OT")
        g_K = sem("g_K")
        a_PL, g_PL = sem("a_PL"), sem("g_PL")

        with nc.Block() as block:
            @block.sync
            def _(sp):
                def body(i, first, last):
                    for j in range(BT):
                        s = BT * i + j
                        need(sp, pe_T, s - BT + 1)
                        b = i * BT + j
                        sp.dma_start(z_in[:, j, :, :], ctx_in[b, 0:LAST, :].rearrange("(p c) l -> p c l", c=CH)
                                     ).then_inc(z_got[j], 16)
                        if first and j == 0:
                            sp.wait_ge(vl_put, 32)
                        need(sp, v_PL, s - BT + 1)
                        sp.dma_start(v_last_in[0:2 * NQ, j, :], vlast_dram[b].rearrange("a (m q) -> (a m) q", q=P)
                                     ).then_inc(vl_got[j], 16)
                        sp.dma_start(v_last_in[LO_ROW:LAST_ROWS, j, :], vlast_dram[b, 0].rearrange("(m q) -> m q", q=P)
                                     ).then_inc(vl_got[j], 16)
                        beside(sp, b)
                    if first:
                        ahead(sp)
                peeled(sp, n_tile, body)

            def transpose_z(pe, s, i, j):
                pe.wait_ge(z_got[j], 16 * i + 16)
                for k in range(KL):
                    for c in range(CH):
                        at = (k * CH + c) * P
                        mm = pe.transpose(bank_misc[:, at:at + P], z_in[:, j, c, k * P:(k + 1) * P], ident[:])
                mm.then_inc(pe_T, 1)

            def turn_x(pe, i):
                pe.wait_ge(v_ln, LN * i + 4)
                for k in range(KC):
                    mm = pe.transpose(bank_misc[:, k * P:(k + 1) * P], xn[:, k * P:(k + 1) * P], ident[:])
                mm.then_inc(pe_X, 1)

            def project_q(pe, i):
                pe.wait_ge(a_X, i + 1)
                for m in range(NQ):
                    for k in range(KC):
                        mm = pe.matmul(bank_misc[:, m * P:(m + 1) * P], WqT[:, k, m * P:(m + 1) * P], xnT[:, k, :],
                                       start=(k == 0), stop=(k == KC - 1))
                mm.then_inc(pe_Q, 1)

            @block.tensor
            def _(pe):
                def turn_p(s):
                    need(pe, a_O, s)
                    need(pe, v_O, s)
                    for c in range(CH):
                        pe.wait_ge(v_N, s + 1)
                        for m in range(NQ):
                            mm = pe.transpose(bank_pt[c][:, m * P:(m + 1) * P], Pr[:, m, c * P:(c + 1) * P], ident[:])
                        mm.then_inc(pe_PT, 1)

                def turn_last(s):
                    pe.transpose(bank_o[0:LAST_ROWS, 0:P],
                                 p_last[:].rearrange("p a m -> p (a m)"), ident[:]).then_inc(pe_PL, 1)

                def values(s, j):
                    pe.wait_ge(g_PL, s + 1)
                    pe.matmul(bank_o[:], v_last[:], PL[:].rearrange("a m q -> a (m q)"), start=True, stop=False,
                              skip_group_check=True)
                    pe.wait_ge(a_V, 2 * s + 2)
                    pe.wait_ge(v_PT, s + 1)
                    pe.wait_ge(a_PT, s + 1)
                    for c in range(CH):
                        for m in range(NQ):
                            mm = pe.matmul(bank_o[:, m * P:(m + 1) * P], V[:, j % 2, c, m * P:(m + 1) * P],
                                           PT[:, c, m, :], start=False, stop=(c == CH - 1), skip_group_check=True)
                    mm.then_inc(pe_O, 1)

                def project_o(i):
                    pe.wait_ge(a_OT, i + 1)
                    pe.wait_ge(v_OT, i + 1)
                    for m in range(NQ):
                        mm = product(pe, bank_misc[:], (OT_hi[:, m, :], OT_lo[:, m, :]),
                                     (WoT_hi[:, m, :], WoT_lo[:, m, :]), m == 0, m == NQ - 1)
                    mm.then_inc(pe_OP, 1)

                turn_x(pe, 0)
                project_q(pe, 0)
                pe.wait_ge(a_Q, 1)
                transpose_z(pe, 0, 0, 0)

                def body(i, first, last):
                    for j in range(BT):
                        s = BT * i + j
                        some = not (first and j == 0)
                        pe.wait_ge(a_T, s + 1)
                        pe.wait_ge(v_T, s + 1)
                        for h in range(2):
                            need(pe, a_V, 2 * s + h - 1)
                            for m in (2 * h, 2 * h + 1):
                                for k in range(KL):
                                    mm = product(pe, bank_kv[h][:, (m % 2) * LAST:(m % 2 + 1) * LAST],
                                                 (Wkv_hi[:, k, m * P:(m + 1) * P], Wkv_lo[:, k, m * P:(m + 1) * P]),
                                                 (zT_hi[:, k].rearrange("p c q -> p (c q)"),
                                                  zT_lo[:, k].rearrange("p c q -> p (c q)")),
                                                 k == 0, k == KL - 1)
                            mm.then_inc(pe_K, 1)
                        if some:
                            turn_p(s - 1)
                            turn_last(s - 1)
                        for c in range(CH):
                            pe.wait_ge(a_K, 2 * s + c + 1)
                            pe.wait_ge(v_K, 2 * s + c + 1)
                            for k in range(KL):
                                mm = product(pe, bank_kv[c][:], (zT_hi[:, k, c, :], zT_lo[:, k, c, :]),
                                             (Wkv_hi[:, k, C:2 * C], Wkv_lo[:, k, C:2 * C]), k == 0, k == KL - 1)
                            mm.then_inc(pe_V, 1)
                        if not (last and j == BT - 1):
                            if j == 0 and not first:
                                pe.wait_ge(v_OP, i)
                            if j == 2 and not last:
                                pe.wait_ge(a_X, i + 2)
                            if j == 3:
                                pe.wait_ge(a_Q, i + 2)
                            transpose_z(pe, s + 1, i + (j + 1) // BT, (j + 1) % BT)
                        pe.wait_ge(v_Q, i + 1)
                        pe.wait_ge(g_K, s + 1)
                        for m in range(NQ):
                            pe.wait_ge(v_K, 2 * s + m // 2 + 1)
                            if m < 2:
                                need(pe, a_E, 4 * s + m - 3)
                            elif some:
                                pe.wait_ge(v_PT if m == 2 else a_PT, s)
                            mm = product(pe, bank_s[m][:, 0:KW], (Q_hi[:, m, j, :], Q_lo[:, m, j, :]),
                                         (K_hi[:, m, :], K_lo[:, m, :]), True, True)
                            mm.then_inc(pe_S, 1)
                        if some:
                            values(s - 1, (j - 1) % BT)
                        if j > 0 and not (last and j < 3):
                            pe.wait_ge(a_T, s + 1 if last else s + 2)
                            pe.wait_ge(v_T, s + 1 if last else s + 2)
                        if j == 1 and not last:
                            turn_x(pe, i + 1)
                        if j == 2 and not last:
                            project_q(pe, i + 1)
                        if j == 3 and not first:
                            project_o(i - 1)
                peeled(pe, n_tile, body)
                s_end = BT * n_tile
                turn_p(s_end - 1)
                turn_last(s_end - 1)
                values(s_end - 1, BT - 1)
                pe.wait_ge(v_OP, n_tile)
                project_o(n_tile - 1)

            def own_heads(eng, i, j, hhs, done, pe_first):
                for hh in hhs:
                    r = slice(hh * HD, (hh + 1) * HD)
                    src = bank_o[r, :].rearrange("p (m q) -> p m q", m=NQ)[:, :, hh * HD:(hh + 1) * HD]
                    dst = OT[r, :, j * HD:(j + 1) * HD]
                    op = eng.copy(dst, src) if pe_first else eng.tensor_copy(dst, src)
                op.then_inc(done, 1)

            @block.scalar
            def _(act):
                def z_hi(s):
                    act.wait_ge(pe_T, s + 1)
                    act.copy(zT_hi[:].rearrange("p k c q -> p (k c q)"), bank_misc[:]).then_inc(a_T, 1)

                def x_out(i):
                    act.wait_ge(pe_X, i + 1)
                    act.copy(xnT[:].rearrange("p k q -> p (k q)"), bank_misc[:]).then_inc(a_X, 1)

                def q_hi(i):
                    act.wait_ge(pe_Q, i + 1)
                    need(act, v_Q, i)
                    act.mul(Qp[:], bank_misc[:], SCALE).then_inc(a_Q, 1)

                def spread_hi(i):
                    act.wait_ge(a_Q, i + 1)
                    need(act, pe_S, 4 * BT * i)
                    for hh in range(4):
                        r = slice(hh * HD, (hh + 1) * HD)
                        op = act.copy(Q_hi[r, :, :, r], Qp[r, :].rearrange("p (m b t) -> p m b t", m=NQ, b=BT))
                    op.then_inc(a_Qh, 1)

                def pt_out(s):
                    act.wait_ge(pe_PT, 2 * s + 2)
                    act.copy(PT[:, 1].rearrange("p m q -> p (m q)"), bank_pt[1][:]).then_inc(a_PT, 1)
                    act.wait_ge(pe_PL, s + 1)
                    need(act, g_PL, s)
                    act.copy(pl_parts[:], bank_o[0:LAST_ROWS, 0:P]).then_inc(a_PL, 1)

                def ot_hi(i):
                    act.wait_ge(a_O, BT * i + BT)
                    act.wait_ge(v_O, BT * i + BT)
                    act.copy(OT_hi[:], OT[:]).then_inc(a_OT, 1)

                def o_out(s, i, j):
                    act.wait_ge(pe_O, s + 1)
                    if j == 0:
                        need(act, v_OT, i)
                    own_heads(act, i, j, (0, 1), a_O, True)

                x_out(0)
                q_hi(0)
                z_hi(0)
                spread_hi(0)

                def body(i, first, last):
                    for j in range(BT):
                        s = BT * i + j
                        some = not (first and j == 0)
                        for h in range(2):
                            act.wait_ge(pe_K, 2 * s + h + 1)
                            act.copy(K_hi[:, 2 * h:2 * h + 2, 0:LAST],
                                     bank_kv[h][:].rearrange("p (m q) -> p m q", m=2)).then_inc(a_K, 1)
                        if j == 1 and not first:
                            ot_hi(i - 1)
                        if some:
                            pt_out(s - 1)
                        for c in range(CH):
                            act.wait_ge(pe_V, 2 * s + c + 1)
                            act.copy(V[:, j % 2, c, :], bank_kv[c][:]).then_inc(a_V, 1)
                        if not (last and j == BT - 1):
                            z_hi(s + 1)
                        for m in range(NQ):
                            act.wait_ge(v_mx, 4 * s + m + 1)
                            if m == 0:
                                need(act, pe_PL, s)
                                need(act, v_R, s)
                            act.activation(Pr[:, m, 0:NK], bank_s[m][:, 0:NK], ACT.Exp, bias=nmax[:, m:m + 1],
                                           scale=1.0, accum_out=rsum[:, m:m + 1]).then_inc(a_E, 1)
                        if j == BT - 1 and not last:
                            spread_hi(i + 1)
                        if some:
                            o_out(s - 1, i if j else i - 1, (j - 1) % BT)
                        if j == 1 and not last:
                            x_out(i + 1)
                        if j == 2 and not last:
                            q_hi(i + 1)
                peeled(act, n_tile, body)
                s_end = BT * n_tile
                pt_out(s_end - 1)
                o_out(s_end - 1, n_tile - 1, BT - 1)
                ot_hi(n_tile - 1)

            @block.vector
            def _(dve):
                def z_lo(s):
                    dve.wait_ge(a_T, s + 1)
                    dve.tensor_tensor(zT_lo[:].rearrange("p k c q -> p (k c q)"), bank_misc[:],
                                      zT_hi[:].bitcast(F32).rearrange("p k c q -> p (k c q)"),
                                      ALU.subtract).then_inc(v_T, 1)

                def spread_lo(i):
                    dve.wait_ge(a_Qh, i + 1)
                    for hh in range(4):
                        r = slice(hh * HD, (hh + 1) * HD)
                        op = dve.tensor_tensor(Q_lo[r, :, :, r], Qp[r, :].rearrange("p (m b t) -> p m b t", m=NQ, b=BT),
                                               Q_hi[r, :, :, r].bitcast(F32), ALU.subtract)
                    op.then_inc(v_Q, 1)

                def pt_out(s, i, j):
                    dve.wait_ge(pe_PT, 2 * s + 1)
                    need(dve, pe_O, s)
                    dve.tensor_copy(PT[:, 0].rearrange("p m q -> p (m q)"), bank_pt[0][:]).then_inc(v_PT, 1)
                    dve.wait_ge(vl_got[j], 32 * i + 32)
                    dve.tensor_copy(v_last[:], v_last_in[:, j, :])
                    dve.wait_ge(a_PL, s + 1)
                    low = slice(LO_ROW, LAST_ROWS)
                    dve.tensor_tensor(pl_parts[low, :], bank_o[low, 0:P], pl_parts[low, :].bitcast(F32),
                                      ALU.subtract).then_inc(v_PL, 1)

                def ot_lo(i):
                    dve.wait_ge(a_OT, i + 1)
                    dve.tensor_tensor(OT_lo[:], OT[:], OT_hi[:].bitcast(F32), ALU.subtract).then_inc(v_OT, 1)

                def o_out(s, i, j):
                    dve.wait_ge(pe_O, s + 1)
                    if j == 0:
                        need(dve, v_OT, i)
                    own_heads(dve, i, j, (2, 3), v_O, False)

                def add_residual(i):
                    dve.wait_ge(pe_OP, i + 1)
                    dve.tensor_tensor(x_res[:, i, :], bank_misc[:], x_res[:, i, :], ALU.add).then_inc(v_OP, 1)

                dve.memset(waiter[:], 0.0).then_inc(v_OP, 1)
                z_lo(0)
                spread_lo(0)

                def body(i, first, last):
                    for j in range(BT):
                        s = BT * i + j
                        some = not (first and j == 0)
                        if j == 1 and not last:
                            normalise(dve, i + 1)
                        for h in range(2):
                            dve.wait_ge(a_K, 2 * s + h + 1)
                            dve.tensor_tensor(K_lo[:, 2 * h:2 * h + 2, 0:LAST],
                                              bank_kv[h][:].rearrange("p (m q) -> p m q", m=2),
                                              K_hi[:, 2 * h:2 * h + 2, 0:LAST].bitcast(F32),
                                              ALU.subtract).then_inc(v_K, 1)
                        if j == 1 and not first:
                            ot_lo(i - 1)
                        if some:
                            pt_out(s - 1, i if j else i - 1, (j - 1) % BT)
                        if j == 0 and not last:
                            if first:
                                dve.wait_ge(x_rest, 16)
                            statistics(dve, i + 1)
                        for m in range(NQ):
                            dve.wait_ge(pe_S, 4 * s + m + 1)
                            if m == 0:
                                need(dve, a_E, 4 * s)
                            dve.tensor_reduce(nmax[:, m:m + 1], bank_s[m][:, 0:NK], AX_X, ALU.max,
                                              negate=True).then_inc(v_mx, 1)
                            if m == 1 and not (last and j == BT - 1):
                                z_lo(s + 1)
                        dve.wait_ge(a_E, 4 * s + 4)
                        dve.reciprocal(rinv[:], rsum[:]).then_inc(v_R, 1)
                        dve.wait_ge(v_R, s + 1)
                        need(dve, pe_PL, s)
                        dve.tensor_tensor(p_last[:], Pr[:, :, LAST].unsqueeze(1).to_broadcast([P, LAST_ROWS // NQ, NQ]),
                                          rinv[:].unsqueeze(1).to_broadcast([P, LAST_ROWS // NQ, NQ]), ALU.mult)
                        for m in range(NQ):
                            op = dve.tensor_scalar(Pr[:, m, 0:LAST], Pr[:, m, 0:LAST], rinv[:, m:m + 1], None, ALU.mult)
                        op.then_inc(v_N, 1)
                        if some:
                            o_out(s - 1, i if j else i - 1, (j - 1) % BT)
                        if j == BT - 1 and not last:
                            spread_lo(i + 1)
                        if j == BT - 1 and not first:
                            add_residual(i - 1)
                peeled(dve, n_tile, body)
                s_end = BT * n_tile
                pt_out(s_end - 1, n_tile - 1, BT - 1)
                o_out(s_end - 1, n_tile - 1, BT - 1)
                ot_lo(n_tile - 1)
                add_residual(n_tile - 1)
                dve.wait_ge(v_OP, n_tile + 1)

            @block.gpsimd
            def _(pool):
                def mask_last(s):
                    pool.wait_ge(v_PL, s + 1)
                    need(pool, pe_O, s)
                    pool.tensor_tensor(PL[:], pl_parts[:].bitcast(F32).unsqueeze(1).to_broadcast([LAST_ROWS, NQ, P]),
                                       quad_mask[:], ALU.mult).then_inc(g_PL, 1)

                def body(i, first, last):
                    for j in range(BT):
                        s = BT * i + j
                        need(pool, pe_S, 4 * s)
                        b = i * BT + j
                        pool.tensor_copy(K_hi[:, :, LAST], Kl_hi[:, :, bass.ds(b, 1)].rearrange("p m o -> p (m o)"))
                        pool.tensor_copy(K_lo[:, :, LAST], Kl_lo[:, :, bass.ds(b, 1)].rearrange("p m o -> p (m o)")
                                         ).then_inc(g_K, 1)
                        if not (first and j == 0):
                            mask_last(s - 1)
                        if j == 0 and not last:
                            rstd_of(pool, i + 1)
                peeled(pool, n_tile, body)
                mask_last(BT * n_tile - 1)


class Steps:

    def __init__(self, sem, names):
        self.sem, self.names, self.next = sem, names.split(), 0

    def done(self, op, name):
        assert self.names[self.next] == name, (name, self.names[self.next])
        self.next = (self.next + 1) % len(self.names)
        return op.then_inc(self.sem, 1)

    def wait(self, eng, i, name):
        need(eng, self.sem, len(self.names) * i + self.names.index(name) + 1)


def statistics(dve, steps, i, suffix, x, st6, mv, waiter):
    dve.memset(waiter[:], 0.0)
    steps.done(dve.bn_stats(st6[:], x), "stats" + suffix)
    steps.wait(dve, i, "stats" + suffix)
    dve.memset(waiter[:], 0.0)
    steps.done(dve.bn_aggr(mv[:], st6[:]), "aggr" + suffix)
    steps.wait(dve, i, "aggr" + suffix)
    steps.done(dve.tensor_scalar(mv[:, 1:2], mv[:, 1:2], EPS, None, ALU.add), "eps" + suffix)


def normalise(dve, steps, pool_steps, i, suffix, x, mv, rstd, out):
    pool_steps.wait(dve, i, "rstd" + suffix)
    steps.done(dve.tensor_scalar(out[:], x, mv[:, 0:1], rstd[:], ALU.subtract, ALU.mult), "xn" + suffix)


class SelfAttentionWeights:

    def __init__(self, nc, ctx, wq, w_down, wk_up, wv_up, wo, Wr, rope):
        def sb(name, shape):
            return ctx.enter_context(nc.sbuf_tensor(name, shape, F32))

        def rows(name, w):
            return sb(name, [P, w.shape[0] // P, w.shape[1]])

        self.q, self.down, self.k, self.v, self.o = (rows(*a) for a in (
            ("sa_wq", wq), ("sa_down", w_down), ("sa_wk", wk_up), ("sa_wv", wv_up), ("sa_wo", wo)))
        self.router = rows("sa_wr", Wr)
        self.rope = sb("rope_t", [P, 2, rope.shape[1] // 2])
        self.got = ctx.enter_context(nc.semaphore("sa_w_got"))
        self.loads = [(dst, src.rearrange("(k p) c -> p k c", p=P)) for dst, src in (
            (self.q, wq), (self.down, w_down), (self.k, wk_up), (self.v, wv_up), (self.o, wo), (self.router, Wr))]
        self.loads.append((self.rope, rope.rearrange("p (a d) -> p a d", a=2)))

    def load(self, sp):
        for dst, src in self.loads:
            sp.dma_start(dst[:], src).then_inc(self.got, 16)

    def wait(self, eng):
        eng.wait_ge(self.got, 16 * len(self.loads))


def self_attention_and_routing(nc, w, zeroed, ahead, finish, x_res, ident, xs_dram,
                               gate_w, row_all, pick_all, count, region, Tlen):
    n_tile, C = x_res.shape[1], x_res.shape[2]
    E = w.router.shape[2]
    L = w.down.shape[2]
    KC, KL, NQ, HD, BT = C // P, L // P, C // P, 32, P // Tlen
    NH = C // HD
    SCALE = HD ** -0.5
    assert HD == Tlen

    with ExitStack() as ctx:
        def sb(name, shape, dt=F32):
            return ctx.enter_context(nc.sbuf_tensor(name, shape, dt))

        def steps(name, names):
            return Steps(ctx.enter_context(nc.semaphore(name)), names)

        Wdown, Wg, rope_t = w.down, w.router, w.rope
        Wq_hi, Wq_lo = sb("sa_wq_hi", [P, KC, C], F32R), sb("sa_wq_lo", [P, KC, C], F32R)
        Wk_hi, Wk_lo = sb("sa_wk_hi", [P, KL, C], F32R), sb("sa_wk_lo", [P, KL, C], F32R)
        Wv_hi, Wv_lo = sb("sa_wv_hi", [P, KL, C], F32R), sb("sa_wv_lo", [P, KL, C], F32R)
        Wo_hi, Wo_lo = sb("sa_wo_hi", [P, KC, C], F32R), sb("sa_wo_lo", [P, KC, C], F32R)
        split_weights = [(w.k, Wk_hi, Wk_lo), (w.q, Wq_hi, Wq_lo), (w.v, Wv_hi, Wv_lo), (w.o, Wo_hi, Wo_lo)]
        below = sb("below", [P, P])
        ones = sb("ones", [P, P])
        rank8 = sb("rank8", [P, E])
        start8 = sb("start8", [P, E])
        mhalf = sb("sa_mhalf", [P, 1])
        xn, xnT = sb("sa_xn", [P, C]), sb("sa_xnT", [P, KC, P])
        xT_hi, xT_lo = sb("sa_xT_hi", [P, KC, P], F32R), sb("sa_xT_lo", [P, KC, P], F32R)
        latT_hi, latT_lo = sb("latT_hi", [P, KL, P], F32R), sb("latT_lo", [P, KL, P], F32R)
        qraw, kraw = sb("qraw", [P, C]), sb("kraw", [P, C])
        part_cos, part_sin = sb("part_cos", [P, C]), sb("part_sin", [P, C])
        qr, kr = sb("qr", [P, C]), sb("kr", [P, C])
        Vt = sb("Vt", [P, C])
        Qd = sb("Qd", [P, NQ, BT, P])
        KT = sb("sa_KT", [P, NQ, P])
        Ex, Pm = sb("Ex", [P, NQ * BT, Tlen]), sb("Pm", [P, NQ, P])
        mx, sm, ri = sb("mx", [P, NQ * BT]), sb("sm", [P, NQ * BT]), sb("ri", [P, NQ * BT])
        PTd = sb("PTd", [P, NQ, BT, P])
        OT_hi, OT_lo = sb("sa_OT_hi", [P, NQ, P], F32R), sb("sa_OT_lo", [P, NQ, P], F32R)
        xn2, xn2T = sb("xn2", [P, C]), sb("xn2T", [P, KC, P])
        st6, mv, rstd = sb("sa_st6", [P, 6]), sb("sa_mv", [P, 2]), sb("sa_rstd", [P, 1])
        st6b, mvb, rstdb = sb("sb_st6", [P, 6]), sb("sb_mv", [P, 2]), sb("sb_rstd", [P, 1])
        waiter, carrier = sb("sa_waiter", [P, 1]), sb("sa_carrier", [P, 1])
        lg, cand = sb("lg", [P, E]), sb("cand", [P, E])
        oh = sb("oh", [P, 2, E])
        best, top = sb("best", [P, 2]), sb("top", [P, 2])
        both, dest = sb("both", [P, E]), sb("dest", [P, E])
        prod, posf = sb("prod", [P, 2, E]), sb("posf", [P, 2])
        idx = sb("idx", [P, 2], U32)
        dl, ex = sb("dl", [P, 1]), sb("ex", [P, 2])
        bank = [ctx.enter_context(nc.psum_tensor(f"sa_bank{i}", [P, 512], F32)) for i in range(8)]

        c_set = ctx.enter_context(nc.semaphore("sa_c_set"))
        w_hi, w_lo = ctx.enter_context(nc.semaphore("sa_w_hi")), ctx.enter_context(nc.semaphore("sa_w_lo"))
        sent = ctx.enter_context(nc.semaphore("rows_sent"))
        pX, aX, vX = steps("pX", "XT"), steps("aX", "xnT hi"), steps("vX", "lo")
        pA, aA, aV, vA = steps("pA", "lat K Q V"), steps("aA", "latT kraw qraw"), steps("aV", "V"), steps("vA", "latT")
        vL, gL = steps("vL", "stats aggr eps xn"), steps("gL", "rstd")
        gA = steps("gA", "k1 k2 kr q1 q2 qr")
        pB, aB, vB = steps("pB", "QT KT S"), steps("aB", "q0 kt q exp"), steps("vB", "q0 q mx sub sum rec prob")
        pC, pO, pD = steps("pC", "PT PV0 PV1 PV2 PV3"), steps("pO", "OP"), steps("pD", "XT2 G R")
        aC, aD = steps("aC", "pt0 pt " + " ".join(f"half{m} ov{m}" for m in range(NQ))), steps("aD", "xt2 ew")
        vC = steps("vC", "pt0 pt ov0 ov1 ov2 ov3 add")
        vD = steps("vD", "stats2 aggr2 eps2 xn2 lg top0 eq0 best0 oh0 less top1 eq1 best1 oh1 both dl e1 w0 w1 "
                         "dest prod pos idx cnt")
        gD = steps("gD", "rstd2")

        def has(i, k):
            return not isinstance(i, int) or i + k < n_tile

        def tiles(eng, body):
            for i in range(2):
                body(i)
            with eng.Fori(2, n_tile - 2) as i:
                body(i)
            for i in range(n_tile - 2, n_tile):
                body(i)

        bank_pv = [bank[b] for b in (6, 7, 4, 5)]

        def flat(t):
            return t[:].rearrange("p k c -> p (k c)")

        with nc.Block() as block:
            @block.sync
            def _(sp):
                ahead(sp)

            @block.tensor
            def _(pe):
                def A_turn(i):
                    vL.wait(pe, i, "xn")
                    aX.wait(pe, i - 1, "xnT")
                    aD.wait(pe, i - 3, "xt2")
                    for k in range(KC):
                        mm = pe.transpose(bank[0][:, k * P:(k + 1) * P], xn[:, k * P:(k + 1) * P], ident[:])
                    pX.done(mm, "XT")

                def A_q(i, half):
                    if half == 0:
                        aX.wait(pe, i, "hi")
                        vX.wait(pe, i, "lo")
                        vC.wait(pe, i - 2, "add")
                    for k in range(half * KC // 2, (half + 1) * KC // 2):
                        mm = product(pe, bank[1][:], (xT_hi[:, k, :], xT_lo[:, k, :]), (Wq_hi[:, k, :], Wq_lo[:, k, :]),
                                     k == 0, k == KC - 1)
                    if half == 1:
                        pA.done(mm, "Q")

                def A_lat(i):
                    aX.wait(pe, i, "xnT")
                    aA.wait(pe, i - 1, "kraw")
                    vD.wait(pe, i - 3, "cnt")
                    for m in range(KL):
                        for k in range(KC):
                            mm = pe.matmul(bank[2][:, m * P:(m + 1) * P], Wdown[:, k, m * P:(m + 1) * P],
                                           xnT[:, k, :], start=(k == 0), stop=(k == KC - 1))
                    pA.done(mm, "lat")

                def A_up(i, b, hi, lo, name):
                    for k in range(KL):
                        mm = product(pe, bank[b][:], (latT_hi[:, k, :], latT_lo[:, k, :]), (hi[:, k, :], lo[:, k, :]),
                                     k == 0, k == KL - 1)
                    pA.done(mm, name)

                def A_k(i):
                    aA.wait(pe, i, "latT")
                    vA.wait(pe, i, "latT")
                    A_up(i, 2, Wk_hi, Wk_lo, "K")

                def A_v(i):
                    aV.wait(pe, i - 1, "V")
                    vD.wait(pe, i - 2, "lg")
                    A_up(i, 3, Wv_hi, Wv_lo, "V")

                def C_turn(i):
                    vD.wait(pe, i, "xn2")
                    if has(i, 2):
                        aX.wait(pe, i + 2, "xnT")
                    for k in range(KC):
                        mm = pe.transpose(bank[0][:, k * P:(k + 1) * P], xn2[:, k * P:(k + 1) * P], ident[:])
                    pD.done(mm, "XT2")

                def C_gate(i):
                    aD.wait(pe, i, "xt2")
                    if has(i, 1):
                        aV.wait(pe, i + 1, "V")
                    for k in range(KC):
                        mm = pe.matmul(bank[3][:, 0:E], xn2T[:, k, :], Wg[:, k, :], start=(k == 0), stop=(k == KC - 1))
                    pD.done(mm, "G")

                def C_rank(i):
                    if has(i, 2):
                        aA.wait(pe, i + 2, "kraw")
                    vD.wait(pe, i, "both")
                    pe.matmul(bank[2][:, 0:E], below[:], both[:], start=True, stop=True)
                    pD.done(pe.matmul(bank[2][:, E:2 * E], ones[:], both[:], start=True, stop=True), "R")

                A_turn(0)
                A_lat(0)
                A_turn(1)
                pe.wait_ge(w_lo, 1)
                A_k(0)
                pe.wait_ge(w_lo, 2)
                A_q(0, 0)
                A_q(0, 1)
                pe.wait_ge(w_lo, 3)
                A_v(0)

                def body(i):
                    behind = not (isinstance(i, int) and i == 0)
                    gA.wait(pe, i, "qr")
                    vC.wait(pe, i - 1, "ov2")
                    for m in range(NQ):
                        mm = pe.transpose(bank[4][:, m * P:(m + 1) * P], qr[:, m * P:(m + 1) * P], ident[:])
                    pB.done(mm, "QT")
                    gA.wait(pe, i, "kr")
                    vC.wait(pe, i - 1, "ov3")
                    for m in range(NQ):
                        mm = pe.transpose(bank[5][:, m * P:(m + 1) * P], kr[:, m * P:(m + 1) * P], ident[:])
                    pB.done(mm, "KT")
                    if has(i, 1):
                        A_q(i + 1, 0)
                    for m in range(NQ):
                        if m % 2 == 0:
                            aB.wait(pe, i, "q" if m else "kt")
                            vB.wait(pe, i, "q" if m else "q0")
                        for b in range(BT):
                            at = (m * BT + b) * Tlen
                            mm = pe.matmul(bank[6][:, at:at + Tlen], Qd[:, m, b, :],
                                           KT[:, m, b * Tlen:(b + 1) * Tlen], start=True, stop=True)
                    pB.done(mm, "S")
                    if behind:
                        C_turn(i - 1)
                    if has(i, 1):
                        A_lat(i + 1)
                    if behind:
                        C_gate(i - 1)
                    if has(i, 2):
                        A_turn(i + 2)
                    if has(i, 1):
                        A_k(i + 1)
                    vB.wait(pe, i, "prob")
                    for m in range(NQ):
                        mm = pe.transpose(bank[5][:, m * P:(m + 1) * P], Pm[:, m, :], ident[:])
                    pC.done(mm, "PT")
                    if has(i, 1):
                        A_q(i + 1, 1)
                    aV.wait(pe, i, "V")
                    for m in range(NQ):
                        if m % 2 == 0:
                            aC.wait(pe, i, "pt" if m else "pt0")
                            vC.wait(pe, i, "pt" if m else "pt0")
                        mm = pe.matmul(bank_pv[m][:], Vt[:, m * P:(m + 1) * P],
                                       PTd[:, m].rearrange("p b q -> p (b q)"), start=True, stop=True)
                        pC.done(mm, f"PV{m}")
                    if has(i, 1):
                        A_v(i + 1)
                    if behind:
                        C_rank(i - 1)
                    vC.wait(pe, i, "ov3")
                    if has(i, 1):
                        aA.wait(pe, i + 1, "qraw")
                    if isinstance(i, int) and i == 0:
                        pe.wait_ge(w_lo, 4)
                    for m in range(NQ):
                        mm = product(pe, bank[1][:], (OT_hi[:, m, :], OT_lo[:, m, :]), (Wo_hi[:, m, :], Wo_lo[:, m, :]),
                                     m == 0, m == NQ - 1)
                    pO.done(mm, "OP")
                tiles(pe, body)
                C_turn(n_tile - 1)
                C_gate(n_tile - 1)
                C_rank(n_tile - 1)

            def own(copy, dst, src, parts):
                for q in parts:
                    op = copy(dst(q), src(q))
                return op

            rows = [slice(q * HD, (q + 1) * HD) for q in range(4)]

            halves = (slice(0, NQ // 2), slice(NQ // 2, NQ))

            def split_q(copy, parts, ms):
                return own(copy, lambda q: Qd[rows[q], ms, :, rows[q]],
                           lambda q: bank[4][rows[q], :].rearrange("p (m b t) -> p m b t", m=NQ, b=BT)[:, ms], parts)

            def split_p(copy, parts, ms):
                return own(copy, lambda q: PTd[rows[q], ms, q, :],
                           lambda q: bank[5][rows[q], :].rearrange("p (m q) -> p m q", m=NQ)[:, ms], parts)

            def head_out(t, m, q):
                return t[rows[q], m, :].rearrange("p (b t) -> p b t", b=BT)

            def head_in(m, q):
                return bank_pv[m][rows[q], :].rearrange("p (b q) -> p b q", b=BT)[:, :, rows[q]]

            @block.scalar
            def _(act):
                def out(b, n=C):
                    return bank[b][:, 0:n].rearrange("p (k q) -> p k q", q=P)

                def weights_hi(n):
                    raw, hi, _lo = split_weights[n]
                    act.copy(flat(hi), flat(raw)).then_inc(w_hi, 1)

                def A_xnT(i):
                    pX.wait(act, i, "XT")
                    pA.wait(act, i - 1, "lat")
                    vX.wait(act, i - 1, "lo")
                    aX.done(act.copy(xnT[:], out(0)), "xnT")

                def A_hi(i):
                    aX.wait(act, i, "xnT")
                    pA.wait(act, i - 1, "Q")
                    aX.done(act.copy(xT_hi[:], xnT[:]), "hi")

                def A_qraw(i):
                    pA.wait(act, i, "Q")
                    gA.wait(act, i - 1, "q2")
                    aA.done(act.copy(qraw[:], bank[1][:]), "qraw")

                def A_lat(i):
                    pA.wait(act, i, "lat")
                    pA.wait(act, i - 1, "V")
                    aA.done(act.copy(latT_hi[:], out(2, L)), "latT")

                def A_kraw(i):
                    pA.wait(act, i, "K")
                    gA.wait(act, i - 1, "k2")
                    aA.done(act.copy(kraw[:], bank[2][:]), "kraw")

                def A_v(i):
                    pA.wait(act, i, "V")
                    pC.wait(act, i - 1, "PV3")
                    aV.done(act.copy(Vt[:], bank[3][:]), "V")

                def D_turn(i):
                    pD.wait(act, i, "XT2")
                    aD.done(act.copy(xn2T[:], out(0)), "xt2")

                def D_weight(i):
                    vD.wait(act, i, "dl")
                    aD.done(act.activation(ex[:, 0:1], dl[:], ACT.Exp), "ew")

                w.wait(act)
                A_xnT(0)
                weights_hi(0)
                A_lat(0)
                A_hi(0)
                weights_hi(1)
                A_xnT(1)
                A_kraw(0)
                weights_hi(2)
                A_qraw(0)
                A_v(0)
                A_hi(1)
                weights_hi(3)
                act.wait_ge(c_set, 8)

                def body(i):
                    behind = not (isinstance(i, int) and i == 0)
                    pB.wait(act, i, "QT")
                    aB.done(split_q(act.copy, (0, 1, 2), halves[0]), "q0")
                    pB.wait(act, i, "KT")
                    aB.done(act.copy(KT[:], out(5)), "kt")
                    aB.done(split_q(act.copy, (0, 1, 2), halves[1]), "q")
                    if behind:
                        D_turn(i - 1)
                    vB.wait(act, i, "sub")
                    aB.done(act.activation(Ex[:], Ex[:], ACT.Exp, scale=SCALE), "exp")
                    if has(i, 1):
                        A_lat(i + 1)
                    if has(i, 2):
                        A_xnT(i + 2)
                    if has(i, 1):
                        A_kraw(i + 1)
                    pC.wait(act, i, "PT")
                    aC.done(split_p(act.copy, (0, 1), halves[0]), "pt0")
                    aC.done(split_p(act.copy, (0, 1), halves[1]), "pt")
                    if has(i, 1):
                        A_qraw(i + 1)
                    for m in range(NQ):
                        pC.wait(act, i, f"PV{m}")
                        if m == 0:
                            pO.wait(act, i - 1, "OP")
                        for half in range(2):
                            aC.done(own(act.copy, lambda q: head_out(OT_hi, m, q), lambda q: head_in(m, q),
                                        (2 * half, 2 * half + 1)), f"ov{m}" if half else f"half{m}")
                        if m == 1 and behind:
                            D_weight(i - 1)
                    if has(i, 2):
                        A_hi(i + 2)
                    if has(i, 1):
                        A_v(i + 1)
                tiles(act, body)
                D_turn(n_tile - 1)
                D_weight(n_tile - 1)

            @block.vector
            def _(dve):
                def weights_lo(n):
                    raw, hi, lo = split_weights[n]
                    dve.wait_ge(w_hi, n + 1)
                    dve.tensor_tensor(flat(lo), flat(raw), flat(hi).bitcast(F32), ALU.subtract).then_inc(w_lo, 1)

                def A_stats(i):
                    statistics(dve, vL, i, "", x_res[:, i, :], st6, mv, waiter)

                def A_norm(i):
                    pX.wait(dve, i - 1, "XT")
                    normalise(dve, vL, gL, i, "", x_res[:, i, :], mv, rstd, xn)

                def A_lat(i):
                    aA.wait(dve, i, "latT")
                    vA.done(dve.tensor_tensor(latT_lo[:], bank[2][:, 0:L].rearrange("p (k q) -> p k q", q=P),
                                              latT_hi[:].bitcast(F32), ALU.subtract), "latT")

                def A_lo(i):
                    aX.wait(dve, i, "hi")
                    vX.done(dve.tensor_tensor(xT_lo[:], xnT[:], xT_hi[:].bitcast(F32), ALU.subtract), "lo")

                def D_stats(i):
                    statistics(dve, vD, i, "2", x_res[:, i, :], st6b, mvb, waiter)

                def D_norm(i):
                    need(dve, sent, 32 * i)
                    normalise(dve, vD, gD, i, "2", x_res[:, i, :], mvb, rstdb, xn2)

                def D_choose(i, which):
                    if 0 in which:
                        pD.wait(dve, i, "G")
                        vD.done(dve.tensor_copy(lg[:], bank[3][:, 0:E]), "lg")
                    for n in which:
                        vD.wait(dve, i, "less" if n else "lg")
                        vD.done(dve.tensor_reduce(top[:, n:n + 1], lg[:], AX_X, ALU.max), f"top{n}")
                        vD.wait(dve, i, f"top{n}")
                        vD.done(dve.scalar_tensor_tensor(cand[:], lg[:], top[:, n:n + 1], rank8[:],
                                                         ALU.is_equal, ALU.mult), f"eq{n}")
                        vD.wait(dve, i, f"eq{n}")
                        vD.done(dve.tensor_reduce(best[:, n:n + 1], cand[:], AX_X, ALU.max), f"best{n}")
                        vD.wait(dve, i, f"best{n}")
                        vD.done(dve.tensor_scalar(oh[:, n, :], rank8[:], best[:, n:n + 1], None, ALU.is_equal), f"oh{n}")
                        vD.wait(dve, i, f"oh{n}")
                        if n == 0:
                            vD.done(dve.scalar_tensor_tensor(lg[:], oh[:, 0, :], -3e38, lg[:], ALU.mult, ALU.add), "less")
                    if 1 in which:
                        vD.done(dve.tensor_tensor(both[:], oh[:, 0, :], oh[:, 1, :], ALU.add), "both")
                        vD.done(dve.tensor_tensor(dl[:], top[:, 1:2], top[:, 0:1], ALU.subtract), "dl")

                def D_place(i):
                    aD.wait(dve, i, "ew")
                    vD.done(dve.tensor_scalar(ex[:, 1:2], ex[:, 0:1], 1.0, None, ALU.add), "e1")
                    vD.wait(dve, i, "e1")
                    vD.done(dve.reciprocal(gate_w[:, i, 0:1], ex[:, 1:2]), "w0")
                    vD.wait(dve, i, "w0")
                    vD.done(dve.tensor_tensor(gate_w[:, i, 1:2], ex[:, 0:1], gate_w[:, i, 0:1], ALU.mult), "w1")
                    pD.wait(dve, i, "R")
                    vD.done(dve.tensor_tensor(dest[:], bank[2][:, 0:E], count[:], ALU.add), "dest")
                    vD.wait(dve, i, "dest")
                    vD.done(dve.tensor_tensor(prod[:], oh[:], dest[:].unsqueeze(1).to_broadcast([P, 2, E]), ALU.mult), "prod")
                    vD.wait(dve, i, "prod")
                    vD.done(dve.tensor_reduce(posf[:], prod[:], AX_X, ALU.add), "pos")
                    vD.wait(dve, i, "pos")
                    need(dve, sent, 32 * i)
                    dve.tensor_copy(row_all[:, i, :], posf[:])
                    dve.tensor_copy(pick_all[:, i, :], oh[:].rearrange("p n e -> p (n e)"))
                    vD.done(dve.tensor_copy(idx[:], posf[:]), "idx")
                    vD.done(dve.tensor_tensor(count[:], bank[2][:, E:2 * E], count[:], ALU.add), "cnt")
                    vD.wait(dve, i, "cnt")

                A_stats(0)
                A_norm(0)
                w.wait(dve)
                A_stats(1)
                A_norm(1)
                weights_lo(0)
                A_lat(0)
                A_lo(0)
                weights_lo(1)
                weights_lo(2)
                A_lo(1)
                weights_lo(3)
                dve.wait_ge(c_set, 8)

                def body(i):
                    behind = not (isinstance(i, int) and i == 0)
                    pB.wait(dve, i, "QT")
                    vB.done(split_q(dve.tensor_copy, (3,), halves[0]), "q0")
                    vB.done(split_q(dve.tensor_copy, (3,), halves[1]), "q")
                    if behind:
                        D_stats(i - 1)
                    if has(i, 2):
                        A_stats(i + 2)
                    if behind:
                        D_norm(i - 1)
                    pB.wait(dve, i, "S")
                    group = "p (g k) -> p g k"
                    vB.done(dve.tensor_reduce(mx[:], bank[6][:].rearrange(group, k=Tlen), AX_X, ALU.max), "mx")
                    vB.wait(dve, i, "mx")
                    vB.wait(dve, i - 1, "prob")
                    vB.done(dve.tensor_tensor(Ex[:], bank[6][:].rearrange(group, k=Tlen),
                                              mx[:].unsqueeze(2).to_broadcast([P, NQ * BT, Tlen]), ALU.subtract), "sub")
                    if has(i, 2):
                        A_norm(i + 2)
                    aB.wait(dve, i, "exp")
                    vB.done(dve.tensor_reduce(sm[:], Ex[:], AX_X, ALU.add), "sum")
                    if has(i, 1):
                        A_lat(i + 1)
                    vB.wait(dve, i, "sum")
                    vB.done(dve.reciprocal(ri[:], sm[:]), "rec")
                    vB.wait(dve, i, "rec")
                    vB.done(dve.tensor_tensor(Pm[:].rearrange("p m (b k) -> p (m b) k", k=Tlen), Ex[:],
                                              ri[:].unsqueeze(2).to_broadcast([P, NQ * BT, Tlen]), ALU.mult), "prob")
                    if behind:
                        D_choose(i - 1, (0,))
                    pC.wait(dve, i, "PT")
                    vC.done(split_p(dve.tensor_copy, (2, 3), halves[0]), "pt0")
                    vC.done(split_p(dve.tensor_copy, (2, 3), halves[1]), "pt")
                    if behind:
                        D_choose(i - 1, (1,))
                    for m in range(NQ):
                        for q in range(4):
                            if q % 2 == 0:
                                aC.wait(dve, i, f"ov{m}" if q else f"half{m}")
                            op = dve.tensor_tensor(head_out(OT_lo, m, q), head_in(m, q), head_out(OT_hi, m, q).bitcast(F32),
                                                   ALU.subtract)
                        vC.done(op, f"ov{m}")
                    if behind:
                        D_place(i - 1)
                    if has(i, 2):
                        A_lo(i + 2)
                    pO.wait(dve, i, "OP")
                    vC.done(dve.tensor_tensor(x_res[:, i, :], bank[1][:], x_res[:, i, :], ALU.add), "add")
                    vC.wait(dve, i, "add")
                tiles(dve, body)
                D_stats(n_tile - 1)
                D_norm(n_tile - 1)
                D_choose(n_tile - 1, (0, 1))
                D_place(n_tile - 1)
                finish(dve)

            @block.gpsimd
            def _(pool):
                pool.memset(mhalf[:], -0.5).then_inc(c_set, 1)
                pool.memset(ones[:], 1.0).then_inc(c_set, 1)
                pool.wait_ge(c_set, 2)

                def power(steps_in, steps_out, i, suffix, mv_, rstd_):
                    steps_in.wait(pool, i, "eps" + suffix)
                    steps_in.wait(pool, i - 1, "xn" + suffix)
                    steps_out.done(pool.tensor_tensor(rstd_[:], mv_[:, 1:2], mhalf[:], ALU.pow), "rstd" + suffix)

                def rotate(i, name, src, out, out_name, used):
                    aA.wait(pool, i, name + "raw")
                    if name == "k":
                        gA.wait(pool, i - 1, "qr")
                    else:
                        gA.wait(pool, i, "kr")
                    heads = "p (h d) -> p h d"
                    gA.done(pool.tensor_tensor(part_cos[:].rearrange(heads, h=NH), src[:].rearrange(heads, h=NH),
                                               rope_t[:, 0, :].unsqueeze(1).to_broadcast([P, NH, HD]), ALU.mult), name + "1")
                    pair = "p (h f e) -> p h f e"
                    for e in range(2):
                        op = pool.tensor_tensor(
                            part_sin[:].rearrange(pair, h=NH, e=2)[:, :, :, e],
                            src[:].rearrange(pair, h=NH, e=2)[:, :, :, 1 - e],
                            rope_t[:, 1, :].rearrange("p (f e) -> p f e", e=2)[:, :, e].unsqueeze(1)
                            .to_broadcast([P, NH, HD // 2]), ALU.mult)
                    gA.done(op, name + "2")
                    gA.wait(pool, i, name + "2")
                    pB.wait(pool, i - 1, used)
                    gA.done(pool.tensor_tensor(out[:], part_cos[:], part_sin[:], ALU.add), out_name)

                def send(i):
                    vD.wait(pool, i, "idx")
                    pool.tensor_tensor(carrier[:], mhalf[:], mhalf[:], ALU.add)
                    for n in range(2):
                        pool.indirect_dma_start(xs_dram, bass.IndirectOffsetOnAxis(ap=idx[:, n:n + 1], axis=0),
                                                xn2[:], None).then_inc(sent, 16)

                power(vL, gL, 0, "", mv, rstd)
                power(vL, gL, 1, "", mv, rstd)
                pool.memset(Qd[:], 0.0).then_inc(c_set, 1)
                pool.memset(PTd[:], 0.0).then_inc(c_set, 1)
                pool.iota(rank8[:], pattern=[[-1, E]], base=E, channel_multiplier=0,
                          allow_small_or_imprecise_dtypes=True).then_inc(c_set, 1)
                pool.iota(start8[:], pattern=[[region, E]], base=0, channel_multiplier=0,
                          allow_small_or_imprecise_dtypes=True).then_inc(c_set, 1)
                pool.wait_ge(c_set, 6)
                pool.tensor_copy(count[:], start8[:]).then_inc(c_set, 1)
                pool.affine_select(out=below[:], in_=ones[:], compare_op=ALU.is_ge, fill=0.0, base=-1,
                                   pattern=[[1, P]], channel_multiplier=-1).then_inc(c_set, 1)
                w.wait(pool)
                zeroed(pool)
                rotate(0, "k", kraw, kr, "kr", "KT")
                rotate(0, "q", qraw, qr, "qr", "QT")
                pool.wait_ge(c_set, 8)

                def body(i):
                    if not (isinstance(i, int) and i == 0):
                        power(vD, gD, i - 1, "2", mvb, rstdb)
                    if has(i, 2):
                        power(vL, gL, i + 2, "", mv, rstd)
                    if has(i, 1):
                        rotate(i + 1, "k", kraw, kr, "kr", "KT")
                        rotate(i + 1, "q", qraw, qr, "qr", "QT")
                    if not (isinstance(i, int) and i == 0):
                        send(i - 1)
                tiles(pool, body)
                power(vD, gD, n_tile - 1, "2", mvb, rstdb)
                send(n_tile - 1)
                pool.wait_ge(sent, 32 * n_tile)


class TileTable:

    def __init__(self, nc, ctx, E, n_tile, n_work, rows, region, most):
        def sb(name, shape, dt=F32):
            return ctx.enter_context(nc.sbuf_tensor(name, shape, dt))
        self.E, self.n_work, self.rows, self.region = E, n_work, rows, region
        self.n_step = n_step = most // rows
        self.table = sb("table", [1, 2, n_work], I32)
        self.pos = [sb(f"pos{n}", [P, n_tile], U32) for n in range(2)]
        self.weight = [sb(f"weight{n}", [P, n_tile]) for n in range(2)]
        self.start = sb("t_start", [P, E])
        self.level = sb("t_level", [P, n_step])
        self.upto = sb("t_upto", [P, E, E])
        self.ks = sb("t_ks", [P, n_work])
        self.const = ctx.enter_context(nc.semaphore("t_const"))
        self.v = ctx.enter_context(nc.semaphore("t_vector"))

    def constants(self, pool):
        cs, E = self.const, self.E
        imprecise = dict(allow_small_or_imprecise_dtypes=True)
        pool.iota(self.start[:], pattern=[[self.region, E]], base=0, channel_multiplier=0, **imprecise).then_inc(cs, 1)
        pool.iota(self.level[:], pattern=[[self.rows, self.n_step]], base=0, channel_multiplier=0, **imprecise).then_inc(cs, 1)
        pool.iota(self.ks[:], pattern=[[1, self.n_work]], base=0, channel_multiplier=0, **imprecise).then_inc(cs, 1)
        pool.memset(self.upto[:], 1.0).then_inc(cs, 1)
        pool.wait_ge(cs, 4)
        pool.affine_select(out=self.upto[:], in_=self.upto[:], compare_op=ALU.is_ge, fill=0.0, base=0,
                           pattern=[[1, E], [-1, E]], channel_multiplier=0).then_inc(cs, 1)

    def scratch(self, nc, ctx, n_pick):
        def sb(name, shape):
            return ctx.enter_context(nc.sbuf_tensor(name, shape, F32))
        E, n_work = self.E, self.n_work
        self.n_row, self.n_t, self.incl, self.shift = (sb(n, [P, E]) for n in ("t_nrow", "t_nt", "t_incl", "t_shift"))
        self.cmp, self.trip = sb("t_cmp", [P, E, self.n_step]), sb("t_trip", [P, E, E])
        self.past, self.pastv = sb("t_past", [P, n_work, E]), sb("t_pastv", [P, n_work, E])
        self.ek, self.first, self.used, self.d1, self.d2, self.d3 = (
            sb(n, [P, n_work]) for n in ("t_ek", "t_first", "t_used", "t_d1", "t_d2", "t_d3"))
        self.moved, self.move = sb("t_moved", [P, n_pick, E]), sb("t_move", [P, n_pick])
        self.posf, self.less, self.share = (sb(n, [P, n_pick // 2, 2]) for n in ("t_posf", "t_less", "t_share"))

    def chain(self, dve, op):
        self.n_done += 1
        op.then_inc(self.v, 1)
        dve.wait_ge(self.v, self.n_done)

    def fill(self, dve, count):
        self.n_done = 0
        E, n_work, n_step = self.E, self.n_work, self.n_step
        n_row, n_t, incl, cmp, trip = self.n_row, self.n_t, self.incl, self.cmp, self.trip
        past, pastv, ek, first, used = self.past, self.pastv, self.ek, self.first, self.used
        d1, d2, d3, ks = self.d1, self.d2, self.d3, self.ks

        def chain(op):
            self.chain(dve, op)

        def each_e(t, m):
            return t[:].unsqueeze(1).to_broadcast([P, m, E])

        dve.wait_ge(self.const, 5)
        chain(dve.tensor_tensor(n_row[:], count[:], self.start[:], ALU.subtract))
        chain(dve.tensor_tensor(cmp[:], n_row[:].unsqueeze(2).to_broadcast([P, E, n_step]),
                                self.level[:].unsqueeze(1).to_broadcast([P, E, n_step]), ALU.is_gt))
        chain(dve.tensor_reduce(n_t[:], cmp[:], AX_X, ALU.add))
        chain(dve.tensor_scalar(n_t[:, 0:1], n_t[:, 0:1], 1.0, None, ALU.max))
        chain(dve.tensor_tensor(trip[:], each_e(n_t, E), self.upto[:], ALU.mult))
        chain(dve.tensor_reduce(incl[:], trip[:], AX_X, ALU.add))
        chain(dve.tensor_tensor(past[:], each_e(incl, n_work),
                                ks[:].unsqueeze(2).to_broadcast([P, n_work, E]), ALU.is_le))
        chain(dve.tensor_reduce(ek[:], past[:], AX_X, ALU.add))
        chain(dve.tensor_tensor(pastv[:], past[:], each_e(incl, n_work), ALU.mult))
        chain(dve.tensor_reduce(first[:], pastv[:], AX_X, ALU.max))
        chain(dve.tensor_scalar(used[:], ek[:], float(E), None, ALU.is_lt))
        chain(dve.tensor_tensor(d1[:], ks[:], first[:], ALU.subtract))
        chain(dve.tensor_tensor(d2[:], d1[:], used[:], ALU.mult))
        chain(dve.tensor_scalar(d1[:], d2[:], float(self.rows), None, ALU.mult))
        chain(dve.scalar_tensor_tensor(d3[:], ek[:], float(self.region), d1[:], ALU.mult, ALU.add))
        chain(dve.tensor_copy(self.table[:, 1, :], d3[0:1, :]))
        chain(dve.tensor_scalar(d1[:], ek[:], float(E - 1), None, ALU.min))
        chain(dve.tensor_copy(self.table[:, 0, :], d1[0:1, :]))

    def find_rows(self, dve, row_all, pick_all, gate_w):
        E, n_t, incl, shift, moved, move = self.E, self.n_t, self.incl, self.shift, self.moved, self.move
        posf, less, share, n_pick = self.posf, self.less, self.share, pick_all.shape[1] * 2

        def chain(op):
            self.chain(dve, op)

        chain(dve.tensor_tensor(shift[:], incl[:], n_t[:], ALU.subtract))
        chain(dve.tensor_scalar(shift[:], shift[:], float(self.rows), None, ALU.mult))
        chain(dve.tensor_tensor(shift[:], shift[:], self.start[:], ALU.subtract))
        chain(dve.tensor_tensor(moved[:], pick_all[:].rearrange("p i (n e) -> p (i n) e", e=E),
                                shift[:].unsqueeze(1).to_broadcast([P, n_pick, E]), ALU.mult))
        chain(dve.tensor_reduce(move[:], moved[:], AX_X, ALU.add))
        chain(dve.tensor_tensor(posf[:].rearrange("p i n -> p (i n)"),
                                row_all[:].rearrange("p i n -> p (i n)"), move[:], ALU.add))
        chain(dve.tensor_tensor(self.pos[0][:], posf[:, :, 0], posf[:, :, 1], ALU.min))
        chain(dve.tensor_tensor(self.pos[1][:], posf[:, :, 0], posf[:, :, 1], ALU.max))
        for n in range(2):
            chain(dve.tensor_tensor(less[:, :, n], posf[:, :, n], posf[:, :, 1 - n], ALU.is_lt))
        for late in range(2):
            for n in range(2):
                chain(dve.tensor_tensor(share[:, :, n], gate_w[:, :, n], less[:, :, n ^ late], ALU.mult))
            chain(dve.tensor_reduce(self.weight[late][:], share[:], AX_X, ALU.add))


class WeightSlot:

    def __init__(self, nc, ctx, c, C, pair):
        self.c, self.pair = c, pair
        self.w13 = ctx.enter_context(nc.sbuf_tensor(f"raw13_{c}", [P, 2, C // P, pair * P], F32))
        self.w2 = ctx.enter_context(nc.sbuf_tensor(f"raw2_{c}", [P, pair, C], F32))
        self.got = ctx.enter_context(nc.semaphore(f"raw_got{c}"))

    def load(self, sp, W1, W3, W2, e):
        cols = slice(self.c * self.pair * P, (self.c + 1) * self.pair * P)
        for a, src in enumerate((W1, W3)):
            sp.dma_start(self.w13[:, a], src[bass.ds(e, 1), :, cols].rearrange("e (k p) h -> p (e k) h", p=P)
                         ).then_inc(self.got, 16)
        sp.dma_start(self.w2[:], W2[bass.ds(e, 1), cols, :].rearrange("e (b p) w -> p (e b) w", p=P)).then_inc(self.got, 16)


def experts(nc, W1, W3, W2, xs_dram, ys_dram, tiles, find_rows, x_res, first_slot, n_work, rows, ident):
    table = tiles.table
    n_tile = x_res.shape[1]
    E, C, H = W1.shape
    KC, NH = C // P, H // P
    PAIR = 2
    NS = NH // PAIR
    CH = rows // P
    W = PAIR * P
    n_rows = xs_dram.shape[0]

    with ExitStack() as ctx:
        def sb(name, shape, dt=F32):
            return ctx.enter_context(nc.sbuf_tensor(name, shape, dt))

        def steps(name, names):
            return Steps(ctx.enter_context(nc.semaphore(name)), names)

        slots = [first_slot] + [WeightSlot(nc, ctx, c, C, PAIR) for c in range(1, NS)]
        hi13, lo13 = sb("hi13", [P, NS, 2, KC, W], F32R), sb("lo13", [P, NS, 2, KC, W], F32R)
        hi2, lo2 = sb("hi2", [P, NS, PAIR, C], F32R), sb("lo2", [P, NS, PAIR, C], F32R)
        xg = sb("xg", [P, CH, C])
        xT_hi, xT_lo = sb("xT_hi", [P, KC, rows], F32R), sb("xT_lo", [P, KC, rows], F32R)
        sl, af = sb("sl", [P, 2, rows]), sb("af", [P, 2, rows])
        a_hi, a_lo = sb("a_hi", [P, 2, rows], F32R), sb("a_lo", [P, 2, rows], F32R)
        ysb = sb("ysb", [P, CH, C])
        RING = 6
        early = sb("early", [P, RING, C])
        one, carrier = sb("e_one", [P, 1]), sb("e_carrier", [P, 1])
        bank = [ctx.enter_context(nc.psum_tensor(f"mo_bank{i}", [P, 512], F32)) for i in range(6)]
        bank_hg, bank_y, bank_x = bank[0:2], bank[2:4], bank[4:6]

        x_got = ctx.enter_context(nc.semaphore("x_got"))
        y_put = ctx.enter_context(nc.semaphore("y_put"))
        early_got = [ctx.enter_context(nc.semaphore(f"early_got{i}")) for i in range(n_tile)]
        rows_found = ctx.enter_context(nc.semaphore("rows_found"))
        early_in = ctx.enter_context(nc.semaphore("early_in"))
        one_set = ctx.enter_context(nc.semaphore("e_one_set"))
        carried = ctx.enter_context(nc.semaphore("e_carried"))
        adds = {2: range(0, 3), 3: range(3, 7), 4: range(7, 11), 5: range(11, n_tile)}
        pM = steps("pM", "HG0 HG1 Y0 HG2 Y1 HG3 Y2 HG4 Y3 HG5 Y4 Y5")
        pX = steps("pX", "XT")
        pieces = [(c, q) for c in range(NS) for q in range(3)]
        aM, aX = steps("aM", "s0 s1 s2 s3 s4 s5 y"), steps("aX", "x0 x1")
        aW, vW = (steps(n, " ".join(f"p{c}{q}" for c, q in pieces)) for n in ("aW", "vW"))
        vM, vX = steps("vM", " ".join(f"m{j} h{j} a{j}" for j in range(NH)) + " y"), steps("vX", "x0 x1")
        start = {0: [(0, 1, 0), (0, 1, 1), (0, 1, 2)]}
        when = {0: [(0, 2, 0)], 1: [(0, 2, 1), (0, 2, 2)], 2: [(1, 0, 0), (1, 0, 1)], 3: [(1, 0, 2)],
                4: [(1, 1, 0), (1, 1, 1)], 6: [(1, 1, 2)]}

        def part(c, q):
            if q == 2:
                return [t.rearrange("p b w -> p (b w)") for t in (slots[c].w2[:], hi2[:, c], lo2[:, c])]
            return [t.rearrange("p k w -> p (k w)") for t in (slots[c].w13[:, q], hi13[:, c, q], lo13[:, c, q])]

        with nc.Block() as block:
            @block.sync
            def _(sp):
                def load(k):
                    if isinstance(k, int) and k == 0:
                        e, row = 0, 0
                    else:
                        e = sp.value_load(table[0:1, 0, bass.ds(k, 1)], min_val=0, max_val=E - 1)
                        row = sp.value_load(table[0:1, 1, bass.ds(k, 1)], min_val=0, max_val=n_rows - rows)
                    pX.wait(sp, k - 1, "XT")
                    sp.dma_start(xg[:], xs_dram[bass.ds(row, rows), :].rearrange("(c p) w -> p c w", p=P)).then_inc(x_got, 16)
                    for c, slot in enumerate(slots):
                        vW.wait(sp, k - 1, f"p{c}2")
                        if not (isinstance(k, int) and k == 0 and c == 0):
                            slot.load(sp, W1, W3, W2, e)

                def store(k):
                    aM.wait(sp, k, "y")
                    vM.wait(sp, k, "y")
                    sp.dma_start(ys_dram[bass.ds(k * rows, rows), :].rearrange("(c p) w -> p c w", p=P), ysb[:]).then_inc(y_put, 16)

                def body(k, first, last):
                    load(k)
                    if not first:
                        store(k - 1)
                peeled(sp, n_work, body)
                store(n_work - 1)
                sp.wait_ge(y_put, 16 * n_work)

            @block.tensor
            def _(pe):
                def turn(k):
                    pe.wait_ge(x_got, 16 * k + 16)
                    aX.wait(pe, k - 1, "x1")
                    vX.wait(pe, k - 1, "x1")
                    for c in range(CH):
                        for q in range(KC):
                            mm = pe.transpose(bank_x[c][:, q * P:(q + 1) * P], xg[:, c, q * P:(q + 1) * P], ident[:])
                    pX.done(mm, "XT")

                def hg(k, j):
                    c, o = j // PAIR, (j % PAIR) * P
                    if j == 0:
                        aX.wait(pe, k, "x1")
                        vX.wait(pe, k, "x1")
                    vW.wait(pe, k, f"p{c}1")
                    if j > 1:
                        vM.wait(pe, k, f"m{j - 2}")
                    else:
                        vM.wait(pe, k - 1, f"m{NH - 2 + j}")
                    for a in range(2):
                        for q in range(KC):
                            mm = product(pe, bank_hg[j % 2][:, a * rows:(a + 1) * rows],
                                         (hi13[:, c, a, q, o:o + P], lo13[:, c, a, q, o:o + P]),
                                         (xT_hi[:, q, :], xT_lo[:, q, :]), q == 0, q == KC - 1)
                    pM.done(mm, f"HG{j}")

                def down(k, j):
                    if j == 0:
                        aM.wait(pe, k - 1, "y")
                        vM.wait(pe, k - 1, "y")
                    c, b = j // PAIR, j % PAIR
                    vW.wait(pe, k, f"p{c}2")
                    vM.wait(pe, k, f"a{j}")
                    for r in range(CH):
                        mm = product(pe, bank_y[r][:], (a_hi[:, j % 2, r * P:(r + 1) * P], a_lo[:, j % 2, r * P:(r + 1) * P]),
                                     (hi2[:, c, b, :], lo2[:, c, b, :]), j == 0, j == NH - 1)
                    pM.done(mm, f"Y{j}")

                turn(0)

                def body(k, first, last):
                    for j in range(NH):
                        hg(k, j)
                        if j == NH - 1 and not last:
                            turn(k + 1)
                        if j:
                            down(k, j - 1)
                    down(k, NH - 1)
                peeled(pe, n_work, body)

            def slot_free(eng, k, c):
                pM.wait(eng, k - 1, f"Y{PAIR * c + PAIR - 1}")

            @block.scalar
            def _(act):
                def split(k, c, q):
                    raw, hi, _lo = part(c, q)
                    act.wait_ge(slots[c].got, 48 * k + 48)
                    slot_free(act, k, c)
                    aW.done(act.copy(hi, raw), f"p{c}{q}")

                def x_hi(k):
                    if not (isinstance(k, int) and k == 0):
                        pM.wait(act, k - 1, f"HG{NH - 1}")
                    pX.wait(act, k, "XT")
                    for c in range(CH):
                        aX.done(act.copy(xT_hi[:, :, c * P:(c + 1) * P],
                                         bank_x[c][:].rearrange("p (k q) -> p k q", q=P)), f"x{c}")

                for q in range(3):
                    split(0, 0, q)
                x_hi(0)

                def body(k, first, last):
                    for j in range(NH):
                        pM.wait(act, k, f"HG{j}")
                        if j > 1:
                            vM.wait(act, k, f"m{j - 2}")
                        else:
                            vM.wait(act, k - 1, f"m{NH - 2 + j}")
                        aM.done(act.activation(sl[:, j % 2, :], bank_hg[j % 2][:, 0:rows], ACT.Silu), f"s{j}")
                        if j == NH - 1 and not last:
                            x_hi(k + 1)
                        for ahead, c, q in (start.get(j, []) if first else []) + when.get(j, []):
                            if not (ahead and last):
                                split(k + ahead, c, q)
                    pM.wait(act, k, f"Y{NH - 1}")
                    need(act, y_put, 16 * k)
                    aM.done(act.copy(ysb[:, 0, :], bank_y[0][:]), "y")
                    if not last:
                        for ahead, c, q in when[NH]:
                            split(k + ahead, c, q)
                peeled(act, n_work, body)

            @block.vector
            def _(dve):
                def split(k, c, q):
                    raw, hi, lo = part(c, q)
                    aW.wait(dve, k, f"p{c}{q}")
                    vW.done(dve.tensor_tensor(lo, raw, hi.bitcast(F32), ALU.subtract), f"p{c}{q}")

                def x_lo(k):
                    for c in range(CH):
                        aX.wait(dve, k, f"x{c}")
                        vX.done(dve.tensor_tensor(xT_lo[:, :, c * P:(c + 1) * P],
                                                  bank_x[c][:].rearrange("p (k q) -> p k q", q=P),
                                                  xT_hi[:, :, c * P:(c + 1) * P].bitcast(F32), ALU.subtract), f"x{c}")

                def add_early(i):
                    dve.wait_ge(early_got[i], 16)
                    dve.scalar_tensor_tensor(x_res[:, i, :], early[:, i % RING, :], tiles.weight[0][:, i:i + 1],
                                             x_res[:, i, :], ALU.mult, ALU.add).then_inc(early_in, 1)

                for q in range(3):
                    split(0, 0, q)
                x_lo(0)

                def body(k, first, last):
                    for j in range(NH):
                        u = j % 2
                        aM.wait(dve, k, f"s{j}")
                        vM.done(dve.tensor_tensor(af[:, u, :], bank_hg[u][:, rows:2 * rows], sl[:, u, :], ALU.mult), f"m{j}")
                        if j > 1:
                            pM.wait(dve, k, f"Y{j - 2}")
                        else:
                            pM.wait(dve, k - 1, f"Y{NH - 2 + j}")
                        vM.wait(dve, k, f"m{j}")
                        vM.done(dve.tensor_copy(a_hi[:, u, :], af[:, u, :]), f"h{j}")
                        vM.wait(dve, k, f"h{j}")
                        vM.done(dve.tensor_tensor(a_lo[:, u, :], af[:, u, :], a_hi[:, u, :].bitcast(F32), ALU.subtract), f"a{j}")
                        if j == NH - 1 and not last:
                            x_lo(k + 1)
                        for ahead, c, q in (start.get(j, []) if first else []) + when.get(j, []):
                            if not (ahead and last):
                                split(k + ahead, c, q)
                        if j == NH - 1 and first:
                            find_rows(dve)
                            dve.memset(one[:], 1.0).then_inc(rows_found, 1)
                        if last:
                            for i in adds.get(j, ()):
                                add_early(i)
                    pM.wait(dve, k, f"Y{NH - 1}")
                    need(dve, y_put, 16 * k)
                    vM.done(dve.tensor_copy(ysb[:, 1, :], bank_y[1][:]), "y")
                    if not last:
                        for ahead, c, q in when[NH]:
                            split(k + ahead, c, q)
                peeled(dve, n_work, body)

            @block.gpsimd
            def _(pool):
                pool.wait_ge(rows_found, 1)
                pool.wait_ge(y_put, 16 * (n_work - 1))
                for i in range(n_tile):
                    need(pool, early_in, i - RING + 1)
                    need(pool, carried, i)
                    pool.tensor_tensor(carrier[:], one[:], one[:], ALU.add).then_inc(carried, 1)
                    pool.indirect_dma_start(early[:, i % RING, :], None, ys_dram[0:(n_work - 1) * rows, :],
                                            bass.IndirectOffsetOnAxis(ap=tiles.pos[0][:, i:i + 1], axis=0)
                                            ).then_inc(early_got[i], 16)


def combine(nc, x_res, ys_dram, pos, weight, out):
    n_tile, C = x_res.shape[1], x_res.shape[2]
    with ExitStack() as ctx:
        late = ctx.enter_context(nc.sbuf_tensor("late", [P, n_tile, C], F32))
        got = [ctx.enter_context(nc.semaphore(f"late_got{i}")) for i in range(n_tile)]
        added = ctx.enter_context(nc.semaphore("late_added"))
        put = ctx.enter_context(nc.semaphore("out_put"))
        out_t = out.rearrange("(i p) c -> p i c", p=P)

        with nc.Block() as block:
            @block.gpsimd
            def _(pool):
                for i in range(n_tile):
                    pool.indirect_dma_start(late[:, i, :], None, ys_dram,
                                            bass.IndirectOffsetOnAxis(ap=pos[:, i:i + 1], axis=0)).then_inc(got[i], 16)

            @block.vector
            def _(dve):
                for i in range(n_tile):
                    dve.wait_ge(got[i], 16)
                    dve.scalar_tensor_tensor(x_res[:, i, :], late[:, i, :], weight[:, i:i + 1], x_res[:, i, :],
                                             ALU.mult, ALU.add).then_inc(added, 1)

            @block.sync
            def _(sp):
                for i in range(n_tile):
                    sp.wait_ge(added, i + 1)
                    sp.dma_start(out_t[:, i, :], x_res[:, i, :]).then_inc(put, 16)
                sp.wait_ge(put, 16 * n_tile)


def perceiver_block(nc, x, ctx_512, xWq, xWkv, xWo, wq, w_down, wk_up, wv_up, wo, Wr, W1, W2, W3, rope, out):
    B, T, C = x.shape
    E = Wr.shape[1]
    n_tok = B * T
    n_tile = n_tok // P
    rows = 2 * P
    region = n_tok + rows
    n_work = (2 * n_tok - E) // rows + E
    xs = nc.dram_tensor("xs", (E * region + rows, C), F32).ap()
    ys = nc.dram_tensor("ys", (n_work * rows, C), F32).ap()
    v_last = nc.dram_tensor("v_last_rows", (B, 2, C), F32).ap()

    with ExitStack() as ctx:
        def sb(name, shape, dt=F32):
            return ctx.enter_context(nc.sbuf_tensor(name, shape, dt))
        x_res = sb("x_res", [P, n_tile, C])
        gate_w = sb("gate_w", [P, n_tile, 2])
        row_all = sb("row_all", [P, n_tile, 2])
        pick_all = sb("pick_all", [P, n_tile, 2 * E])
        count = sb("count", [P, E])
        zeros = sb("zeros", [P, C])
        x_zero = ctx.enter_context(nc.semaphore("xs_zeroed"))
        n_fill = xs.shape[0] // B
        assert n_fill * B == xs.shape[0]
        fill_p = max(d for d in range(1, P + 1) if n_fill % d == 0)
        first_slot = WeightSlot(nc, ctx, 0, C, 2)
        tiles = TileTable(nc, ctx, E, n_tile, n_work, rows, region, n_tok)

        def zero_rows(sp, b):
            sp.dma_start(xs[bass.ds(b * n_fill, n_fill), :].rearrange("(p c) w -> p c w", p=fill_p),
                         zeros[0:fill_p, :].unsqueeze(1).to_broadcast([fill_p, n_fill // fill_p, C])).then_inc(x_zero, 16)

        ident, quad_mask = block_constants(nc, ctx, zeros, tiles)
        tiles.scratch(nc, ctx, 2 * n_tile)
        with ExitStack() as attention:
            weights = SelfAttentionWeights(nc, attention, wq, w_down, wk_up, wv_up, wo, Wr, rope)
            cross_attention(nc, x.rearrange("b t c -> (b t) c"), ctx_512, xWq, xWkv, xWo, x_res, ident, quad_mask,
                            v_last, weights.load, zero_rows)
            self_attention_and_routing(nc, weights, lambda eng: eng.wait_ge(x_zero, 16 * B),
                                       lambda sp: first_slot.load(sp, W1, W3, W2, 0),
                                       lambda dve: tiles.fill(dve, count), x_res, ident, xs, gate_w, row_all, pick_all, count, region, T)
        experts(nc, W1, W3, W2, xs, ys, tiles, lambda dve: tiles.find_rows(dve, row_all, pick_all, gate_w), x_res,
                first_slot, n_work, rows, ident)
        combine(nc, x_res, ys, tiles.pos[1], tiles.weight[1], out.rearrange("b t c -> (b t) c"))


_INS = ['x', 'ctx_512', 'L0_xattn_Wq', 'L0_xattn_Wkv', 'L0_xattn_Wo', 'L0_attn_wq', 'L0_attn_w_down', 'L0_attn_wk_up',
        'L0_attn_wv_up', 'L0_attn_wo', 'L0_ffn_Wr', 'L0_ffn_W1', 'L0_ffn_W2', 'L0_ffn_W3']


def kernel(**inputs):
    import numpy as _np
    import concourse.bacc as _bacc
    from concourse import mybir as _mybir
    from concourse.bass_utils import run_bass_kernel_spmd as _run

    nc = _bacc.Bacc("TRN2", target_bir_lowering=False, num_devices=1)
    arrays, args = {}, []
    for name in _INS:
        a = _np.ascontiguousarray(inputs[name])
        arrays[f"in_{name}_dram"] = a
        args.append(nc.dram_tensor(f"in_{name}_dram", a.shape, _mybir.dt.from_np(a.dtype), kind="ExternalInput").ap())
    B, T, C = inputs['x'].shape
    args.append(nc.inline_tensor(rope_tables(T, 32), name="rope_tables").ap())
    out = nc.dram_tensor("out_0_dram", (B, T, C), _mybir.dt.float32, kind="ExternalOutput").ap()
    perceiver_block(nc, *args, out)
    r = _run(nc, [arrays], core_ids=[0])
    return r.results[0]["out_0_dram"]
```
